# Optimizing a Trainium2 kernel written in Bass

```python
import numpy as np
import jax
import jax.numpy as jnp

def _softmax(x, axis=-1):
    return jax.nn.softmax(x, axis=axis)

def _gelu(x):
    return jax.nn.gelu(x, approximate=True)

def _silu(x):
    return jax.nn.silu(x)

def _sigmoid(x):
    return jax.nn.sigmoid(x)

def _layernorm(x, axis=-1, eps=1e-05):
    m = jnp.mean(x, axis=axis, keepdims=True)
    v = jnp.var(x, axis=axis, keepdims=True)
    return (x - m) / jnp.sqrt(v + eps)

def _scatter_add(tgt, idx, src, axis=0):
    return tgt.at[idx].add(src)

def _segment_sum(src, seg, n):
    return jax.ops.segment_sum(src, seg, n)
kernel_name = 'mk_vit_tower_cls_d1_tok_img768_r4_31e5c6'

def setup_inputs(seed: int=0):
    np.random.seed(seed)
    _w = jnp.asarray

    def _rec_inputs():
        import jax
        import jax.numpy as jnp
        _rk = jax.random.key(seed)
        x = -0.000222058 + 0.999998 * jax.random.normal(jax.random.fold_in(_rk, 1), (128, 3, 64, 64), jnp.float32)
        cls_tok = 0.02 * jax.random.normal(jax.random.fold_in(_rk, 5), (1, 1, 192), jnp.float32)
        return (x, cls_tok)
    x, cls_tok = _rec_inputs()

    def _L0_tok_setup():
        import jax, jax.numpy as jnp
        import numpy as np
        from jax import lax
        HIDDEN = 192
        C_IN = 3
        PATCH = 16
        SIDE = 32
        NUM_PATCHES = SIDE * SIDE

        def _position_ids(nb_h, nb_w):
            boundaries = np.arange(1.0 / SIDE, 1.0, 1.0 / SIDE, dtype=np.float32)
            frac_h = np.arange(0.0, 1.0 - 1e-06, 1.0 / nb_h, dtype=np.float32)
            frac_w = np.arange(0.0, 1.0 - 1e-06, 1.0 / nb_w, dtype=np.float32)
            bh = np.searchsorted(boundaries, frac_h, side='right')
            bw = np.searchsorted(boundaries, frac_w, side='right')
            return jnp.asarray((bh[:, None] * SIDE + bw).reshape(-1), dtype=jnp.int32)
        key = jax.random.key(seed)
        k1, k2, k3 = jax.random.split(key, 3)
        pixel_values = jax.random.normal(k1, (32, C_IN, 128, 128), dtype=jnp.float32)
        conv_w = jax.random.normal(k2, (HIDDEN, C_IN, PATCH, PATCH), dtype=jnp.float32) * 0.02
        conv_b = jnp.zeros((HIDDEN,), dtype=jnp.float32)
        pos_table = jax.random.normal(k3, (NUM_PATCHES, HIDDEN), dtype=jnp.float32) * 0.02
        return {'pixel_values': pixel_values, 'conv_w': conv_w, 'conv_b': conv_b, 'pos_table': pos_table}
    _L0_tok_all = _L0_tok_setup()
    _L0_tok_in = {k: v for k, v in _L0_tok_all.items() if k in ('conv_w', 'conv_b', 'pos_table')}
    del _L0_tok_all

    def _L0_attn_setup():
        import jax, jax.numpy as jnp
        import numpy as np
        from jax import lax
        HID, STATE, K, EXP = (192, 16, 4, 2)
        INNER = HID * EXP
        B_SZ, L = (2, 256)

        def silu(v):
            return v * jax.nn.sigmoid(v)

        def _forward(x, W_in, conv_w, conv_b, W_x, W_dt, b_dt, A_log, D, W_out, gamma, beta):
            xz = x @ W_in
            x_inner, z = jnp.split(xz, 2, axis=-1)
            x_conv = lax.conv_general_dilated(x_inner, conv_w, window_strides=(1,), padding=[((K - 1) // 2, K // 2)], dimension_numbers=('NWC', 'WIO', 'NWC')) + conv_b
            x_conv = silu(x_conv)
            BC = x_conv @ W_x
            Bm, Cm = jnp.split(BC, 2, axis=-1)
            delta = jax.nn.softplus(x_conv @ W_dt + b_dt)
            A = -jnp.exp(A_log)

            def step(h, inp):
                x_t, d_t, B_t, C_t = inp
                A_disc = jnp.exp(d_t[:, :, None] * A)
                h = A_disc * h + (d_t * x_t)[:, :, None] * B_t[:, None, :]
                y_t = jnp.einsum('bds,bs->bd', h, C_t)
                return (h, y_t)
            xs = (jnp.swapaxes(x_conv, 0, 1), jnp.swapaxes(delta, 0, 1), jnp.swapaxes(Bm, 0, 1), jnp.swapaxes(Cm, 0, 1))
            h0 = jnp.zeros((x.shape[0], A.shape[0], A.shape[1]), dtype=x.dtype)
            _, ys = lax.scan(step, h0, xs)
            y = jnp.swapaxes(ys, 0, 1) + D * x_conv
            y = y * silu(z)
            out = y @ W_out
            mu = jnp.mean(out, axis=-1, keepdims=True)
            var = jnp.mean(jnp.square(out - mu), axis=-1, keepdims=True)
            return (out - mu) * lax.rsqrt(var + 1e-05) * gamma + beta
        key = jax.random.key(seed)
        ks = jax.random.split(key, 12)
        s = 0.02
        x = jax.random.normal(ks[0], (B_SZ, L, HID), dtype=jnp.float32)
        W_in = jax.random.normal(ks[1], (HID, INNER * 2), dtype=jnp.float32) * s
        conv_w = jax.random.normal(ks[2], (K, INNER, INNER), dtype=jnp.float32) * s
        conv_b = jnp.zeros((INNER,), dtype=jnp.float32)
        W_x = jax.random.normal(ks[3], (INNER, STATE * 2), dtype=jnp.float32) * s
        W_dt = jax.random.normal(ks[4], (INNER, INNER), dtype=jnp.float32) * s
        b_dt = jnp.zeros((INNER,), dtype=jnp.float32)
        A_log = jnp.log(jax.random.uniform(ks[5], (INNER, STATE), minval=1.0, maxval=16.0, dtype=jnp.float32))
        D = jnp.ones((INNER,), dtype=jnp.float32)
        W_out = jax.random.normal(ks[6], (INNER, HID), dtype=jnp.float32) * s
        gamma = jnp.ones((HID,), dtype=jnp.float32)
        beta = jnp.zeros((HID,), dtype=jnp.float32)
        return {'x': x, 'W_in': W_in, 'conv_w': conv_w, 'conv_b': conv_b, 'W_x': W_x, 'W_dt': W_dt, 'b_dt': b_dt, 'A_log': A_log, 'D': D, 'W_out': W_out, 'gamma': gamma, 'beta': beta}
    _L0_attn_all = _L0_attn_setup()
    _L0_attn_in = {k: v for k, v in _L0_attn_all.items() if k in ('W_in', 'conv_w', 'conv_b', 'W_x', 'W_dt', 'b_dt', 'A_log', 'D', 'W_out', 'gamma', 'beta')}
    del _L0_attn_all

    def _L0_ffn_setup():
        import jax, jax.numpy as jnp
        import numpy as np
        EPS_NORM = 1e-06
        EPS_Q = 1e-05

        def rmsnorm(x, g):
            return x * jax.lax.rsqrt(jnp.mean(x * x, axis=-1, keepdims=True) + EPS_NORM) * g

        def activation_quant(x):
            scale = 127.0 / jnp.maximum(jnp.max(jnp.abs(x), axis=-1, keepdims=True), EPS_Q)
            return jnp.clip(jnp.round(x * scale), -128, 127) / scale

        def weight_quant(w):
            scale = 1.0 / jnp.maximum(jnp.mean(jnp.abs(w)), EPS_Q)
            return jnp.clip(jnp.round(w * scale), -1, 1) / scale

        def bitlinear(x, w, g):
            x_norm = rmsnorm(x, g)
            x_q = x_norm + jax.lax.stop_gradient(activation_quant(x_norm) - x_norm)
            w_q = w + jax.lax.stop_gradient(weight_quant(w) - w)
            return jnp.einsum('bsd,od->bso', x_q, w_q)
        key = jax.random.key(seed)
        k1, k2, k3 = jax.random.split(key, 3)
        B, S, D, H = (8, 1024, 192, 512)
        x = jax.random.normal(k1, (B, S, D), dtype=jnp.float32)
        w_in = jax.random.normal(k2, (2 * H, D), dtype=jnp.float32) * 0.002
        w_out = jax.random.normal(k3, (D, H), dtype=jnp.float32) * 0.002
        g_in = jnp.ones((D,), dtype=jnp.float32)
        g_out = jnp.ones((H,), dtype=jnp.float32)
        return {'x': x, 'w_in': w_in, 'g_in': g_in, 'w_out': w_out, 'g_out': g_out}
    _L0_ffn_all = _L0_ffn_setup()
    _L0_ffn_in = {k: v for k, v in _L0_ffn_all.items() if k in ('w_in', 'g_in', 'w_out', 'g_out')}
    del _L0_ffn_all
    return {'x': x, 'cls_tok': cls_tok, 'L0_tok_conv_w': _L0_tok_in['conv_w'], 'L0_tok_conv_b': _L0_tok_in['conv_b'], 'L0_tok_pos_table': _L0_tok_in['pos_table'], 'L0_attn_W_in': _L0_attn_in['W_in'], 'L0_attn_conv_w': _L0_attn_in['conv_w'], 'L0_attn_conv_b': _L0_attn_in['conv_b'], 'L0_attn_W_x': _L0_attn_in['W_x'], 'L0_attn_W_dt': _L0_attn_in['W_dt'], 'L0_attn_b_dt': _L0_attn_in['b_dt'], 'L0_attn_A_log': _L0_attn_in['A_log'], 'L0_attn_D': _L0_attn_in['D'], 'L0_attn_W_out': _L0_attn_in['W_out'], 'L0_attn_gamma': _L0_attn_in['gamma'], 'L0_attn_beta': _L0_attn_in['beta'], 'L0_ffn_w_in': _L0_ffn_in['w_in'], 'L0_ffn_g_in': _L0_ffn_in['g_in'], 'L0_ffn_w_out': _L0_ffn_in['w_out'], 'L0_ffn_g_out': _L0_ffn_in['g_out']}

def reference(x, cls_tok, L0_tok_conv_w, L0_tok_conv_b, L0_tok_pos_table, L0_attn_W_in, L0_attn_conv_w, L0_attn_conv_b, L0_attn_W_x, L0_attn_W_dt, L0_attn_b_dt, L0_attn_A_log, L0_attn_D, L0_attn_W_out, L0_attn_gamma, L0_attn_beta, L0_ffn_w_in, L0_ffn_g_in, L0_ffn_w_out, L0_ffn_g_out):
    import jax
    import jax.numpy as jnp

    def _L0_tok_ref(pixel_values, conv_w, conv_b, pos_table):
        import jax, jax.numpy as jnp
        import numpy as np
        from jax import lax
        HIDDEN = 192
        C_IN = 3
        PATCH = 16
        SIDE = 32
        NUM_PATCHES = SIDE * SIDE

        def _position_ids(nb_h, nb_w):
            boundaries = np.arange(1.0 / SIDE, 1.0, 1.0 / SIDE, dtype=np.float32)
            frac_h = np.arange(0.0, 1.0 - 1e-06, 1.0 / nb_h, dtype=np.float32)
            frac_w = np.arange(0.0, 1.0 - 1e-06, 1.0 / nb_w, dtype=np.float32)
            bh = np.searchsorted(boundaries, frac_h, side='right')
            bw = np.searchsorted(boundaries, frac_w, side='right')
            return jnp.asarray((bh[:, None] * SIDE + bw).reshape(-1), dtype=jnp.int32)
        B, _, H, W = pixel_values.shape
        nb_h, nb_w = (H // PATCH, W // PATCH)
        patches = lax.conv_general_dilated(pixel_values, conv_w, window_strides=(PATCH, PATCH), padding='VALID', dimension_numbers=('NCHW', 'OIHW', 'NCHW'))
        patches = patches + conv_b[None, :, None, None]
        embeddings = patches.reshape(B, HIDDEN, nb_h * nb_w).transpose(0, 2, 1)
        pos_ids = _position_ids(nb_h, nb_w)
        pos_emb = pos_table[pos_ids]
        return embeddings + pos_emb[None, :, :]

    def _L0_attn_ref(x, W_in, conv_w, conv_b, W_x, W_dt, b_dt, A_log, D, W_out, gamma, beta):
        import jax, jax.numpy as jnp
        import numpy as np
        from jax import lax
        HID, STATE, K, EXP = (192, 16, 4, 2)
        INNER = HID * EXP
        B_SZ, L = (2, 256)

        def silu(v):
            return v * jax.nn.sigmoid(v)

        def _forward(x, W_in, conv_w, conv_b, W_x, W_dt, b_dt, A_log, D, W_out, gamma, beta):
            xz = x @ W_in
            x_inner, z = jnp.split(xz, 2, axis=-1)
            x_conv = lax.conv_general_dilated(x_inner, conv_w, window_strides=(1,), padding=[((K - 1) // 2, K // 2)], dimension_numbers=('NWC', 'WIO', 'NWC')) + conv_b
            x_conv = silu(x_conv)
            BC = x_conv @ W_x
            Bm, Cm = jnp.split(BC, 2, axis=-1)
            delta = jax.nn.softplus(x_conv @ W_dt + b_dt)
            A = -jnp.exp(A_log)

            def step(h, inp):
                x_t, d_t, B_t, C_t = inp
                A_disc = jnp.exp(d_t[:, :, None] * A)
                h = A_disc * h + (d_t * x_t)[:, :, None] * B_t[:, None, :]
                y_t = jnp.einsum('bds,bs->bd', h, C_t)
                return (h, y_t)
            xs = (jnp.swapaxes(x_conv, 0, 1), jnp.swapaxes(delta, 0, 1), jnp.swapaxes(Bm, 0, 1), jnp.swapaxes(Cm, 0, 1))
            h0 = jnp.zeros((x.shape[0], A.shape[0], A.shape[1]), dtype=x.dtype)
            _, ys = lax.scan(step, h0, xs)
            y = jnp.swapaxes(ys, 0, 1) + D * x_conv
            y = y * silu(z)
            out = y @ W_out
            mu = jnp.mean(out, axis=-1, keepdims=True)
            var = jnp.mean(jnp.square(out - mu), axis=-1, keepdims=True)
            return (out - mu) * lax.rsqrt(var + 1e-05) * gamma + beta
        return _forward(x, W_in, conv_w, conv_b, W_x, W_dt, b_dt, A_log, D, W_out, gamma, beta)

    def _L0_ffn_ref(x, w_in, g_in, w_out, g_out):
        import jax, jax.numpy as jnp
        import numpy as np
        EPS_NORM = 1e-06
        EPS_Q = 1e-05

        def rmsnorm(x, g):
            return x * jax.lax.rsqrt(jnp.mean(x * x, axis=-1, keepdims=True) + EPS_NORM) * g

        def activation_quant(x):
            scale = 127.0 / jnp.maximum(jnp.max(jnp.abs(x), axis=-1, keepdims=True), EPS_Q)
            return jnp.clip(jnp.round(x * scale), -128, 127) / scale

        def weight_quant(w):
            scale = 1.0 / jnp.maximum(jnp.mean(jnp.abs(w)), EPS_Q)
            return jnp.clip(jnp.round(w * scale), -1, 1) / scale

        def bitlinear(x, w, g):
            x_norm = rmsnorm(x, g)
            x_q = x_norm + jax.lax.stop_gradient(activation_quant(x_norm) - x_norm)
            w_q = w + jax.lax.stop_gradient(weight_quant(w) - w)
            return jnp.einsum('bsd,od->bso', x_q, w_q)
        h = bitlinear(x, w_in, g_in)
        up, gate = jnp.split(h, 2, axis=-1)
        y = jax.nn.silu(gate) * up
        return bitlinear(y, w_out, g_out)
    h = _L0_tok_ref(x, L0_tok_conv_w, L0_tok_conv_b, L0_tok_pos_table)
    h = jnp.concatenate([jnp.broadcast_to(cls_tok, (h.shape[0], 1, h.shape[2])), h], axis=1)
    h = h + _L0_attn_ref(_layernorm(h, axis=-1), L0_attn_W_in, L0_attn_conv_w, L0_attn_conv_b, L0_attn_W_x, L0_attn_W_dt, L0_attn_b_dt, L0_attn_A_log, L0_attn_D, L0_attn_W_out, L0_attn_gamma, L0_attn_beta)
    h = h + _L0_ffn_ref(_layernorm(h, axis=-1), L0_ffn_w_in, L0_ffn_g_in, L0_ffn_w_out, L0_ffn_g_out)
    return h

_drawn_inputs = setup_inputs


def setup_inputs(seed=0):
    import zlib

    import numpy as np

    out = dict(_drawn_inputs(seed))
    spreads = {'L0_tok_conv_b': (0.0, 0.1),
     'L0_attn_conv_b': (0.0, 0.1),
     'L0_attn_b_dt': (0.0, 0.8),
     'L0_attn_D': (1.0, 0.2),
     'L0_attn_gamma': (1.0, 0.2),
     'L0_attn_beta': (0.0, 0.1),
     'L0_ffn_g_in': (1.0, 0.6),
     'L0_ffn_g_out': (1.0, 0.6)}
    factors = {'L0_attn_W_x': 8.0,
     'L0_attn_W_dt': 8.0,
     'L0_attn_A_log': 8.0,
     'L0_ffn_w_in': 8.0,
     'L0_ffn_w_out': 8.0}
    for name, (base, spread) in spreads.items():
        noise = np.random.default_rng([zlib.crc32(name.encode()), seed]).standard_normal(out[name].shape)
        drawn = base * np.exp(spread * noise) if base else spread * noise
        out[name] = jnp.asarray(drawn.astype(out[name].dtype))
    for name, factor in factors.items():
        out[name] = (out[name] * factor).astype(out[name].dtype)
    return out
```

```python
from contextlib import ExitStack

import numpy as np
import concourse.bass as bass
import concourse.mybir as mybir

F32 = mybir.dt.float32
BF16 = mybir.dt.bfloat16
ACT = mybir.ActivationFunctionType
ALU = mybir.AluOpType
AX = mybir.AxisListType

P = 128
SIDE, PATCH, GRID = 64, 16, 4
T = 1 + GRID * GRID
HID, HC = 192, 96
KP = 3 * PATCH * PATCH // P
INNER, IC = 384, 3
STATE, TAPS = 16, 4
FFN, FC = 512, 4
PAIRS = (T - 1) // 2
CH = STATE // 2
BANK = 512
DC = STATE * INNER // BANK
POOL_SLOTS = CH // 2
DB = 3
ROUND = 12582912.0
SHARED = 16700
LAST_LAG = 6
POS_TABLE_SIDE = 32


class Steps:

    def __init__(self, eng, sem, apart=None):
        self.eng, self.sem, self.n, self.turns, self.apart = eng, sem, 0, 0, apart

    def mark(self, ins):
        ins.then_inc(self.sem, 1)
        self.n += 1
        return self.n

    def wait(self, n):
        if self.apart:
            self.apart(self.eng, self.sem, self.turns + n)
        else:
            self.eng.wait_ge(self.sem, self.turns + n)

    def then(self, ins):
        self.wait(self.mark(ins))

    def enter(self, turn, per_turn):
        self.first, self.per_turn, self.turns = self.n, per_turn, turn * per_turn

    def leave(self, turns):
        assert self.n - self.first == self.per_turn, (self.sem, self.n - self.first)
        self.n, self.turns = self.first + turns * self.per_turn, 0


def wait(eng, sem, value):
    if not isinstance(value, int) or value > 0:
        eng.wait_ge(sem, value)


def chunks_of(k):
    upto = lambda states: -(-states * INNER // BANK)
    return range(upto(2 * k), upto(2 * k + 2))


def exists(tile):
    return not isinstance(tile, int) or 0 <= tile < T


def vit_block(nc, x, cls_tok, tok_w, tok_b, pos_table, w_in, conv_w, conv_b, w_x, w_dt, b_dt, a_log, d_skip,
              w_out, gamma, beta, f_in, g_in, f_out, g_out, out):
    ctx = ExitStack()
    with ctx:
        def sb(name, shape, dt=F32):
            return ctx.enter_context(nc.sbuf_tensor(name, shape, dt))

        def sem(name):
            return ctx.enter_context(nc.semaphore(name))

        ident = sb("ident", [P, P])
        ones = sb("ones", [P, P])
        mhalf = sb("mhalf", [P, 1])
        mone = sb("mone", [P, 1])
        res = sb("res", [P, T, HID])
        gate = [sb(f"gate{i}", [P, INNER]) for i in range(2)]
        xinT = sb("xinT", [P, IC, (T + 3) * P])
        cw = sb("cw", [P, TAPS, IC, INNER])
        wdt = sb("wdt", [P, IC, INNER])
        wx = sb("wx", [P, IC, 2 * STATE])
        wo = sb("wo", [P, IC, HID])
        cb = sb("cb", [P, IC])
        bdt = sb("bdt", [P, IC])
        dsk = sb("dsk", [P, IC])
        A = sb("A", [P, IC, STATE])
        gam = sb("gam", [P, HID])
        gi = sb("gi", [P, HID])
        go = sb("go", [P, FFN])
        f1 = sb("f1", [HC, 2, 2 * FFN], BF16)
        f2 = sb("f2", [P, FC, HID], BF16)
        ws = sb("ws", [P, 2])
        state = sb("state", [P, STATE, INNER])
        xb = sb("xb", [P, IC, 2 * P])
        sg = sb("sg", [P, IC, 2 * P])
        db, sp = xb, sg
        xcT = sb("xcT", [P, IC, 2 * P])
        dltT = sb("dltT", [P, IC, 2 * P])
        uT = sb("uT", [P, IC, 2 * P])
        dxT = sb("dxT", [P, IC, 2 * P])
        bc = sb("bc", [P, 2, 2 * STATE])
        bcn = sb("bcn", [P, 2, 2 * STATE])
        ow = sb("ow", [P, HID])
        dx = sb("dx", [P, INNER])
        acc = sb("acc", [P, 2, INNER])
        ysum = sb("ysum", [P, INNER])
        ydve = sb("ydve", [P, INNER])
        shared = sb("shared", [P, SHARED])
        at = [0]

        def part(n):
            at[0] += n
            assert at[0] <= SHARED, at[0]
            return shared[:, at[0] - n:at[0]]

        xr = [part(3 * PATCH * SIDE).rearrange("p (c i w) -> p c i w", c=3, i=PATCH) for _ in range(2)]
        wi = part(2 * 2 * INNER)[0:HC].rearrange("p (c n) -> p c n", c=2)
        twT = part(KP * HID).rearrange("p (c n) -> p c n", c=KP)
        pos = part(T * HID).rearrange("p (t n) -> p t n", t=T)
        tb = part(HID)
        bet = part(HID)
        patch = [b[:].rearrange("p c n -> p (c n)").rearrange("p (c n) -> p c n", c=KP) for b in (xcT, dltT)]
        px = [b[:].rearrange("p c n -> p (c n)") for b in (uT, dxT)]
        xn = [part(HID) for _ in range(GRID)]
        xnT = part(2 * GRID * P)[0:HC].rearrange("p (c n) -> p c n", c=2)
        zs = [part(INNER) for _ in range(2)]
        raw = state[:].rearrange("p s n -> p (s n)")
        rawT = raw[0:HC, 0:2 * KP * P].rearrange("p (c n) -> p c n", c=2)
        raw1 = raw[:, 1536:1536 + 8 * HID].rearrange("p (c n) -> p c n", c=8)
        raw2 = raw[0:HC, 3072:3072 + 2 * FFN].rearrange("p (c n) -> p c n", c=2)
        at[0] = 0
        decay = part(STATE * IC * 2 * P).rearrange("p (s c n) -> p s c n", s=STATE, c=IC)
        prod = [part(2 * INNER).rearrange("p (s n) -> p s n", s=2)]
        yz, o1, wq, t1, sig, aa = (part(n) for n in (INNER, HID, HID, HID, FFN, FFN))
        yzT = sb("yzT", [P, IC, P])
        y2 = sb("y2", [P, FFN])
        v2 = sb("v2", [P, FFN])
        t2 = part(FFN)
        sq = part(FFN)
        q1 = sb("q1", [HC, 2, P], BF16)
        q2 = sb("q2", [P, FC, P], BF16)
        st = sb("st", [P, 6])
        mv = [sb(f"mv{i}", [P, 2]) for i in range(2)]
        rs = [sb(f"rs{i}", [P, 2]) for i in range(2)]
        stA = sb("stA", [P, 6])
        mvA = sb("mvA", [P, 2])
        rsA = sb("rsA", [P, 2])
        stF = sb("stF", [P, 6])
        mvF = sb("mvF", [P, 2])
        amF = sb("amF", [P, 1])
        s1 = sb("s1", [P, 5])
        c2 = sb("c2", [P, 2])
        c1 = sb("c1", [P, 2, 2])
        ss = sb("ss", [P, 1])
        am2 = sb("am2", [P, 1])
        s2 = sb("s2", [P, 8])
        wsum = sb("wsum", [P, 2])
        wsc = sb("wsc", [P, 2])

        gate_d = nc.dram_tensor("gate_d", (T - 1, P, INNER), F32, kind="Internal").ap()
        ps = ctx.enter_context(nc.psum_tensor("ps", [P, 8 * BANK], F32))

        def bank(b, n=BANK, rows=P, off=0):
            return ps[0:rows, b * BANK + off:b * BANK + off + n]

        S = {n: sem(n) for n in (
            "x_even x_odd consts_loaded raws_loaded conv_loaded ident_built ones_set raw_scaled raw_turned "
            "tok_turned wsum_ready ws_ready ws_inverse "
            "patch_packed patch_turned patch_act patch_dve emb_ready emb_used mv_ready rs_ready xn_ready "
            "xn_turned xnT_ready xin_ready xin_act xin_dve z_ready zsig_ready z_used "
            "act_step dve_step pool_step a_ready pads_zeroed pos_ready "
            "lin_ready lin_used sig_ready xc_ready sp_ready delta_ready uT_ready dxT_ready bc_ready bcn_ready bc_copied "
            "decay_made decay_turned decay_used u_turned dx_turned dx_ready state_ready rows_read y_ready "
            "gate_kept gate_even_in gate_odd_in yz_ready yz_turned yzT_ready o_ready ow_ready mvA_ready rsA_ready o1_ready h1_ready y_dve y_joined w_ready s1_ready t1_ready "
            "q1_turned q1_ready f1_ready fsig_ready f1_used v2_ready sumsq_ready am2_ready s2_ready t2_ready "
            "q2_turned q2_ready f2_ready final_ready stored").split()}

        def apart(eng, sem, value):
            if isinstance(value, int):
                wait(eng, sem, value)
            else:
                value = eng.lower_val(value)
                eng.wait_ge(S["consts_loaded"], 16 * n_const)
                eng.wait_ge(sem, value)

        def product_read(g, j):
            return (S["emb_ready"], g * GRID + j - 1) if j >= 2 else (S["xn_turned"], g * GRID + 1)

        block = ctx.enter_context(nc.Block())
        x_rows = x.rearrange("b c (g i) w -> g b c i w", g=GRID)
        n_const, n_conv = 15, 3

        def chunks(v, c):
            return v.rearrange("(c p) -> p c", c=c)

        @block.sync
        def _(sp_):
            q = sp_
            q.dma_start(rawT, tok_w.rearrange("(c p) k i j -> p c (k i j)", c=2)).then_inc(S["raws_loaded"], 16)
            q.dma_start(raw1, f_in.rearrange("(c p) n -> p c n", c=8)).then_inc(S["raws_loaded"], 16)
            q.dma_start(raw2, f_out.rearrange("(c p) n -> p c n", c=2)).then_inc(S["raws_loaded"], 16)
            q.dma_start(xr[0], x_rows[0]).then_inc(S["x_even"], 16)
            q.wait_ge(S["consts_loaded"], 16 * n_const)
            q.dma_start(xr[1], x_rows[1]).then_inc(S["x_odd"], 16)
            for tap_w, src in ((cw[:], conv_w.rearrange("t (c p) n -> p t c n", c=IC)),
                               (wdt[:], w_dt.rearrange("(c p) n -> p c n", c=IC)),
                               (wo[:], w_out.rearrange("(c p) n -> p c n", c=IC))):
                q.dma_start(tap_w, src).then_inc(S["conv_loaded"], 16)

            for g in range(GRID):
                if g + 2 < GRID:
                    q.wait_ge(S["patch_packed"], GRID * (g + 1))
                    q.dma_start(xr[g % 2], x_rows[g + 2]).then_inc(S[("x_even", "x_odd")[g % 2]], 16)
                q.wait_ge(S["z_used"], 1 + GRID * (g + 1))
                q.dma_start(gate_d[g * GRID:(g + 1) * GRID].rearrange("t p n -> p t n"),
                            state[:, g * GRID:(g + 1) * GRID, :]).then_inc(S["gate_kept"], 16)
            q.wait_ge(S["gate_kept"], 16 * GRID)

            def fetch_gate(t, par):
                wait(q, S["yz_ready"], t - 1)
                q.dma_start(gate[par][:], gate_d[bass.ds(t - 1, 1)].rearrange("o p n -> (o p) n")).then_inc(
                    S[("gate_even_in", "gate_odd_in")[par]], 16)

            def store(t):
                q.wait_ge(S["final_ready"], t + 1)
                q.dma_start(out[:, bass.ds(t, 1), :], res[:, bass.ds(t, 1), :]).then_inc(S["stored"], 16)

            for t in range(1, 5):
                fetch_gate(t, t % 2)
            with q.Fori(0, 6) as i:
                for h in range(2):
                    fetch_gate(2 * i + 5 + h, (1 + h) % 2)
                    store(2 * i + h)
            for t in range(12, T):
                store(t)
            q.wait_ge(S["stored"], 16 * T)

        @block.gpsimd
        def _(pool):
            own = Steps(pool, S["pool_step"], apart)
            pool.memset(mhalf[:], -0.5)
            pool.memset(mone[:], -1.0)
            pool.memset(ones[:], 1.0).then_inc(S["ones_set"], 1)
            own.then(pool.memset(ident[:], 0.0))
            pool.affine_select(out=ident[:], in_=ident[:], compare_op=ALU.not_equal, fill=1.0, base=0,
                               pattern=[[-1, P]], channel_multiplier=1).then_inc(S["ident_built"], 1)
            pool.memset(xinT[:, :, 0:P], 0.0)
            pool.memset(xinT[:, :, (T + 1) * P:(T + 3) * P], 0.0).then_inc(S["pads_zeroed"], 1)
            pool.wait_ge(S["ws_ready"], 1)
            pool.wait_ge(S["ones_set"], 1)
            pool.tensor_tensor(wsc[:], ws[:], mone[:].to_broadcast([P, 2]), ALU.pow).then_inc(S["ws_inverse"], 1)

            def root(t, par):
                apart(pool, S["mv_ready"], t + 1)
                own.then(pool.tensor_scalar(rs[par][:, 0:1], mv[par][:, 1:2], 1e-5, None, ALU.add))
                pool.tensor_tensor(rs[par][:, 1:2], rs[par][:, 0:1], mhalf[:], ALU.pow).then_inc(S["rs_ready"], 1)
                wait(pool, S["xn_ready"], t + 1)
                r = res[:, bass.ds(t, 1), :]
                pool.tensor_tensor(r, r, bet.rearrange("p (o n) -> p o n", o=1), ALU.add)

            def pack(n):
                g, j = n // GRID, n % GRID
                if j == 0:
                    pool.wait_ge(S[("x_even", "x_odd")[g % 2]], 16 * (g // 2) + 16)
                wait(pool, S["patch_turned"], n - 1)
                pool.tensor_copy(px[n % 2].rearrange("p (i n) -> p i n", n=PATCH),
                                 xr[g % 2].rearrange("p c i w -> p (c i) w")[
                                     :, :, j * PATCH:(j + 1) * PATCH]).then_inc(S["patch_packed"], 1)

            pack(0)
            pack(1)
            pool.wait_ge(S["consts_loaded"], 16 * n_const)
            pool.tensor_tensor(pos[:, 1:T, :], pos[:, 1:T, :],
                               tb.rearrange("p (o n) -> p o n", o=1).to_broadcast([P, T - 1, HID]),
                               ALU.add).then_inc(S["pos_ready"], 1)
            root(0, 0)

            for n in range(GRID * GRID):
                if n + 2 < GRID * GRID:
                    pack(n + 2)
                root(n + 1, (n + 1) % 2)

            def conv_gate(q_, n):
                wait(pool, S["sig_ready"], q_ + 1)
                wait(pool, S["lin_ready"], 6 * q_)
                wait(pool, S["bc_ready"], q_)
                pool.tensor_tensor(xcT[:, :, 0:n], xb[:, :, 0:n], sg[:, :, 0:n], ALU.mult).then_inc(S["xc_ready"], 1)

            def inputs(q_, n):
                wait(pool, S["delta_ready"], q_ + 1)
                wait(pool, S["xc_ready"], q_ + 1)
                wait(pool, S["u_turned"], 2 * q_ - 1)
                pool.tensor_tensor(uT[:, :, 0:n], dltT[:, :, 0:n], xcT[:, :, 0:n], ALU.mult).then_inc(S["uT_ready"], 1)
                wait(pool, S["dx_turned"], 2 * q_ - 1)
                pool.tensor_tensor(dxT[:, :, 0:n], xcT[:, :, 0:n],
                                   dsk[:].rearrange("p (c o) -> p c o", o=1).to_broadcast([P, IC, n]),
                                   ALU.mult).then_inc(S["dxT_ready"], 1)

            def outputs(t, par, k):
                if k == 0:
                    wait(pool, S["y_ready"], t)
                apart(pool, S["state_ready"], t * CH + k + 1)
                to = acc if k == 0 else prod[0]
                for r in range(2):
                    s_ = 2 * k + r
                    last = pool.tensor_scalar(to[:, r, :], state[:, s_, :], bc[:, par, STATE + s_:STATE + s_ + 1],
                                              1.0, ALU.mult, ALU.mult)
                last.then_inc(S["rows_read"], 1)
                pool.wait_ge(S["rows_read"], t * POOL_SLOTS + k // 2 + 1)
                if k > 0:
                    own.then(pool.tensor_tensor(acc[:], acc[:], prod[0], ALU.add))
                if k == CH - 2:
                    wait(pool, S["yz_ready"], t)
                    pool.tensor_tensor(ysum[:], acc[:, 0, :], acc[:, 1, :], ALU.add).then_inc(S["y_ready"], 1)

            def small_root(t):
                apart(pool, S["mvA_ready"], t + 1)
                own.then(pool.tensor_scalar(rsA[:, 0:1], mvA[:, 1:2], 1e-5, None, ALU.add))
                pool.tensor_tensor(rsA[:, 1:2], rsA[:, 0:1], mhalf[:], ALU.pow).then_inc(S["rsA_ready"], 1)

            def residual(t):
                pool.wait_ge(S["o1_ready"], t + 1)
                own.then(pool.tensor_tensor(o1, o1, gam[:], ALU.mult))
                r = res[:, bass.ds(t, 1), :]
                pool.tensor_tensor(r, r, o1.rearrange("p (o n) -> p o n", o=1), ALU.add).then_inc(S["h1_ready"], 1)

            def first_scales(t, par):
                apart(pool, S["w_ready"], t + 1)
                own.then(pool.tensor_scalar(s1[:, 0:1], mvF[:, 1:2], 1.0 + 1e-6, 1e-11, ALU.mult, ALU.add))
                own.then(pool.tensor_tensor(s1[:, 1:2], s1[:, 0:1], mhalf[:], ALU.pow))
                own.then(pool.tensor_scalar(s1[:, 2:3], amF[:], s1[:, 1:2], 1e-5, ALU.mult, ALU.max))
                own.then(pool.tensor_tensor(s1[:, 3:4], s1[:, 2:3], mone[:], ALU.pow))
                apart(pool, S["t1_ready"], t)
                pool.tensor_scalar(s1[:, 4:5], s1[:, 3:4], s1[:, 1:2], 127.0, ALU.mult, ALU.mult)
                apart(pool, S["fsig_ready"], t - 1)
                pool.tensor_scalar(c1[:, par, 1:2], s1[:, 2:3], ws[:, 0:1], -1.0 / 127.0, ALU.mult, ALU.mult)
                pool.tensor_scalar(c1[:, par, 0:1], s1[:, 2:3], ws[:, 0:1], 1.0 / 127.0, ALU.mult,
                                   ALU.mult).then_inc(S["s1_ready"], 1)

            def weigh(t):
                pool.wait_ge(S["f1_used"], t + 1)
                wait(pool, S["t2_ready"], t)
                wait(pool, S["am2_ready"], t)
                pool.tensor_tensor(v2[:], y2[:], go[:], ALU.mult).then_inc(S["v2_ready"], 1)

            def second_scales(t, par):
                apart(pool, S["sumsq_ready"], t + 1)
                pool.wait_ge(S["am2_ready"], t + 1)
                c = c1[:, par, 0:1]
                apart(pool, S["s1_ready"], t + 1)
                own.then(pool.tensor_scalar(s2[:, 0:1], c, c, 1.0, ALU.mult, ALU.mult))
                own.then(pool.tensor_scalar(s2[:, 1:2], ss[:], s2[:, 0:1], s2[:, 0:1], ALU.mult, ALU.mult))
                own.then(pool.tensor_scalar(s2[:, 2:3], s2[:, 1:2], 1.0 / FFN, 1e-6, ALU.mult, ALU.add))
                own.then(pool.tensor_tensor(s2[:, 3:4], s2[:, 2:3], mhalf[:], ALU.pow))
                own.then(pool.tensor_tensor(s2[:, 4:5], s2[:, 3:4], s2[:, 0:1], ALU.mult))
                own.then(pool.tensor_scalar(s2[:, 5:6], am2[:], s2[:, 4:5], 1e-5, ALU.mult, ALU.max))
                own.then(pool.tensor_tensor(s2[:, 6:7], s2[:, 5:6], mone[:], ALU.pow))
                apart(pool, S["t2_ready"], t)
                pool.tensor_scalar(s2[:, 7:8], s2[:, 6:7], s2[:, 4:5], 127.0, ALU.mult, ALU.mult)
                apart(pool, S["final_ready"], t - 1)
                pool.tensor_scalar(c2[:, par:par + 1], s2[:, 5:6], ws[:, 1:2], 1.0 / 127.0, ALU.mult,
                                   ALU.mult).then_inc(S["s2_ready"], 1)

            def step(t, j, pair):
                par = (1 + j) % 2
                scan = exists(t)
                for k in range(CH):
                    if k == 3 and exists(t - 4):
                        second_scales(t - 4, par)
                    if k == 4 and exists(t - 2):
                        first_scales(t - 2, par)
                    if k == 7 and exists(t - 1):
                        small_root(t - 1)
                    if k == 1 and exists(t - 2):
                        residual(t - 2)
                    if k == 0 and exists(t - 4):
                        weigh(t - 4)
                    if scan and k % 2 == 0:
                        outputs(t, par, k)
                    if j == 1 and k == 2 and (pair is not None) and (not isinstance(pair, int) or pair < PAIRS - 1):
                        inputs(pair + 2, 2 * P)
                    if j == 0 and k == 1 and (pair is not None) and (not isinstance(pair, int) or pair < PAIRS - 1):
                        conv_gate(pair + 2, 2 * P)

            conv_gate(0, P)
            inputs(0, P)
            conv_gate(1, 2 * P)
            for k in range(0, CH, 2):
                outputs(0, 0, k)
            inputs(1, 2 * P)
            walk(pool, step, own, POOL_STEPS)

        @block.scalar
        def _(act):
            own = Steps(act, S["act_step"])
            act.preload_act_table_set("natural_log_exp_and_others")
            step_ = POS_TABLE_SIDE // GRID
            rows = pos_table.rearrange("(h a w b) n -> a b h w n", h=GRID, a=step_, w=GRID)[0, 0]
            for h in range(GRID):
                act.dma_start(pos[:, 1 + GRID * h:1 + GRID * (h + 1), :],
                              rows[h:h + 1].to_broadcast([P, GRID, HID])).then_inc(S["consts_loaded"], 16)
            act.dma_start(tb, tok_b.rearrange("(o n) -> o n", o=1).to_broadcast([P, HID])).then_inc(S["consts_loaded"], 16)
            act.dma_start(res[:, 0, :], cls_tok.rearrange("a b n -> (a b) n").to_broadcast([P, HID])).then_inc(S["consts_loaded"], 16)
            act.dma_start(wi, w_in.rearrange("(c p) n -> p c n", c=2)).then_inc(S["consts_loaded"], 16)
            act.dma_start(bet, beta.rearrange("(o n) -> o n", o=1).to_broadcast([P, HID])).then_inc(S["consts_loaded"], 16)
            act.dma_start(gam[:], gamma.rearrange("(o n) -> o n", o=1).to_broadcast([P, HID])).then_inc(S["consts_loaded"], 16)
            act.dma_start(gi[:], g_in.rearrange("(o n) -> o n", o=1).to_broadcast([P, HID])).then_inc(S["consts_loaded"], 16)
            act.dma_start(go[:], g_out.rearrange("(o n) -> o n", o=1).to_broadcast([P, FFN])).then_inc(S["consts_loaded"], 16)
            with nc.allow_non_contiguous_dma(reason="a few hundred numbers"):
                act.dma_start(cb[:], chunks(conv_b, IC)).then_inc(S["consts_loaded"], 16)
                act.dma_start(bdt[:], chunks(b_dt, IC)).then_inc(S["consts_loaded"], 16)
                act.dma_start(dsk[:], chunks(d_skip, IC)).then_inc(S["consts_loaded"], 16)
            act.dma_start(A[:], a_log.rearrange("(c p) s -> p c s", c=IC)).then_inc(S["consts_loaded"], 16)
            act.dma_start(wx[:], w_x.rearrange("(c p) n -> p c n", c=IC)).then_inc(S["conv_loaded"], 16)
            act.wait_ge(S["consts_loaded"], 16 * n_const)
            own.then(act.activation(A[:], A[:], ACT.Exp))
            act.activation(A[:], A[:], ACT.Copy, scale=-1.0).then_inc(S["a_ready"], 1)

            def normal_T(t, j, par):
                wait(act, S["xn_turned"], t + 1)
                if j == 0:
                    wait(act, S["z_ready"], t)
                act.activation(xnT[:, :, j * P:(j + 1) * P],
                               bank(6 + par, 2 * P, HC).rearrange("p (c n) -> p c n", c=2),
                               ACT.Copy).then_inc(S["xnT_ready"], 1)

            def z_sigmoid(t, j, par):
                z = bank((3, 4, 5, 3)[j], INNER)
                wait(act, S["z_ready"], t + 1)
                wait(act, S["z_used"], t - 1 if j else t)
                own.then(act.activation(zs[par], z, ACT.Exp, scale=-1.0))
                own.then(act.activation(zs[par], zs[par], ACT.Ln, bias=1.0))
                act.activation(zs[par], zs[par], ACT.Exp, scale=-1.0).then_inc(S["zsig_ready"], 1)

            normal_T(0, 0, 0)
            wait(act, S["xin_ready"], 3)
            act.activation(xinT[:, 0:2, P:2 * P], ps[:, 0:2 * BANK].rearrange("p (c n) -> p c n", c=2)[:, :, 0:P],
                           ACT.Copy).then_inc(S["xin_act"], 1)
            z_sigmoid(0, 0, 0)
            with act.Fori(0, GRID) as g:
                own.enter(g, 2 * GRID)
                for j in range(GRID):
                    t = g * GRID + 1 + j
                    act.wait_ge(S["patch_turned"], t)
                    act.wait_ge(*product_read(g, j))
                    act.activation(patch[j % 2][:, 0:4, :],
                                   bank(2 * (j % 2)).rearrange("p (c n) -> p c n", c=4),
                                   ACT.Copy).then_inc(S["patch_act"], 1)
                for j in range(GRID):
                    normal_T(g * GRID + 1 + j, j, (1 + j) % 2)
                act.wait_ge(S["xin_ready"], 3 * g + 6)
                for c in range(2):
                    last = act.activation(xinT[:, c, bass.ds((g * GRID + 2) * P, GRID * P)], bank(c), ACT.Copy)
                last.then_inc(S["xin_act"], 1)
                for j in range(GRID):
                    z_sigmoid(g * GRID + 1 + j, j, (1 + j) % 2)
                own.leave(GRID)

            def linear(n_, dst, bias, cols):
                wait(act, S["lin_ready"], n_ + 1)
                return act.activation(dst, bank(5, cols), ACT.Identity, bias=bias)

            def conv_chunk(q_, m, n):
                wait(act, S["delta_ready"], q_)
                linear(6 * q_ + m, xb[:, m, 0:n], cb[:, m:m + 1], n).then_inc(S["lin_used"], 1)

            def conv_sigmoid(q_, n):
                act.wait_ge(S["lin_used"], 6 * q_ + 3)
                own.then(act.activation(sg[:, :, 0:n], xb[:, :, 0:n], ACT.Exp, scale=-1.0))
                own.then(act.activation(sg[:, :, 0:n], sg[:, :, 0:n], ACT.Ln, bias=1.0))
                act.activation(sg[:, :, 0:n], sg[:, :, 0:n], ACT.Exp, scale=-1.0).then_inc(S["sig_ready"], 1)

            def delta_chunk(q_, m, n):
                wait(act, S["xc_ready"], q_ + 1)
                linear(6 * q_ + 3 + m, db[:, m, 0:n], bdt[:, m:m + 1], n).then_inc(S["lin_used"], 1)

            def softplus(q_, n):
                act.wait_ge(S["lin_used"], 6 * q_ + 6)
                own.then(act.activation(sp[:, :, 0:n], db[:, :, 0:n], ACT.Exp))
                act.activation(sp[:, :, 0:n], sp[:, :, 0:n], ACT.Ln, bias=1.0).then_inc(S["sp_ready"], 1)

            def decays(pair, s_):
                if s_ in (0, CH):
                    act.wait_ge(S["delta_ready"], pair + 2)
                wait(act, S["decay_turned"], (2 * pair - 1) * DC + (IC * s_ + IC - 1) * P // BANK + 1)
                for c in range(IC):
                    last = act.activation(decay[:, s_, c, :], dltT[:, c, :], ACT.Exp, scale=A[:, c, s_:s_ + 1])
                last.then_inc(S["decay_made"], 1)

            def bc_copy(q_, tiles=2):
                wait(act, S["bc_ready"], q_ + 1)
                wait(act, S["bc_copied"], 2 * q_ - 1)
                act.activation(bcn[:].rearrange("p t n -> p (t n)")[:, 0:tiles * 2 * STATE],
                               bank(3, tiles * 2 * STATE), ACT.Copy).then_inc(
                    S["bcn_ready"], 1)

            def d_term(t):
                act.wait_ge(S["dx_turned"], t + 1)
                wait(act, S["y_dve"], (t - 1) * CH + 1)
                act.activation(dx[:], bank(3, INNER), ACT.Copy).then_inc(S["dx_ready"], 1)

            def step(t, j, pair):
                par = (1 + j) % 2
                has = lambda d: pair is not None and (not isinstance(pair, int) or pair < PAIRS - d)
                for k in range(CH):
                    if k == 0 and exists(t):
                        d_term(t)
                    if has(1) and j == 0:
                        if k == 0:
                            conv_chunk(pair + 2, 2, 2 * P)
                            conv_sigmoid(pair + 2, 2 * P)
                        if k in (3, 4, 5):
                            delta_chunk(pair + 2, k - 3, 2 * P)
                        if k == 6:
                            softplus(pair + 2, 2 * P)
                    if has(2) and j == 1 and k in (0, 4):
                        conv_chunk(pair + 3, k // 4, 2 * P)
                    if has(1) and j == 1 and k == 6:
                        bc_copy(pair + 2)
                    if has(0) and j == 0:
                        decays(pair, CH + k)
                    if has(1) and j == 1:
                        decays(pair + 1, k)
                    if k == 3 and exists(t - 1):
                        act.wait_ge(S["yz_turned"], t)
                        wait(act, S["o_ready"], t - 1)
                        act.activation(yzT[:].rearrange("p c n -> p (c n)"), bank(3, INNER),
                                       ACT.Copy).then_inc(S["yzT_ready"], 1)
                    if k == 5 and exists(t - 1):
                        act.wait_ge(S["o_ready"], t)
                        wait(act, S["o1_ready"], t - 1)
                        act.activation(ow[:], bank(3, HID), ACT.Copy).then_inc(S["ow_ready"], 1)
                    if k == 6 and exists(t - 2):
                        act.wait_ge(S["s1_ready"], t - 1)
                        wait(act, S["q1_turned"], t - 2)
                        act.activation(t1, wq, ACT.Copy, bias=ROUND, scale=s1[:, 4:5]).then_inc(S["t1_ready"], 1)
                    if k == 5 and exists(t - 3):
                        act.wait_ge(S["f1_ready"], t - 2)
                        own.then(act.activation(sig, bank(6), ACT.Exp, scale=c1[:, 1 - par, 1:2]))
                        own.then(act.activation(sig, sig, ACT.Ln, bias=1.0))
                        act.activation(sig, sig, ACT.Exp, scale=-1.0).then_inc(S["fsig_ready"], 1)
                    if k == 0 and exists(t - 4):
                        act.wait_ge(S["f1_used"], t - 3)
                        wait(act, S["s2_ready"], t - 4)
                        act.activation(sq[:], y2[:], ACT.Square, accum_out=ss[:]).then_inc(S["sumsq_ready"], 1)
                    if k == 5 and exists(t - 4):
                        act.wait_ge(S["s2_ready"], t - 3)
                        wait(act, S["q2_turned"], t - 4)
                        act.activation(t2[:], v2[:], ACT.Copy, bias=ROUND, scale=s2[:, 7:8]).then_inc(S["t2_ready"], 1)

            for q_, n in ((0, P), (1, 2 * P)):
                for m in range(IC):
                    conv_chunk(q_, m, n)
                if q_ == 1:
                    d_term(0)
                conv_sigmoid(q_, n)
                for m in range(IC):
                    delta_chunk(q_, m, n)
                softplus(q_, n)
                bc_copy(q_, n // P)
            for m in range(2):
                conv_chunk(2, m, 2 * P)
            for s_ in range(CH):
                decays(0, s_)
            walk(act, step, own, ACT_STEPS)

        @block.vector
        def _(dve):
            own = Steps(dve, S["dve_step"], apart)
            dve.wait_ge(S["raws_loaded"], 48)
            own.then(dve.memset(wsum[:], 0.0))
            dve.tensor_reduce(wsum[:, 0:1], raw1, AX.XY, ALU.add, apply_absolute_value=True)
            dve.tensor_reduce(wsum[0:HC, 1:2], raw2, AX.XY, ALU.add,
                              apply_absolute_value=True).then_inc(S["wsum_ready"], 1)
            dve.wait_ge(S["wsum_ready"], 2)
            for i, n in enumerate((2 * FFN * HID, FFN * HID)):
                last = dve.tensor_scalar(ws[:, i:i + 1], bank(7, 2)[:, i:i + 1], 1.0 / n, 1e-5, ALU.mult, ALU.max)
            last.then_inc(S["ws_ready"], 1)
            dve.wait_ge(S["ws_inverse"], 1)
            for i, w in ((0, raw1), (1, raw2)):
                rows_ = w.shape[0]
                own.then(dve.tensor_scalar(w, w, wsc[0:rows_, i:i + 1], 1.0, ALU.mult, ALU.min))
                dve.tensor_scalar(w, w, -1.0, ROUND, ALU.max, ALU.add).then_inc(S["raw_scaled"], 1)
            for k in range(KP):
                dve.wait_ge(S["tok_turned"], k + 1)
                dve.tensor_copy(twT[:, k, :], bank(k % 2, HID)).then_inc(S["raw_turned"], 1)
            for c in range(8):
                dve.wait_ge(S["tok_turned"], KP + c + 1)
                dve.tensor_scalar(f1[:, :, c * P:(c + 1) * P],
                                  bank(c % 2, 2 * P, HC).rearrange("p (c n) -> p c n", c=2), ROUND, None,
                                  ALU.subtract).then_inc(S["raw_turned"], 1)
            for c in range(FC):
                dve.wait_ge(S["tok_turned"], KP + 8 + c + 1)
                dve.tensor_scalar(f2[:, c, :], bank(c % 2, HID), ROUND, None,
                                  ALU.subtract).then_inc(S["raw_turned"], 1)

            def normalise(t, j, par, src):
                own.then(dve.bn_stats(st[:], src))
                dve.bn_aggr(mv[par][:], st[:]).then_inc(S["mv_ready"], 1)
                wait(dve, S["rs_ready"], t + 1)
                wait(dve, S["xn_turned"], t - j)
                dve.tensor_scalar(xn[j], src, mv[par][:, 0:1], rs[par][:, 1:2], ALU.subtract,
                                  ALU.mult).then_inc(S["xn_ready"], 1)

            def z_gate(t, j, par, kept):
                wait(dve, S["zsig_ready"], t + 1)
                dve.tensor_tensor(kept, bank((3, 4, 5, 3)[j], INNER), zs[par], ALU.mult).then_inc(S["z_used"], 1)

            dve.wait_ge(S["consts_loaded"], 16 * n_const)
            normalise(0, 0, 0, res[:, 0, :])
            dve.wait_ge(S["xin_ready"], 3)
            dve.tensor_copy(xinT[:, 2, P:2 * P], bank(2, P)).then_inc(S["xin_dve"], 1)
            z_gate(0, 0, 0, gate[0][:])
            dve.wait_ge(S["pos_ready"], 1)
            with dve.Fori(0, GRID) as g:
                own.enter(g, 2 * GRID)

                def patch_copy(j):
                    t = g * GRID + 1 + j
                    dve.wait_ge(S["patch_turned"], t)
                    dve.wait_ge(*product_read(g, j))
                    dve.tensor_copy(patch[j % 2][:, 4:6, :],
                                    bank(2 * (j % 2) + 1, 2 * P).rearrange("p (c n) -> p c n", c=2)
                                    ).then_inc(S["patch_dve"], 1)

                patch_copy(0)
                for j in range(GRID):
                    if j + 1 < GRID:
                        patch_copy(j + 1)
                    t = g * GRID + 1 + j
                    dve.wait_ge(S["emb_ready"], t)
                    e = res[:, bass.ds(t, 1), :].rearrange("p o n -> p (o n)")
                    own.then(dve.tensor_tensor(e, bank(4 + j % 2, HID),
                                               pos[:, bass.ds(t, 1), :].rearrange("p o n -> p (o n)"), ALU.add))
                    normalise(t, j, (1 + j) % 2, e)
                dve.wait_ge(S["xin_ready"], 3 * g + 6)
                dve.tensor_copy(xinT[:, 2, bass.ds((g * GRID + 2) * P, GRID * P)], bank(2)).then_inc(S["xin_dve"], 1)
                for j in range(GRID):
                    z_gate(g * GRID + 1 + j, j, (1 + j) % 2,
                           state[:, bass.ds(g * GRID + j, 1), :].rearrange("p o n -> p (o n)"))
                own.leave(GRID)

            def make_delta(q_, n):
                dve.wait_ge(S["sp_ready"], q_ + 1)
                wait(dve, S["decay_made"], 16 * (q_ - 1))
                wait(dve, S["uT_ready"], q_)
                dve.scalar_tensor_tensor(dltT[:, :, 0:n], sp[:, :, 0:n], 80.0, db[:, :, 0:n], ALU.min,
                                         ALU.max).then_inc(S["delta_ready"], 1)

            u = bank(4, INNER)

            def copy_bc(t, j, par, place):
                wait(dve, S["bcn_ready"], place)
                wait(dve, S["rows_read"], (t - 1) * POOL_SLOTS)
                dve.tensor_copy(bc[:, par, :], bcn[:, j, :]).then_inc(S["bc_copied"], 1)
                wait(dve, S["bc_copied"], t + 1)

            def decay_state(t, i):
                dve.wait_ge(S["decay_turned"], (t - 1) * DC + i + 1)
                dve.wait_ge(S["rows_read"], (t - 1) * POOL_SLOTS + (BANK * (i + 1) - 1) // (2 * INNER) // 2 + 1)
                h = state[:].rearrange("p s n -> p (s n)")[:, i * BANK:(i + 1) * BANK]
                dve.tensor_tensor(h, bank(i % DB), h, ALU.mult).then_inc(S["decay_used"], 1)

            def add_input(t, par, k):
                dve.wait_ge(S["decay_used"], (t - 1) * DC + chunks_of(k)[-1] + 1)
                for r in range(2):
                    s_ = 2 * k + r
                    last = dve.scalar_tensor_tensor(state[:, s_, :], u, bc[:, par, s_:s_ + 1], state[:, s_, :],
                                                    ALU.mult, ALU.add)
                last.then_inc(S["state_ready"], 1)

            def output(t, par, k, r):
                s_, n = 2 * k + r, k - 1 + r
                if n == 0:
                    dve.wait_ge(S["dx_ready"], t + 1)
                    wait(dve, S["yz_ready"], t)
                    before = dx
                else:
                    wait(dve, S["y_dve"], t * CH + n)
                    before = ydve
                dve.wait_ge(S["state_ready"], t * CH + k + 1)
                dve.scalar_tensor_tensor(ydve[:], state[:, s_, :], bc[:, par, STATE + s_:STATE + s_ + 1], before[:],
                                         ALU.mult, ALU.add).then_inc(S["y_dve"], 1)

            def step(t, j, pair):
                par = (1 + j) % 2
                has = lambda d: pair is not None and (not isinstance(pair, int) or pair < PAIRS - d)
                flat = lambda a: a.rearrange("p o n -> p (o n)")
                scan = exists(t)
                if scan and pair is not None:
                    copy_bc(t, j, par, pair + 2)
                for k in range(CH):
                    if k == 0 and exists(t - 1):
                        output(t - 1, 1 - par, CH - 1, 0)
                    if scan:
                        for i in chunks_of(k):
                            decay_state(t, i)
                    if k == 1 and exists(t - 1):
                        wait(dve, S["y_dve"], t * CH)
                        wait(dve, S["y_ready"], t)
                        dve.tensor_tensor(ydve[:], ysum[:], ydve[:], ALU.add).then_inc(S["y_joined"], 1)
                    if k == 2 and exists(t - 1):
                        dve.wait_ge(S["y_joined"], t)
                        wait(dve, S["yz_turned"], t - 1)
                        loads = (t - 1) // 2 if isinstance(t, int) else pair
                        if 1 - par:
                            dve.wait_ge(S["gate_odd_in"], 16 * loads + 16)
                        else:
                            wait(dve, S["gate_even_in"], 16 * loads)
                        dve.tensor_tensor(yz, ydve[:], gate[1 - par][:],
                                          ALU.mult).then_inc(S["yz_ready"], 1)
                    if k == 6 and exists(t - 1):
                        apart(dve, S["ow_ready"], t)
                        own.then(dve.bn_stats(stA[:], ow[:]))
                        dve.bn_aggr(mvA[:], stA[:]).then_inc(S["mvA_ready"], 1)
                    if k == 0 and exists(t - 2):
                        dve.wait_ge(S["rsA_ready"], t - 1)
                        wait(dve, S["h1_ready"], t - 2)
                        dve.tensor_scalar(o1, ow[:], mvA[:, 0:1], rsA[:, 1:2], ALU.subtract,
                                          ALU.mult).then_inc(S["o1_ready"], 1)
                    if k == 3 and exists(t - 2):
                        apart(dve, S["h1_ready"], t - 1)
                        h1 = flat(res[:, bass.ds(t - 2, 1), :])
                        own.then(dve.bn_stats(stF[:], h1))
                        apart(dve, S["s1_ready"], t - 2)
                        own.then(dve.bn_aggr(mvF[:], stF[:]))
                        wait(dve, S["t1_ready"], t - 2)
                        own.then(dve.scalar_tensor_tensor(wq, h1, mvF[:, 0:1], gi[:], ALU.subtract, ALU.mult))
                        dve.tensor_reduce(amF[:], wq, AX.X, ALU.max, apply_absolute_value=True).then_inc(
                            S["w_ready"], 1)
                    if k == 1 and exists(t - 3):
                        dve.wait_ge(S["q1_turned"], t - 2)
                        wait(dve, S["f1_ready"], t - 3)
                        dve.tensor_scalar(q1[:], bank(6, 2 * P, HC).rearrange("p (c n) -> p c n", c=2), ROUND, None,
                                          ALU.subtract).then_inc(S["q1_ready"], 1)
                    if k == 7 and exists(t - 3):
                        dve.wait_ge(S["fsig_ready"], t - 2)
                        own.then(dve.tensor_tensor(aa, bank(7), sig, ALU.mult))
                        wait(dve, S["v2_ready"], t - 3)
                        wait(dve, S["sumsq_ready"], t - 3)
                        dve.tensor_tensor(y2[:], bank(6), aa, ALU.mult).then_inc(S["f1_used"], 1)
                    if k == 2 and exists(t - 4):
                        dve.wait_ge(S["v2_ready"], t - 3)
                        wait(dve, S["s2_ready"], t - 4)
                        dve.tensor_reduce(am2[:], v2[:], AX.X, ALU.max, apply_absolute_value=True).then_inc(
                            S["am2_ready"], 1)
                    if k == 1 and exists(t - 5):
                        dve.wait_ge(S["q2_turned"], t - 4)
                        wait(dve, S["f2_ready"], t - 5)
                        dve.tensor_scalar(q2[:].rearrange("p c n -> p (c n)"), bank(7), ROUND, None,
                                          ALU.subtract).then_inc(S["q2_ready"], 1)
                    if k == 3 and exists(t - 5):
                        dve.wait_ge(S["f2_ready"], t - 4)
                        r = flat(res[:, bass.ds(t - 5, 1), :])
                        dve.wait_ge(S["s2_ready"], t - 4)
                        dve.scalar_tensor_tensor(r, bank(7, HID), c2[:, 1 - par:2 - par], r, ALU.mult,
                                                 ALU.add).then_inc(S["final_ready"], 1)
                    if k == 7 and j == 0 and has(1):
                        make_delta(pair + 2, 2 * P)
                    if scan and k % 2 == 0 and k > 0:
                        output(t, par, k - 1, 0)
                    if scan:
                        if k == 0:
                            dve.wait_ge(S["u_turned"], t + 1)
                        add_input(t, par, k)
                    if k == 0 and exists(t - 1):
                        output(t - 1, 1 - par, CH - 1, 1)
                    if scan and k % 2 == 0 and k > 0:
                        output(t, par, k - 1, 1)

            make_delta(0, P)
            make_delta(1, 2 * P)
            copy_bc(0, 0, 0, 1)
            dve.wait_ge(S["gate_kept"], 16 * GRID)
            dve.wait_ge(S["u_turned"], 1)
            for k in range(CH):
                for r in range(2):
                    s_ = 2 * k + r
                    last = dve.tensor_scalar(state[:, s_, :], u, bc[:, 0, s_:s_ + 1], None, ALU.mult)
                last.then_inc(S["state_ready"], 1)
            for k in range(1, CH - 1, 2):
                for r in range(2):
                    output(0, 0, k, r)
            walk(dve, step, own, DVE_STEPS)

        @block.tensor
        def _(pe):
            pe.wait_ge(S["ones_set"], 1)
            pe.wait_ge(S["wsum_ready"], 1)
            pe.matmul(bank(7, 2), ones[:], wsum[:], start=True, stop=True).then_inc(S["wsum_ready"], 1)
            pe.wait_ge(S["ident_built"], 1)
            pe.wait_ge(S["raws_loaded"], 48)
            n = 0
            for k in range(KP):
                wait(pe, S["raw_turned"], n - 1)
                for c in range(2):
                    last = pe.transpose(bank(k % 2, HC, off=c * HC), rawT[:, c, k * P:(k + 1) * P], ident[0:HC, 0:HC])
                last.then_inc(S["tok_turned"], 1)
                n += 1
            pe.wait_ge(S["raw_scaled"], 2)
            for c in range(8):
                wait(pe, S["raw_turned"], n - 1)
                for h in range(2):
                    last = pe.transpose(bank(c % 2, P, HC, h * P), raw1[:, c, h * HC:(h + 1) * HC], ident[:])
                last.then_inc(S["tok_turned"], 1)
                n += 1
            for c in range(FC):
                wait(pe, S["raw_turned"], n - 1)
                for h in range(2):
                    last = pe.transpose(bank(c % 2, HC, off=h * HC), raw2[:, h, c * P:(c + 1) * P], ident[0:HC, 0:HC])
                last.then_inc(S["tok_turned"], 1)
                n += 1

            def turn_normal(t, j, par):
                wait(pe, S["xn_ready"], t + 1)
                wait(pe, S["xnT_ready"], t - 1 if j else t)
                for c in range(2):
                    last = pe.transpose(bank(6 + par, P, HC, c * P), xn[j][:, c * HC:(c + 1) * HC], ident[:])
                last.then_inc(S["xn_turned"], 1)

            def project(t0, tiles, g1):
                wait(pe, S["xnT_ready"], t0 + tiles)
                for m in range(IC):
                    for c in range(2):
                        last = pe.matmul(bank(m, tiles * P), wi[:, c, m * P:(m + 1) * P], xnT[:, c, 0:tiles * P],
                                         start=(c == 0), stop=(c == 1))
                    last.then_inc(S["xin_ready"], 1)
                for j in range(tiles):
                    if j == 0:
                        wait(pe, S["z_used"], t0)
                    if j == 3:
                        pe.wait_ge(S["z_used"], t0 + 1)
                    for c in range(2):
                        last = pe.matmul(bank((3, 4, 5, 3)[j], INNER), xnT[:, c, j * P:(j + 1) * P],
                                         wi[:, c, INNER:2 * INNER], start=(c == 0), stop=(c == 1))
                    last.then_inc(S["z_ready"], 1)

            pe.wait_ge(S["raw_turned"], n)
            pe.wait_ge(S["consts_loaded"], 16 * n_const)
            turn_normal(0, 0, 0)
            project(0, 1, 0)

            with pe.Fori(0, GRID) as g:

                def turn_patch(j):
                    t = g * GRID + 1 + j
                    if j == 0:
                        pe.wait_ge(S["xin_act"], g + 1)
                    if j == 1:
                        pe.wait_ge(S["xin_dve"], g + 1)
                        pe.wait_ge(S["z_used"], t - 1)
                    if j >= 2:
                        pe.wait_ge(S["patch_act"], t - 2)
                        pe.wait_ge(S["patch_dve"], t - 2)
                    pe.wait_ge(S["patch_packed"], t)
                    for k in range(KP):
                        last = pe.transpose(bank(2 * (j % 2) + k // 4, P, off=(k % 4) * P),
                                            px[j % 2][:, k * P:(k + 1) * P], ident[:])
                    last.then_inc(S["patch_turned"], 1)

                turn_patch(0)
                for j in range(GRID):
                    if j + 1 < GRID:
                        turn_patch(j + 1)
                    t = g * GRID + 1 + j
                    pe.wait_ge(S["patch_act"], t)
                    pe.wait_ge(S["patch_dve"], t)
                    if j >= 2:
                        pe.wait_ge(S["mv_ready"], t - 1)
                    for k in range(KP):
                        last = pe.matmul(bank(4 + j % 2, HID), patch[j % 2][:, k, :], twT[:, k, :],
                                         start=(k == 0), stop=(k == KP - 1))
                    last.then_inc(S["emb_ready"], 1)
                for j in range(GRID):
                    turn_normal(g * GRID + 1 + j, j, (1 + j) % 2)
                project(g * GRID + 1, GRID, g + 1)

            def conv_taps(q_, m, n, taps, first_tile):
                if 0 in taps:
                    wait(pe, S["lin_used"], 6 * q_ + m)
                for tap in taps:
                    for c in range(IC):
                        last = pe.matmul(bank(5, n), cw[:, tap, c, m * P:(m + 1) * P],
                                         xinT[:, c, bass.ds((first_tile + tap) * P, n)],
                                         start=(tap == 0 and c == 0), stop=(tap == TAPS - 1 and c == IC - 1))
                if TAPS - 1 in taps:
                    last.then_inc(S["lin_ready"], 1)

            def delta_product(q_, m, n):
                wait(pe, S["xc_ready"], q_ + 1)
                wait(pe, S["lin_used"], 6 * q_ + 3 + m)
                for c in range(IC):
                    last = pe.matmul(bank(5, n), wdt[:, c, m * P:(m + 1) * P], xcT[:, c, 0:n],
                                     start=(c == 0), stop=(c == IC - 1))
                last.then_inc(S["lin_ready"], 1)

            def bc_product(q_, tiles, o_copied):
                wait(pe, S["xc_ready"], q_ + 1)
                wait(pe, S["ow_ready"], o_copied)
                for j in range(tiles):
                    for c in range(IC):
                        last = pe.matmul(bank(3, 2 * STATE, off=2 * STATE * j),
                                         xcT[:, c, j * P:(j + 1) * P], wx[:, c, :],
                                         start=(c == 0), stop=(c == IC - 1))
                last.then_inc(S["bc_ready"], 1)

            def turn_inputs(t, j, q_):
                wait(pe, S["uT_ready"], q_ + 1)
                wait(pe, S["state_ready"], t * CH)
                for c in range(IC):
                    last = pe.transpose(bank(4, P, off=c * P), uT[:, c, j * P:(j + 1) * P], ident[:])
                last.then_inc(S["u_turned"], 1)
                wait(pe, S["dxT_ready"], q_ + 1)
                wait(pe, S["bcn_ready"], q_ + 1)
                wait(pe, S["ow_ready"], t - 1)
                for c in range(IC):
                    last = pe.transpose(bank(3, P, off=c * P), dxT[:, c, j * P:(j + 1) * P], ident[:])
                last.then_inc(S["dx_turned"], 1)

            def turn_decays(t, j, pair, i):
                pe.wait_ge(S["decay_made"], 16 * pair + (4 * i + 3) // IC + 1)
                wait(pe, S["decay_used"], (t - 1) * DC + i + 1 - DB)
                for b in range(4 * i, 4 * i + 4):
                    last = pe.transpose(bank(i % DB, P, off=(b % 4) * P),
                                        decay[:, b // IC, b % IC, j * P:(j + 1) * P], ident[:])
                last.then_inc(S["decay_turned"], 1)

            def step(t, j, pair):
                par = (1 + j) % 2
                has = lambda d: pair is not None and (not isinstance(pair, int) or pair < PAIRS - d)
                for k in range(CH):
                    if exists(t) and k == 0:
                        turn_inputs(t, j, pair + 1)
                    if exists(t):
                        for i in chunks_of(k):
                            turn_decays(t, j, pair, i)
                    if k == 0 and exists(t - 3):
                        pe.wait_ge(S["t1_ready"], t - 2)
                        wait(pe, S["f1_used"], t - 3)
                        for c in range(2):
                            last = pe.transpose(bank(6, P, HC, c * P), t1[:, c * HC:(c + 1) * HC], ident[:])
                        last.then_inc(S["q1_turned"], 1)
                    if k == 0 and exists(t - 5):
                        pe.wait_ge(S["t2_ready"], t - 4)
                        wait(pe, S["f1_used"], min(t - 3, T) if isinstance(t, int) else t - 3)
                        wait(pe, S["final_ready"], t - 5)
                        for c in range(FC):
                            last = pe.transpose(bank(7, P, off=c * P), t2[:, c * P:(c + 1) * P], ident[:])
                        last.then_inc(S["q2_turned"], 1)
                    if k == 3 and exists(t - 1):
                        pe.wait_ge(S["yz_ready"], t)
                        pe.wait_ge(S["dx_ready"], min(t + 1, T) if isinstance(t, int) else t + 1)
                        for c in range(IC):
                            last = pe.transpose(bank(3, P, off=c * P), yz[:, c * P:(c + 1) * P], ident[:])
                        last.then_inc(S["yz_turned"], 1)
                    if k == 4 and exists(t - 1):
                        pe.wait_ge(S["yzT_ready"], t)
                        for c in range(IC):
                            last = pe.matmul(bank(3, HID), yzT[:, c, :], wo[:, c, :],
                                             start=(c == 0), stop=(c == IC - 1))
                        last.then_inc(S["o_ready"], 1)
                    if k == 4 and exists(t - 3):
                        pe.wait_ge(S["q1_ready"], t - 2)
                        wait(pe, S["final_ready"], t - 4)
                        for half in range(2):
                            for c in range(2):
                                last = pe.matmul(bank(6 + half), q1[:, c, :],
                                                 f1[:, c, (1 - half) * FFN:(2 - half) * FFN],
                                                 start=(c == 0), stop=(c == 1))
                        last.then_inc(S["f1_ready"], 1)
                    if k == 2 and exists(t - 5):
                        pe.wait_ge(S["q2_ready"], t - 4)
                        for c in range(FC):
                            last = pe.matmul(bank(7, HID), q2[:, c, :], f2[:, c, :],
                                             start=(c == 0), stop=(c == FC - 1))
                        last.then_inc(S["f2_ready"], 1)
                    if has(1):
                        if j == 0 and 2 <= k < 5:
                            delta_product(pair + 2, k - 2, 2 * P)
                        if j == 1 and k == 5:
                            bc_product(pair + 2, 2, t)
                    if has(2):
                        if j == 0 and k >= 5:
                            conv_taps(pair + 3, 0, 2 * P, ((0,), (1, 2), (3,))[k - 5], pair * 2 + 5)
                        if j == 1:
                            conv_taps(pair + 3, 1 + k // 4, 2 * P, (k % 4,), pair * 2 + 5)

            pe.wait_ge(S["conv_loaded"], 16 * (n_conv + 1))
            pe.wait_ge(S["pads_zeroed"], 1)
            pe.wait_ge(S["xin_act"], GRID + 1)
            pe.wait_ge(S["xin_dve"], GRID + 1)
            pe.wait_ge(S["z_used"], T)
            for m in range(IC):
                conv_taps(0, m, P, range(TAPS), 0)
            for m in range(IC):
                delta_product(0, m, P)
            bc_product(0, 1, 0)
            for m in range(IC):
                conv_taps(1, m, 2 * P, range(TAPS), 1)
            turn_inputs(0, 0, 0)
            for m in range(IC):
                delta_product(1, m, 2 * P)
            bc_product(1, 2, 0)
            for m in range(IC):
                conv_taps(2, m, 2 * P, range(TAPS), 3)
            walk(pe, step, None, 0)


FIRST_LOOPED, LOOPED = 2, 4
POOL_STEPS, ACT_STEPS, DVE_STEPS = 32, 7, 10


def walk(eng, step, own, per_turn):
    def both(pair):
        for j in range(2):
            step(pair * 2 + 1 + j, j, pair)

    for pair in range(FIRST_LOOPED):
        both(pair)
    with eng.Fori(FIRST_LOOPED, FIRST_LOOPED + LOOPED) as pair:
        if own:
            own.enter(pair - FIRST_LOOPED, per_turn)
        both(pair)
        if own:
            own.leave(LOOPED)
    for pair in range(FIRST_LOOPED + LOOPED, PAIRS):
        both(pair)
    for t in range(T, T + LAST_LAG - 1):
        step(t, (t + 1) % 2, None)


_INS = ["x", "cls_tok", "L0_tok_conv_w", "L0_tok_conv_b", "L0_tok_pos_table", "L0_attn_W_in", "L0_attn_conv_w",
        "L0_attn_conv_b", "L0_attn_W_x", "L0_attn_W_dt", "L0_attn_b_dt", "L0_attn_A_log", "L0_attn_D",
        "L0_attn_W_out", "L0_attn_gamma", "L0_attn_beta", "L0_ffn_w_in", "L0_ffn_g_in", "L0_ffn_w_out",
        "L0_ffn_g_out"]


def kernel(**inputs):
    import concourse.bacc as bacc
    from concourse.bass_utils import run_bass_kernel_spmd

    nc = bacc.Bacc("TRN2", target_bir_lowering=False, num_devices=1)
    arrays, args = {}, []
    for name in _INS:
        a = np.ascontiguousarray(inputs[name])
        arrays[f"in_{name}"] = a
        args.append(nc.dram_tensor(f"in_{name}", a.shape, mybir.dt.from_np(a.dtype), kind="ExternalInput").ap())
    args.append(nc.dram_tensor("out", (P, T, HID), F32, kind="ExternalOutput").ap())
    vit_block(nc, *args)
    r = run_bass_kernel_spmd(nc, [arrays], core_ids=[0])
    return r.results[0]["out"]
```

```python
from contextlib import ExitStack

import numpy as np
import concourse.bass as bass
import concourse.mybir as mybir

F32 = mybir.dt.float32
BF16 = mybir.dt.bfloat16
ACT = mybir.ActivationFunctionType
ALU = mybir.AluOpType
AX = mybir.AxisListType

P = 128
SIDE, PATCH, GRID = 64, 16, 4
T = 1 + GRID * GRID
HID, HC = 192, 96
KP = 3 * PATCH * PATCH // P
INNER, IC = 384, 3
STATE, TAPS = 16, 4
FFN, FC = 512, 4
PAIRS = (T - 1) // 2
CH = STATE // 2
BANK = 512
DC = STATE * INNER // BANK
DVE_OUT = (3, 7)
ACT_OUT = tuple(k for k in range(CH) if k not in DVE_OUT)
DECAYS_EARLY = ((), (0, 1), (2,), (3, 4), (5,), (6, 7), (8,), (9, 10))
DECAYS_LATE = ((11,), (12,), (13,), (14,), (15,), (), (), ())
D_SLOT = 2
DB = 2
LIN = (5, 2)
TURN_BANKS = 6
XIN_BANKS = (2, 3, 4)
Z_BANKS = (5, 7, 6, 2)
ROUND = 12582912.0
SHARED = 16832
LAST_LAG = 6
POS_TABLE_SIDE = 32


class Steps:

    def __init__(self, eng, sem, apart=None):
        self.eng, self.sem, self.n, self.turns, self.apart = eng, sem, 0, 0, apart

    def mark(self, ins):
        ins.then_inc(self.sem, 1)
        self.n += 1
        return self.n

    def wait(self, n):
        if self.apart:
            self.apart(self.eng, self.sem, self.turns + n)
        else:
            self.eng.wait_ge(self.sem, self.turns + n)

    def then(self, ins):
        self.wait(self.mark(ins))

    def enter(self, turn, per_turn):
        self.first, self.per_turn, self.turns = self.n, per_turn, turn * per_turn

    def leave(self, turns):
        assert self.n - self.first == self.per_turn, (self.sem, self.n - self.first)
        self.n, self.turns = self.first + turns * self.per_turn, 0


def wait(eng, sem, value):
    if not isinstance(value, int) or value > 0:
        eng.wait_ge(sem, value)


def chunks_of(k):
    upto = lambda states: -(-states * INNER // BANK)
    return range(upto(2 * k), upto(2 * k + 2))


def last_slot(i):
    return (BANK * (i + 1) - 1) // (2 * INNER)


def conv_bank(q, m):
    early = {(1, 0): 0, (1, 1): 1, (1, 2): 6, (2, 0): 7, (2, 1): 6}
    return early[q, m] if isinstance(q, int) and (q, m) in early else LIN[m % 2]


def delta_bank(m):
    return LIN[(1 + m) % 2]


def exists(tile):
    return not isinstance(tile, int) or 0 <= tile < T


def vit_block(nc, x, cls_tok, tok_w, tok_b, pos_table, w_in, conv_w, conv_b, w_x, w_dt, b_dt, a_log, d_skip,
              w_out, gamma, beta, f_in, g_in, f_out, g_out, out):
    ctx = ExitStack()
    with ctx:
        def sb(name, shape, dt=F32):
            return ctx.enter_context(nc.sbuf_tensor(name, shape, dt))

        def sem(name):
            return ctx.enter_context(nc.semaphore(name))

        ident = sb("ident", [P, P])
        ones = sb("ones", [P, P])
        mhalf = sb("mhalf", [P, 1])
        mone = sb("mone", [P, 1])
        res = sb("res", [P, T, HID])
        gate = [sb(f"gate{i}", [P, INNER]) for i in range(2)]
        xinT = sb("xinT", [P, IC, (T + 3) * P])
        cw = sb("cw", [P, TAPS, IC, INNER])
        wdt = sb("wdt", [P, IC, INNER])
        wx = sb("wx", [P, IC, 2 * STATE])
        wo = sb("wo", [P, IC, HID])
        cb = sb("cb", [P, IC])
        bdt = sb("bdt", [P, IC])
        dsk = sb("dsk", [P, IC])
        A = sb("A", [P, IC, STATE])
        gam = sb("gam", [P, HID])
        gi = sb("gi", [P, HID])
        go = sb("go", [P, FFN])
        f1 = sb("f1", [HC, 2, 2 * FFN], BF16)
        f2 = sb("f2", [P, FC, HID], BF16)
        ws = sb("ws", [P, 2])
        state = sb("state", [P, STATE, INNER])
        xb = sb("xb", [P, IC, 2 * P])
        sg = sb("sg", [P, IC, 2 * P])
        db, sp = xb, sg
        xcT = sb("xcT", [P, IC, 2 * P])
        dltT = sb("dltT", [P, IC, 2 * P])
        uT = sb("uT", [P, IC, 2 * P])
        dxT = sb("dxT", [P, IC, 2 * P])
        bc = sb("bc", [P, 2, 2 * STATE])
        bcn = sb("bcn", [P, 2, 2 * STATE])
        ow = sb("ow", [P, HID])
        dx = sb("dx", [P, INNER])
        acc = sb("acc", [P, 2, INNER])
        ysum = sb("ysum", [P, INNER])
        ydve = sb("ydve", [P, INNER])
        shared = sb("shared", [P, SHARED])
        at = [0]

        def part(n):
            at[0] += n
            assert at[0] <= SHARED, at[0]
            return shared[:, at[0] - n:at[0]]

        xr = [part(3 * PATCH * SIDE).rearrange("p (c i w) -> p c i w", c=3, i=PATCH) for _ in range(2)]
        wi = part(2 * 2 * INNER)[0:HC].rearrange("p (c n) -> p c n", c=2)
        twT = part(KP * HID).rearrange("p (c n) -> p c n", c=KP)
        pos = part(T * HID).rearrange("p (t n) -> p t n", t=T)
        tb = part(HID)
        bet = part(HID)
        patch = [b[:].rearrange("p c n -> p (c n)").rearrange("p (c n) -> p c n", c=KP) for b in (xcT, dltT)]
        px = [b[:].rearrange("p c n -> p (c n)") for b in (uT, dxT, xb, sg)]
        xn = [part(HID) for _ in range(GRID)]
        xnT = part(2 * GRID * P)[0:HC].rearrange("p (c n) -> p c n", c=2)
        zs = [part(INNER) for _ in range(2)]
        raw = state[:].rearrange("p s n -> p (s n)")
        rawT = raw[0:HC, 0:2 * KP * P].rearrange("p (c n) -> p c n", c=2)
        raw1 = raw[:, 1536:1536 + 8 * HID].rearrange("p (c n) -> p c n", c=8)
        raw2 = raw[0:HC, 3072:3072 + 2 * FFN].rearrange("p (c n) -> p c n", c=2)
        at[0] = 0
        decay = part(STATE * IC * 2 * P).rearrange("p (s c n) -> p s c n", s=STATE, c=IC)
        prod = [part(2 * INNER).rearrange("p (s n) -> p s n", s=2) for _ in range(2)]
        yz, o1, wq, t1, sig, aa = (part(n) for n in (INNER, HID, HID, HID, FFN, FFN))
        yzT = sb("yzT", [P, IC, P])
        y2 = sb("y2", [P, FFN])
        v2 = sb("v2", [P, FFN])
        t2 = part(FFN)
        sq = part(FFN)
        q1 = sb("q1", [HC, 2, P], BF16)
        q2 = sb("q2", [P, FC, P], BF16)
        st = sb("st", [P, 6])
        mv = [sb(f"mv{i}", [P, 2]) for i in range(2)]
        rs = [sb(f"rs{i}", [P, 2]) for i in range(2)]
        stA = sb("stA", [P, 6])
        mvA = sb("mvA", [P, 2])
        rsA = sb("rsA", [P, 2])
        stF = sb("stF", [P, 6])
        mvF = sb("mvF", [P, 2])
        amF = sb("amF", [P, 1])
        s1 = sb("s1", [P, 5])
        c2 = sb("c2", [P, 2])
        c1 = sb("c1", [P, 2, 2])
        ss = sb("ss", [P, 1])
        am2 = sb("am2", [P, 1])
        s2 = sb("s2", [P, 8])
        wsum = sb("wsum", [P, 2])
        wsc = sb("wsc", [P, 2])

        gate_d = nc.dram_tensor("gate_d", (T - 1, P, INNER), F32, kind="Internal").ap()
        ps = ctx.enter_context(nc.psum_tensor("ps", [P, 8 * BANK], F32))

        def bank(b, n=BANK, rows=P, off=0):
            return ps[0:rows, b * BANK + off:b * BANK + off + n]

        S = {n: sem(n) for n in (
            "x_even x_odd consts_loaded raws_loaded conv_loaded ident_built ones_set raw_scaled raw_turned "
            "tok_turned wsum_ready ws_ready ws_inverse "
            "patch_packed patch_turned patch_act patch_dve emb_ready mv_ready rs_ready xn_ready "
            "xn_turned xnT_ready xin_ready xin_act xin_dve z_ready zsig_ready z_used "
            "act_step dve_step pool_step a_ready pads_zeroed "
            "conv_ready conv_used dlt_ready dlt_used sig_ready xc_ready sp_ready delta_ready uT_ready dxT_ready bc_ready bcn_ready bc_copied "
            "decay_made decay_turned decay_used u_turned dx_turned dx_ready state_ready rows_read y_ready "
            "gate_kept gate_even_in gate_odd_in yz_ready yz_turned yzT_ready o_ready ow_ready mvA_ready rsA_ready o1_ready h1_ready prod_used y_dve y_joined w_ready s1_ready t1_ready "
            "q1_turned q1_ready f1_ready fsig_ready f1_used v2_ready sumsq_ready am2_ready s2_ready t2_ready "
            "q2_turned q2_ready f2_ready final_ready stored").split()}

        def apart(eng, sem, value):
            if isinstance(value, int):
                wait(eng, sem, value)
            else:
                value = eng.lower_val(value)
                eng.wait_ge(S["consts_loaded"], 16 * n_const)
                eng.wait_ge(sem, value)

        def product_read(g, j):
            return (S["emb_ready"], g * GRID + j - 1) if j >= 2 else (S["xn_turned"], g * GRID + 1)

        block = ctx.enter_context(nc.Block())
        x_rows = x.rearrange("b c (g i) w -> g b c i w", g=GRID)
        n_const, n_conv = 15, 3

        def chunks(v, c):
            return v.rearrange("(c p) -> p c", c=c)

        @block.sync
        def _(sp_):
            q = sp_
            q.dma_start(rawT, tok_w.rearrange("(c p) k i j -> p c (k i j)", c=2)).then_inc(S["raws_loaded"], 16)
            q.dma_start(raw1, f_in.rearrange("(c p) n -> p c n", c=8)).then_inc(S["raws_loaded"], 16)
            q.dma_start(raw2, f_out.rearrange("(c p) n -> p c n", c=2)).then_inc(S["raws_loaded"], 16)
            q.dma_start(xr[0], x_rows[0]).then_inc(S["x_even"], 16)
            q.wait_ge(S["consts_loaded"], 16 * n_const)
            q.dma_start(xr[1], x_rows[1]).then_inc(S["x_odd"], 16)
            for tap_w, src in ((cw[:], conv_w.rearrange("t (c p) n -> p t c n", c=IC)),
                               (wdt[:], w_dt.rearrange("(c p) n -> p c n", c=IC)),
                               (wo[:], w_out.rearrange("(c p) n -> p c n", c=IC))):
                q.dma_start(tap_w, src).then_inc(S["conv_loaded"], 16)

            for g in range(GRID):
                if g + 2 < GRID:
                    q.wait_ge(S["patch_packed"], GRID * (g + 1))
                    q.dma_start(xr[g % 2], x_rows[g + 2]).then_inc(S[("x_even", "x_odd")[g % 2]], 16)
                q.wait_ge(S["z_used"], 1 + GRID * (g + 1))
                q.dma_start(gate_d[g * GRID:(g + 1) * GRID].rearrange("t p n -> p t n"),
                            state[:, g * GRID:(g + 1) * GRID, :]).then_inc(S["gate_kept"], 16)
            q.wait_ge(S["gate_kept"], 16 * GRID)

            def fetch_gate(t, par):
                wait(q, S["yz_ready"], t - 1)
                q.dma_start(gate[par][:], gate_d[bass.ds(t - 1, 1)].rearrange("o p n -> (o p) n")).then_inc(
                    S[("gate_even_in", "gate_odd_in")[par]], 16)

            def store(t):
                q.wait_ge(S["final_ready"], t + 1)
                q.dma_start(out[:, bass.ds(t, 1), :], res[:, bass.ds(t, 1), :]).then_inc(S["stored"], 16)

            for t in range(1, 5):
                fetch_gate(t, t % 2)
            with q.Fori(0, 6) as i:
                for h in range(2):
                    fetch_gate(2 * i + 5 + h, (1 + h) % 2)
                    store(2 * i + h)
            for t in range(12, T):
                store(t)
            q.wait_ge(S["stored"], 16 * T)

        @block.gpsimd
        def _(pool):
            own = Steps(pool, S["pool_step"], apart)
            pool.memset(mhalf[:], -0.5)
            pool.memset(mone[:], -1.0)
            pool.memset(ones[:], 1.0).then_inc(S["ones_set"], 1)
            own.then(pool.memset(ident[:], 0.0))
            pool.affine_select(out=ident[:], in_=ident[:], compare_op=ALU.not_equal, fill=1.0, base=0,
                               pattern=[[-1, P]], channel_multiplier=1).then_inc(S["ident_built"], 1)
            pool.memset(xinT[:, :, 0:P], 0.0)
            pool.memset(xinT[:, :, (T + 1) * P:(T + 3) * P], 0.0).then_inc(S["pads_zeroed"], 1)
            pool.wait_ge(S["ws_ready"], 1)
            pool.wait_ge(S["ones_set"], 1)
            pool.tensor_tensor(wsc[:], ws[:], mone[:].to_broadcast([P, 2]), ALU.pow).then_inc(S["ws_inverse"], 1)

            def root(t, par):
                apart(pool, S["mv_ready"], t + 1)
                own.then(pool.tensor_scalar(rs[par][:, 0:1], mv[par][:, 1:2], 1e-5, None, ALU.add))
                pool.tensor_tensor(rs[par][:, 1:2], rs[par][:, 0:1], mhalf[:], ALU.pow).then_inc(S["rs_ready"], 1)
                wait(pool, S["xn_ready"], t + 1)
                r = res[:, bass.ds(t, 1), :]
                pool.tensor_tensor(r, r, bet.rearrange("p (o n) -> p o n", o=1), ALU.add)

            def pack(n):
                g, j = n // GRID, n % GRID
                if j == 0:
                    pool.wait_ge(S[("x_even", "x_odd")[g % 2]], 16 * (g // 2) + 16)
                wait(pool, S["patch_turned"], n + 1 - GRID)
                pool.tensor_copy(px[j].rearrange("p (i n) -> p i n", n=PATCH),
                                 xr[g % 2].rearrange("p c i w -> p (c i) w")[
                                     :, :, j * PATCH:(j + 1) * PATCH]).then_inc(S["patch_packed"], 1)

            pack(0)
            pack(1)
            root(0, 0)
            pack(2)
            pack(3)
            for n in range(GRID * GRID):
                root(n + 1, (n + 1) % 2)
                if n + GRID < GRID * GRID:
                    pack(n + GRID)

            def conv_gate(q_, n):
                wait(pool, S["sig_ready"], q_ + 1)
                wait(pool, S["dlt_ready"], 3 * q_)
                wait(pool, S["bc_ready"], q_)
                wait(pool, S["dxT_ready"], q_)
                pool.tensor_tensor(xcT[:, :, 0:n], xb[:, :, 0:n], sg[:, :, 0:n], ALU.mult).then_inc(S["xc_ready"], 1)

            def inputs(q_, n):
                wait(pool, S["delta_ready"], q_ + 1)
                wait(pool, S["xc_ready"], q_ + 1)
                wait(pool, S["u_turned"], 2 * q_ - 1)
                pool.tensor_tensor(uT[:, :, 0:n], dltT[:, :, 0:n], xcT[:, :, 0:n], ALU.mult).then_inc(S["uT_ready"], 1)
                wait(pool, S["dx_turned"], 2 * q_ - 1)
                pool.tensor_tensor(dxT[:, :, 0:n], xcT[:, :, 0:n],
                                   dsk[:].rearrange("p (c o) -> p c o", o=1).to_broadcast([P, IC, n]),
                                   ALU.mult).then_inc(S["dxT_ready"], 1)

            def outputs(t, k):
                i = ACT_OUT.index(k)
                if i > 0:
                    pool.wait_ge(S["rows_read"], t * len(ACT_OUT) + i + 1)
                    wait(pool, S["prod_used"], t * (len(ACT_OUT) - 1) + i - 1)
                    pool.tensor_tensor(acc[:], acc[:], prod[i % 2], ALU.add).then_inc(S["prod_used"], 1)
                if k == ACT_OUT[-1]:
                    pool.wait_ge(S["prod_used"], (t + 1) * (len(ACT_OUT) - 1))
                    wait(pool, S["yz_ready"], t)
                    pool.tensor_tensor(ysum[:], acc[:, 0, :], acc[:, 1, :], ALU.add).then_inc(S["y_ready"], 1)

            def small_root(t):
                apart(pool, S["mvA_ready"], t + 1)
                own.then(pool.tensor_scalar(rsA[:, 0:1], mvA[:, 1:2], 1e-5, None, ALU.add))
                pool.tensor_tensor(rsA[:, 1:2], rsA[:, 0:1], mhalf[:], ALU.pow).then_inc(S["rsA_ready"], 1)

            def residual(t):
                pool.wait_ge(S["o1_ready"], t + 1)
                own.then(pool.tensor_tensor(o1, o1, gam[:], ALU.mult))
                r = res[:, bass.ds(t, 1), :]
                pool.tensor_tensor(r, r, o1.rearrange("p (o n) -> p o n", o=1), ALU.add).then_inc(S["h1_ready"], 1)

            def first_scales(t, par):
                apart(pool, S["w_ready"], t + 1)
                own.then(pool.tensor_scalar(s1[:, 0:1], mvF[:, 1:2], 1.0 + 1e-6, 1e-11, ALU.mult, ALU.add))
                own.then(pool.tensor_tensor(s1[:, 1:2], s1[:, 0:1], mhalf[:], ALU.pow))
                own.then(pool.tensor_scalar(s1[:, 2:3], amF[:], s1[:, 1:2], 1e-5, ALU.mult, ALU.max))
                own.then(pool.tensor_tensor(s1[:, 3:4], s1[:, 2:3], mone[:], ALU.pow))
                apart(pool, S["t1_ready"], t)
                pool.tensor_scalar(s1[:, 4:5], s1[:, 3:4], s1[:, 1:2], 127.0, ALU.mult, ALU.mult)
                apart(pool, S["fsig_ready"], t - 1)
                pool.tensor_scalar(c1[:, par, 1:2], s1[:, 2:3], ws[:, 0:1], -1.0 / 127.0, ALU.mult, ALU.mult)
                pool.tensor_scalar(c1[:, par, 0:1], s1[:, 2:3], ws[:, 0:1], 1.0 / 127.0, ALU.mult,
                                   ALU.mult).then_inc(S["s1_ready"], 1)

            def weigh(t):
                pool.wait_ge(S["f1_used"], t + 1)
                wait(pool, S["t2_ready"], t)
                wait(pool, S["am2_ready"], t)
                pool.tensor_tensor(v2[:], y2[:], go[:], ALU.mult).then_inc(S["v2_ready"], 1)

            def second_scales(t, par):
                apart(pool, S["sumsq_ready"], t + 1)
                pool.wait_ge(S["am2_ready"], t + 1)
                c = c1[:, par, 0:1]
                apart(pool, S["s1_ready"], t + 1)
                own.then(pool.tensor_scalar(s2[:, 0:1], c, c, 1.0, ALU.mult, ALU.mult))
                own.then(pool.tensor_scalar(s2[:, 1:2], ss[:], s2[:, 0:1], s2[:, 0:1], ALU.mult, ALU.mult))
                own.then(pool.tensor_scalar(s2[:, 2:3], s2[:, 1:2], 1.0 / FFN, 1e-6, ALU.mult, ALU.add))
                own.then(pool.tensor_tensor(s2[:, 3:4], s2[:, 2:3], mhalf[:], ALU.pow))
                own.then(pool.tensor_tensor(s2[:, 4:5], s2[:, 3:4], s2[:, 0:1], ALU.mult))
                own.then(pool.tensor_scalar(s2[:, 5:6], am2[:], s2[:, 4:5], 1e-5, ALU.mult, ALU.max))
                own.then(pool.tensor_tensor(s2[:, 6:7], s2[:, 5:6], mone[:], ALU.pow))
                apart(pool, S["t2_ready"], t)
                pool.tensor_scalar(s2[:, 7:8], s2[:, 6:7], s2[:, 4:5], 127.0, ALU.mult, ALU.mult)
                apart(pool, S["final_ready"], t - 1)
                pool.tensor_scalar(c2[:, par:par + 1], s2[:, 5:6], ws[:, 1:2], 1.0 / 127.0, ALU.mult,
                                   ALU.mult).then_inc(S["s2_ready"], 1)

            def step(t, j, pair):
                par = (1 + j) % 2
                scan = exists(t)
                for k in range(CH):
                    if k == 3 and exists(t - 4):
                        second_scales(t - 4, par)
                    if k == 4 and exists(t - 2):
                        first_scales(t - 2, par)
                    if k == 7 and exists(t - 1):
                        small_root(t - 1)
                    if k == 1 and exists(t - 2):
                        residual(t - 2)
                    if k == 0 and exists(t - 4):
                        weigh(t - 4)
                    if scan and k - 1 in ACT_OUT:
                        outputs(t, k - 1)
                    if j == 1 and k == 2 and (pair is not None) and (not isinstance(pair, int) or pair < PAIRS - 1):
                        inputs(pair + 2, 2 * P)
                    if j == 0 and k == 1 and (pair is not None) and (not isinstance(pair, int) or pair < PAIRS - 1):
                        conv_gate(pair + 2, 2 * P)

            conv_gate(0, P)
            inputs(0, P)
            conv_gate(1, 2 * P)
            for k in ACT_OUT[:3]:
                outputs(0, k)
            inputs(1, 2 * P)
            for k in ACT_OUT[3:]:
                outputs(0, k)
            walk(pool, step, own, POOL_STEPS)

        @block.scalar
        def _(act):
            own = Steps(act, S["act_step"])
            act.preload_act_table_set("natural_log_exp_and_others")
            step_ = POS_TABLE_SIDE // GRID
            rows = pos_table.rearrange("(h a w b) n -> a b h w n", h=GRID, a=step_, w=GRID)[0, 0]
            for h in range(GRID):
                act.dma_start(pos[:, 1 + GRID * h:1 + GRID * (h + 1), :],
                              rows[h:h + 1].to_broadcast([P, GRID, HID])).then_inc(S["consts_loaded"], 16)
            act.dma_start(tb, tok_b.rearrange("(o n) -> o n", o=1).to_broadcast([P, HID])).then_inc(S["consts_loaded"], 16)
            act.dma_start(res[:, 0, :], cls_tok.rearrange("a b n -> (a b) n").to_broadcast([P, HID])).then_inc(S["consts_loaded"], 16)
            act.dma_start(wi, w_in.rearrange("(c p) n -> p c n", c=2)).then_inc(S["consts_loaded"], 16)
            act.dma_start(bet, beta.rearrange("(o n) -> o n", o=1).to_broadcast([P, HID])).then_inc(S["consts_loaded"], 16)
            act.dma_start(gam[:], gamma.rearrange("(o n) -> o n", o=1).to_broadcast([P, HID])).then_inc(S["consts_loaded"], 16)
            act.dma_start(gi[:], g_in.rearrange("(o n) -> o n", o=1).to_broadcast([P, HID])).then_inc(S["consts_loaded"], 16)
            act.dma_start(go[:], g_out.rearrange("(o n) -> o n", o=1).to_broadcast([P, FFN])).then_inc(S["consts_loaded"], 16)
            with nc.allow_non_contiguous_dma(reason="a few hundred numbers"):
                act.dma_start(cb[:], chunks(conv_b, IC)).then_inc(S["consts_loaded"], 16)
                act.dma_start(bdt[:], chunks(b_dt, IC)).then_inc(S["consts_loaded"], 16)
                act.dma_start(dsk[:], chunks(d_skip, IC)).then_inc(S["consts_loaded"], 16)
            act.dma_start(A[:], a_log.rearrange("(c p) s -> p c s", c=IC)).then_inc(S["consts_loaded"], 16)
            act.dma_start(wx[:], w_x.rearrange("(c p) n -> p c n", c=IC)).then_inc(S["conv_loaded"], 16)
            act.wait_ge(S["consts_loaded"], 16 * n_const)
            own.then(act.activation(A[:], A[:], ACT.Exp))
            act.activation(A[:], A[:], ACT.Copy, scale=-1.0).then_inc(S["a_ready"], 1)

            def normal_T(t, j, par):
                wait(act, S["xn_turned"], t + 1)
                if j == 0:
                    wait(act, S["z_ready"], t)
                act.activation(xnT[:, :, j * P:(j + 1) * P],
                               bank(6 + par, 2 * P, HC).rearrange("p (c n) -> p c n", c=2),
                               ACT.Copy).then_inc(S["xnT_ready"], 1)

            def z_sigmoid(t, j, par):
                z = bank(Z_BANKS[j], INNER)
                wait(act, S["z_ready"], t + 1)
                wait(act, S["z_used"], t - 1 if j else t)
                own.then(act.activation(zs[par], z, ACT.Exp, scale=-1.0))
                own.then(act.activation(zs[par], zs[par], ACT.Ln, bias=1.0))
                act.activation(zs[par], zs[par], ACT.Exp, scale=-1.0).then_inc(S["zsig_ready"], 1)

            def patch_part(g, j):
                wait(act, S["patch_turned"], g * GRID + 1 + j)
                act.wait_ge(*product_read(g, j))
                act.activation(patch[j % 2][:, 0:4, :], bank(2 * (j % 2)).rearrange("p (c n) -> p c n", c=4),
                               ACT.Copy).then_inc(S["patch_act"], 1)

            normal_T(0, 0, 0)
            patch_part(0, 0)
            wait(act, S["xin_ready"], 3)
            act.activation(xinT[:, 0:2, P:2 * P], ps[:, 2 * BANK:4 * BANK].rearrange("p (c n) -> p c n", c=2)[:, :, 0:P],
                           ACT.Copy).then_inc(S["xin_act"], 1)
            z_sigmoid(0, 0, 0)

            def row(g, last_row):
                for j in range(1, GRID + (not last_row)):
                    patch_part(g, j)
                for j in range(GRID - 1):
                    normal_T(g * GRID + 1 + j, j, (1 + j) % 2)
                normal_T(g * GRID + GRID, GRID - 1, GRID % 2)
                for j in range(2):
                    z_sigmoid(g * GRID + 1 + j, j, (1 + j) % 2)
                act.wait_ge(S["xin_ready"], 2 * IC * g + 3 * IC)
                for c in range(2):
                    last = act.activation(xinT[:, c, bass.ds((g * GRID + 2) * P, GRID * P)], bank(XIN_BANKS[c]),
                                          ACT.Copy)
                last.then_inc(S["xin_act"], 1)
                for j in range(2, GRID):
                    z_sigmoid(g * GRID + 1 + j, j, (1 + j) % 2)

            with act.Fori(0, GRID - 1) as g:
                own.enter(g, 2 * GRID)
                row(g, False)
                own.leave(GRID - 1)
            row(GRID - 1, True)

            def conv_chunk(q_, m, n):
                wait(act, S["delta_ready"], q_)
                wait(act, S["conv_ready"], 3 * q_ + m + 1)
                act.activation(xb[:, m, 0:n], bank(conv_bank(q_, m), n), ACT.Identity,
                               bias=cb[:, m:m + 1]).then_inc(S["conv_used"], 1)

            def conv_sigmoid(q_, n):
                act.wait_ge(S["conv_used"], 3 * q_ + 3)
                own.then(act.activation(sg[:, :, 0:n], xb[:, :, 0:n], ACT.Exp, scale=-1.0))
                own.then(act.activation(sg[:, :, 0:n], sg[:, :, 0:n], ACT.Ln, bias=1.0))
                act.activation(sg[:, :, 0:n], sg[:, :, 0:n], ACT.Exp, scale=-1.0).then_inc(S["sig_ready"], 1)

            def delta_chunk(q_, m, n):
                wait(act, S["xc_ready"], q_ + 1)
                wait(act, S["dlt_ready"], 3 * q_ + m + 1)
                act.activation(db[:, m, 0:n], bank(delta_bank(m), n), ACT.Identity,
                               bias=bdt[:, m:m + 1]).then_inc(S["dlt_used"], 1)

            def softplus(q_, n):
                act.wait_ge(S["dlt_used"], 3 * q_ + 3)
                own.then(act.activation(sp[:, :, 0:n], db[:, :, 0:n], ACT.Exp))
                act.activation(sp[:, :, 0:n], sp[:, :, 0:n], ACT.Ln, bias=1.0).then_inc(S["sp_ready"], 1)

            def decays(pair, s_):
                if s_ in (0, DECAYS_LATE[0][0]):
                    act.wait_ge(S["delta_ready"], pair + 2)
                wait(act, S["decay_turned"], (2 * pair - 1) * DC + (IC * s_ + IC - 1) * P // BANK + 1)
                for c in range(IC):
                    last = act.activation(decay[:, s_, c, :], dltT[:, c, :], ACT.Exp, scale=A[:, c, s_:s_ + 1])
                last.then_inc(S["decay_made"], 1)

            def bc_copy(q_, tiles=2):
                wait(act, S["bc_ready"], q_ + 1)
                wait(act, S["bc_copied"], 2 * q_ - 1)
                act.activation(bcn[:].rearrange("p t n -> p (t n)")[:, 0:tiles * 2 * STATE],
                               bank(3, tiles * 2 * STATE), ACT.Copy).then_inc(
                    S["bcn_ready"], 1)

            def d_term(t):
                act.wait_ge(S["dx_turned"], t + 1)
                wait(act, S["y_dve"], (t - 1) * 2 * len(DVE_OUT) + 1)
                act.activation(dx[:], bank(3, INNER), ACT.Copy).then_inc(S["dx_ready"], 1)

            def products(t, par, k):
                i = ACT_OUT.index(k)
                if i == 0:
                    wait(act, S["y_ready"], t)
                if i > 2:
                    act.wait_ge(S["prod_used"], t * (len(ACT_OUT) - 1) + i - 2)
                act.wait_ge(S["state_ready"], t * CH + k + 1)
                to = acc[:] if i == 0 else prod[i % 2]
                for r in range(2):
                    s_ = 2 * k + r
                    last = act.activation(to[:, r, :], state[:, s_, :], ACT.Copy,
                                          scale=bc[:, par, STATE + s_:STATE + s_ + 1])
                last.then_inc(S["rows_read"], 1)

            def step(t, j, pair):
                par = (1 + j) % 2
                has = lambda d: pair is not None and (not isinstance(pair, int) or pair < PAIRS - d)
                for k in range(CH):
                    if k == D_SLOT and exists(t):
                        d_term(t)
                    if k == 1 and exists(t - 3):
                        act.wait_ge(S["q1_turned"], t - 2)
                        wait(act, S["f1_ready"], t - 3)
                        act.activation(q1[:], bank(6, 2 * P, HC).rearrange("p (c n) -> p c n", c=2), ACT.Copy,
                                       bias=-ROUND).then_inc(S["q1_ready"], 1)
                    if k == 1 and exists(t - 5):
                        act.wait_ge(S["q2_turned"], t - 4)
                        wait(act, S["f2_ready"], t - 5)
                        act.activation(q2[:].rearrange("p c n -> p (c n)"), bank(7), ACT.Copy,
                                       bias=-ROUND).then_inc(S["q2_ready"], 1)
                    if has(1) and j == 0:
                        if k == 0 and not (isinstance(pair, int) and pair == 0):
                            conv_chunk(pair + 2, 2, 2 * P)
                            conv_sigmoid(pair + 2, 2 * P)
                        if k in (3, 4, 5):
                            delta_chunk(pair + 2, k - 3, 2 * P)
                        if k == 6:
                            softplus(pair + 2, 2 * P)
                    if has(2) and j == 1 and k in (0, 4):
                        conv_chunk(pair + 3, k // 4, 2 * P)
                    if has(1) and j == 1 and k == 6:
                        bc_copy(pair + 2)
                    if has(0) and j == 0:
                        for s_ in DECAYS_LATE[k]:
                            decays(pair, s_)
                    if has(1) and j == 1:
                        for s_ in DECAYS_EARLY[k]:
                            decays(pair + 1, s_)
                    if exists(t) and k - 1 in ACT_OUT:
                        products(t, par, k - 1)
                    if k == 3 and exists(t - 1):
                        act.wait_ge(S["yz_turned"], t)
                        wait(act, S["o_ready"], t - 1)
                        act.activation(yzT[:].rearrange("p c n -> p (c n)"), bank(3, INNER),
                                       ACT.Copy).then_inc(S["yzT_ready"], 1)
                    if k == 5 and exists(t - 1):
                        act.wait_ge(S["o_ready"], t)
                        wait(act, S["o1_ready"], t - 1)
                        act.activation(ow[:], bank(3, HID), ACT.Copy).then_inc(S["ow_ready"], 1)
                    if k == 6 and exists(t - 2):
                        act.wait_ge(S["s1_ready"], t - 1)
                        wait(act, S["q1_turned"], t - 2)
                        act.activation(t1, wq, ACT.Copy, bias=ROUND, scale=s1[:, 4:5]).then_inc(S["t1_ready"], 1)
                    if k == 5 and exists(t - 3):
                        act.wait_ge(S["f1_ready"], t - 2)
                        own.then(act.activation(sig, bank(6), ACT.Exp, scale=c1[:, 1 - par, 1:2]))
                        own.then(act.activation(sig, sig, ACT.Ln, bias=1.0))
                        act.activation(sig, sig, ACT.Exp, scale=-1.0).then_inc(S["fsig_ready"], 1)
                    if k == 0 and exists(t - 4):
                        act.wait_ge(S["f1_used"], t - 3)
                        wait(act, S["s2_ready"], t - 4)
                        act.activation(sq[:], y2[:], ACT.Square, accum_out=ss[:]).then_inc(S["sumsq_ready"], 1)
                    if k == 5 and exists(t - 4):
                        act.wait_ge(S["s2_ready"], t - 3)
                        wait(act, S["q2_turned"], t - 4)
                        act.activation(t2[:], v2[:], ACT.Copy, bias=ROUND, scale=s2[:, 7:8]).then_inc(S["t2_ready"], 1)

            for q_, n in ((0, P), (1, 2 * P)):
                for m in range(IC):
                    conv_chunk(q_, m, n)
                if q_ == 1:
                    d_term(0)
                conv_sigmoid(q_, n)
                if q_ == 1:
                    for k in ACT_OUT[:3]:
                        products(0, 0, k)
                for m in range(IC):
                    delta_chunk(q_, m, n)
                softplus(q_, n)
                bc_copy(q_, n // P)
            for m in range(2):
                conv_chunk(2, m, 2 * P)
            for s_ in range(2):
                decays(0, s_)
            for k in ACT_OUT[3:]:
                products(0, 0, k)
            conv_chunk(2, 2, 2 * P)
            conv_sigmoid(2, 2 * P)
            for s_ in range(2, DECAYS_LATE[0][0]):
                decays(0, s_)
            walk(act, step, own, ACT_STEPS)

        @block.vector
        def _(dve):
            own = Steps(dve, S["dve_step"], apart)
            dve.wait_ge(S["raws_loaded"], 48)
            own.then(dve.memset(wsum[:], 0.0))
            dve.tensor_reduce(wsum[:, 0:1], raw1, AX.XY, ALU.add, apply_absolute_value=True)
            dve.tensor_reduce(wsum[0:HC, 1:2], raw2, AX.XY, ALU.add,
                              apply_absolute_value=True).then_inc(S["wsum_ready"], 1)
            dve.wait_ge(S["wsum_ready"], 2)
            for i, n in enumerate((2 * FFN * HID, FFN * HID)):
                last = dve.tensor_scalar(ws[:, i:i + 1], bank(7, 2)[:, i:i + 1], 1.0 / n, 1e-5, ALU.mult, ALU.max)
            last.then_inc(S["ws_ready"], 1)
            dve.wait_ge(S["ws_inverse"], 1)
            for i, w in ((0, raw1), (1, raw2)):
                rows_ = w.shape[0]
                own.then(dve.tensor_scalar(w, w, wsc[0:rows_, i:i + 1], 1.0, ALU.mult, ALU.min))
                dve.tensor_scalar(w, w, -1.0, ROUND, ALU.max, ALU.add).then_inc(S["raw_scaled"], 1)
            for k in range(KP):
                dve.wait_ge(S["tok_turned"], k + 1)
                dve.tensor_copy(twT[:, k, :], bank(k % TURN_BANKS, HID)).then_inc(S["raw_turned"], 1)
            for c in range(8):
                dve.wait_ge(S["tok_turned"], KP + c + 1)
                dve.tensor_scalar(f1[:, :, c * P:(c + 1) * P],
                                  bank((KP + c) % TURN_BANKS, 2 * P, HC).rearrange("p (c n) -> p c n", c=2), ROUND, None,
                                  ALU.subtract).then_inc(S["raw_turned"], 1)
            for c in range(FC):
                dve.wait_ge(S["tok_turned"], KP + 8 + c + 1)
                dve.tensor_scalar(f2[:, c, :], bank((KP + 8 + c) % TURN_BANKS, HID), ROUND, None,
                                  ALU.subtract).then_inc(S["raw_turned"], 1)

            def stats(par, src):
                own.then(dve.bn_stats(st[:], src))
                dve.bn_aggr(mv[par][:], st[:]).then_inc(S["mv_ready"], 1)

            def normalise(t, j, par, src):
                wait(dve, S["rs_ready"], t + 1)
                wait(dve, S["xn_turned"], t - j)
                dve.tensor_scalar(xn[j], src, mv[par][:, 0:1], rs[par][:, 1:2], ALU.subtract,
                                  ALU.mult).then_inc(S["xn_ready"], 1)

            def z_gate(t, j, par, kept):
                wait(dve, S["zsig_ready"], t + 1)
                dve.tensor_tensor(kept, bank(Z_BANKS[j], INNER), zs[par], ALU.mult).then_inc(S["z_used"], 1)

            dve.wait_ge(S["consts_loaded"], 16 * n_const)
            stats(0, res[:, 0, :])

            def patch_part(g, j):
                wait(dve, S["patch_turned"], g * GRID + 1 + j)
                dve.wait_ge(*product_read(g, j))
                dve.tensor_copy(patch[j % 2][:, 4:6, :],
                                bank(2 * (j % 2) + 1, 2 * P).rearrange("p (c n) -> p c n", c=2)
                                ).then_inc(S["patch_dve"], 1)

            normalise(0, 0, 0, res[:, 0, :])
            patch_part(0, 0)
            dve.wait_ge(S["xin_ready"], 3)
            dve.tensor_copy(xinT[:, 2, P:2 * P], bank(XIN_BANKS[2], P)).then_inc(S["xin_dve"], 1)
            z_gate(0, 0, 0, gate[0][:])
            own.then(dve.tensor_tensor(pos[:, 1:T, :], pos[:, 1:T, :],
                                       tb.rearrange("p (o n) -> p o n", o=1).to_broadcast([P, T - 1, HID]), ALU.add))

            def row(g, last_row):
                for j in range(GRID):
                    t = g * GRID + 1 + j
                    dve.wait_ge(S["emb_ready"], t)
                    e = res[:, bass.ds(t, 1), :].rearrange("p o n -> p (o n)")
                    own.then(dve.tensor_tensor(e, bank(4 + j % 2, HID),
                                               pos[:, bass.ds(t, 1), :].rearrange("p o n -> p (o n)"), ALU.add))
                    stats((1 + j) % 2, e)
                    if j == 0:
                        patch_part(g, 1)
                    if j + 2 < GRID + (not last_row):
                        patch_part(g, j + 2)
                    normalise(t, j, (1 + j) % 2, e)

                def row_gate(j):
                    z_gate(g * GRID + 1 + j, j, (1 + j) % 2,
                           state[:, bass.ds(g * GRID + j, 1), :].rearrange("p o n -> p (o n)"))

                row_gate(0)
                row_gate(1)
                dve.wait_ge(S["xin_ready"], 2 * IC * g + 3 * IC)
                dve.tensor_copy(xinT[:, 2, bass.ds((g * GRID + 2) * P, GRID * P)],
                                bank(XIN_BANKS[2])).then_inc(S["xin_dve"], 1)
                row_gate(2)
                row_gate(3)

            with dve.Fori(0, GRID - 1) as g:
                own.enter(g, 2 * GRID)
                row(g, False)
                own.leave(GRID - 1)
            row(GRID - 1, True)

            def make_delta(q_, n):
                dve.wait_ge(S["sp_ready"], q_ + 1)
                wait(dve, S["decay_made"], 16 * (q_ - 1))
                wait(dve, S["uT_ready"], q_)
                dve.scalar_tensor_tensor(dltT[:, :, 0:n], sp[:, :, 0:n], 80.0, db[:, :, 0:n], ALU.min,
                                         ALU.max).then_inc(S["delta_ready"], 1)

            u = bank(4, INNER)

            def copy_bc(t, j, par, place):
                wait(dve, S["bcn_ready"], place)
                wait(dve, S["rows_read"], (t - 1) * len(ACT_OUT))
                dve.tensor_copy(bc[:, par, :], bcn[:, j, :]).then_inc(S["bc_copied"], 1)
                wait(dve, S["bc_copied"], t + 1)

            def decay_state(t, i):
                dve.wait_ge(S["decay_turned"], (t - 1) * DC + i + 1)
                dve.wait_ge(S["rows_read"], (t - 1) * len(ACT_OUT) + sum(k <= last_slot(i) for k in ACT_OUT))
                h = state[:].rearrange("p s n -> p (s n)")[:, i * BANK:(i + 1) * BANK]
                dve.tensor_tensor(h, bank(i % DB), h, ALU.mult).then_inc(S["decay_used"], 1)

            def add_input(t, par, k):
                dve.wait_ge(S["decay_used"], (t - 1) * DC + chunks_of(k)[-1] + 1)
                for r in range(2):
                    s_ = 2 * k + r
                    last = dve.scalar_tensor_tensor(state[:, s_, :], u, bc[:, par, s_:s_ + 1], state[:, s_, :],
                                                    ALU.mult, ALU.add)
                last.then_inc(S["state_ready"], 1)

            def output(t, par, k, r):
                s_, n = 2 * k + r, 2 * DVE_OUT.index(k) + r
                if n == 0:
                    dve.wait_ge(S["dx_ready"], t + 1)
                    wait(dve, S["yz_ready"], t)
                    before = dx
                else:
                    wait(dve, S["y_dve"], t * 2 * len(DVE_OUT) + n)
                    before = ydve
                dve.wait_ge(S["state_ready"], t * CH + k + 1)
                dve.scalar_tensor_tensor(ydve[:], state[:, s_, :], bc[:, par, STATE + s_:STATE + s_ + 1], before[:],
                                         ALU.mult, ALU.add).then_inc(S["y_dve"], 1)

            def step(t, j, pair):
                par = (1 + j) % 2
                has = lambda d: pair is not None and (not isinstance(pair, int) or pair < PAIRS - d)
                flat = lambda a: a.rearrange("p o n -> p (o n)")
                scan = exists(t)
                if scan and pair is not None:
                    copy_bc(t, j, par, pair + 2)
                for k in range(CH):
                    if k == 0 and exists(t - 1):
                        output(t - 1, 1 - par, CH - 1, 0)
                    if scan:
                        for i in chunks_of(k):
                            decay_state(t, i)
                    if k == 1 and exists(t - 1):
                        wait(dve, S["y_dve"], t * 2 * len(DVE_OUT))
                        wait(dve, S["y_ready"], t)
                        dve.tensor_tensor(ydve[:], ysum[:], ydve[:], ALU.add).then_inc(S["y_joined"], 1)
                    if k == 2 and exists(t - 1):
                        dve.wait_ge(S["y_joined"], t)
                        wait(dve, S["yz_turned"], t - 1)
                        loads = (t - 1) // 2 if isinstance(t, int) else pair
                        if 1 - par:
                            dve.wait_ge(S["gate_odd_in"], 16 * loads + 16)
                        else:
                            wait(dve, S["gate_even_in"], 16 * loads)
                        dve.tensor_tensor(yz, ydve[:], gate[1 - par][:],
                                          ALU.mult).then_inc(S["yz_ready"], 1)
                    if k == 6 and exists(t - 1):
                        apart(dve, S["ow_ready"], t)
                        own.then(dve.bn_stats(stA[:], ow[:]))
                        dve.bn_aggr(mvA[:], stA[:]).then_inc(S["mvA_ready"], 1)
                    if k == 0 and exists(t - 2):
                        dve.wait_ge(S["rsA_ready"], t - 1)
                        wait(dve, S["h1_ready"], t - 2)
                        dve.tensor_scalar(o1, ow[:], mvA[:, 0:1], rsA[:, 1:2], ALU.subtract,
                                          ALU.mult).then_inc(S["o1_ready"], 1)
                    if k == 3 and exists(t - 2):
                        apart(dve, S["h1_ready"], t - 1)
                        h1 = flat(res[:, bass.ds(t - 2, 1), :])
                        own.then(dve.bn_stats(stF[:], h1))
                        apart(dve, S["s1_ready"], t - 2)
                        own.then(dve.bn_aggr(mvF[:], stF[:]))
                        wait(dve, S["t1_ready"], t - 2)
                        own.then(dve.scalar_tensor_tensor(wq, h1, mvF[:, 0:1], gi[:], ALU.subtract, ALU.mult))
                        dve.tensor_reduce(amF[:], wq, AX.X, ALU.max, apply_absolute_value=True).then_inc(
                            S["w_ready"], 1)
                    if k == 7 and exists(t - 3):
                        dve.wait_ge(S["fsig_ready"], t - 2)
                        own.then(dve.tensor_tensor(aa, bank(7), sig, ALU.mult))
                        wait(dve, S["v2_ready"], t - 3)
                        wait(dve, S["sumsq_ready"], t - 3)
                        dve.tensor_tensor(y2[:], bank(6), aa, ALU.mult).then_inc(S["f1_used"], 1)
                    if k == 2 and exists(t - 4):
                        dve.wait_ge(S["v2_ready"], t - 3)
                        wait(dve, S["s2_ready"], t - 4)
                        dve.tensor_reduce(am2[:], v2[:], AX.X, ALU.max, apply_absolute_value=True).then_inc(
                            S["am2_ready"], 1)
                    if k == 3 and exists(t - 5):
                        dve.wait_ge(S["f2_ready"], t - 4)
                        r = flat(res[:, bass.ds(t - 5, 1), :])
                        dve.wait_ge(S["s2_ready"], t - 4)
                        dve.scalar_tensor_tensor(r, bank(7, HID), c2[:, 1 - par:2 - par], r, ALU.mult,
                                                 ALU.add).then_inc(S["final_ready"], 1)
                    if k == 7 and j == 0 and has(1):
                        make_delta(pair + 2, 2 * P)
                    if scan and k - 1 in DVE_OUT:
                        output(t, par, k - 1, 0)
                    if scan:
                        if k == 0:
                            dve.wait_ge(S["u_turned"], t + 1)
                        add_input(t, par, k)
                    if k == 0 and exists(t - 1):
                        output(t - 1, 1 - par, CH - 1, 1)
                    if scan and k - 1 in DVE_OUT:
                        output(t, par, k - 1, 1)

            make_delta(0, P)
            copy_bc(0, 0, 0, 1)
            dve.wait_ge(S["gate_kept"], 16 * GRID)
            dve.wait_ge(S["u_turned"], 1)
            for k in range(CH):
                for r in range(2):
                    s_ = 2 * k + r
                    last = dve.tensor_scalar(state[:, s_, :], u, bc[:, 0, s_:s_ + 1], None, ALU.mult)
                last.then_inc(S["state_ready"], 1)
            make_delta(1, 2 * P)
            for k in DVE_OUT[:-1]:
                for r in range(2):
                    output(0, 0, k, r)
            walk(dve, step, own, DVE_STEPS)

        @block.tensor
        def _(pe):
            pe.wait_ge(S["ones_set"], 1)
            pe.wait_ge(S["wsum_ready"], 1)
            pe.matmul(bank(7, 2), ones[:], wsum[:], start=True, stop=True).then_inc(S["wsum_ready"], 1)
            pe.wait_ge(S["ident_built"], 1)
            pe.wait_ge(S["raws_loaded"], 48)
            n = 0
            for k in range(KP):
                wait(pe, S["raw_turned"], n + 1 - TURN_BANKS)
                for c in range(2):
                    last = pe.transpose(bank(n % TURN_BANKS, HC, off=c * HC), rawT[:, c, k * P:(k + 1) * P], ident[0:HC, 0:HC])
                last.then_inc(S["tok_turned"], 1)
                n += 1
            pe.wait_ge(S["raw_scaled"], 2)
            for c in range(8):
                wait(pe, S["raw_turned"], n + 1 - TURN_BANKS)
                for h in range(2):
                    last = pe.transpose(bank(n % TURN_BANKS, P, HC, h * P), raw1[:, c, h * HC:(h + 1) * HC], ident[:])
                last.then_inc(S["tok_turned"], 1)
                n += 1
            for c in range(FC):
                wait(pe, S["raw_turned"], n + 1 - TURN_BANKS)
                for h in range(2):
                    last = pe.transpose(bank(n % TURN_BANKS, HC, off=h * HC), raw2[:, h, c * P:(c + 1) * P], ident[0:HC, 0:HC])
                last.then_inc(S["tok_turned"], 1)
                n += 1

            def turn_normal(t, j, par):
                wait(pe, S["xn_ready"], t + 1)
                wait(pe, S["xnT_ready"], t - 1 if j else t)
                for c in range(2):
                    last = pe.transpose(bank(6 + par, P, HC, c * P), xn[j][:, c * HC:(c + 1) * HC], ident[:])
                last.then_inc(S["xn_turned"], 1)

            def x_inner(t0, first, tiles):
                wait(pe, S["xnT_ready"], t0 + first + tiles)
                cols = slice(first * P, (first + tiles) * P)
                for m in range(IC):
                    for c in range(2):
                        last = pe.matmul(bank(XIN_BANKS[m], tiles * P, off=first * P), wi[:, c, m * P:(m + 1) * P],
                                         xnT[:, c, cols], start=(c == 0), stop=(c == 1))
                    last.then_inc(S["xin_ready"], 1)

            def z_product(j):
                for c in range(2):
                    last = pe.matmul(bank(Z_BANKS[j], INNER), xnT[:, c, j * P:(j + 1) * P],
                                     wi[:, c, INNER:2 * INNER], start=(c == 0), stop=(c == 1))
                last.then_inc(S["z_ready"], 1)

            pe.wait_ge(S["raw_turned"], n)
            pe.wait_ge(S["consts_loaded"], 16 * n_const)
            turn_normal(0, 0, 0)

            def turn_patch(g, j):
                t = g * GRID + 1 + j
                if j == 1:
                    pe.wait_ge(S["xin_act"], g + 1)
                    pe.wait_ge(S["z_used"], t - 1)
                if j >= 2:
                    pe.wait_ge(S["patch_act"], t - 2)
                    pe.wait_ge(S["patch_dve"], t - 2)
                pe.wait_ge(S["patch_packed"], t)
                for k in range(KP):
                    last = pe.transpose(bank(2 * (j % 2) + k // 4, P, off=(k % 4) * P),
                                        px[j % GRID][:, k * P:(k + 1) * P], ident[:])
                last.then_inc(S["patch_turned"], 1)

            def embed(g, j):
                t = g * GRID + 1 + j
                pe.wait_ge(S["patch_act"], t)
                pe.wait_ge(S["patch_dve"], t)
                if j == 0:
                    pe.wait_ge(S["xin_dve"], g + 1)
                if j >= 2:
                    pe.wait_ge(S["mv_ready"], t - 1)
                for k in range(KP):
                    last = pe.matmul(bank(4 + j % 2, HID), patch[j % 2][:, k, :], twT[:, k, :],
                                     start=(k == 0), stop=(k == KP - 1))
                last.then_inc(S["emb_ready"], 1)

            def row(g, last_row):
                embed(g, 0)
                turn_patch(g, 1)
                for j in range(1, GRID):
                    if j + 1 < GRID + (not last_row):
                        turn_patch(g, j + 1)
                    if j == GRID - 1:
                        turn_normal(g * GRID + 1, 0, 1)
                    embed(g, j)
                t0 = g * GRID + 1
                turn_normal(t0 + 1, 1, 0)
                turn_normal(t0 + 2, 2, 1)
                x_inner(t0, 0, 2)
                pe.wait_ge(S["mv_ready"], t0 + GRID)
                z_product(0)
                turn_normal(t0 + 3, 3, 0)
                pe.wait_ge(S["xnT_ready"], t0 + 3)
                z_product(1)
                x_inner(t0, 2, 2)
                z_product(2)
                pe.wait_ge(S["xin_act"], g + 2)
                z_product(3)

            turn_patch(0, 0)
            x_inner(0, 0, 1)
            z_product(0)
            with pe.Fori(0, GRID - 1) as g:
                row(g, False)
            row(GRID - 1, True)

            def bank_free(q_, m):
                if isinstance(q_, int) and q_ in (1, 2) and (q_, m) != (2, 2):
                    return S["conv_used"], 6 if (q_, m) == (2, 1) else 0
                if isinstance(q_, int) and q_ == 2:
                    return S["dlt_used"], 5
                return (S["dlt_used"], 3 * q_ - 1 + m) if m < 2 else (S["conv_used"], 3 * q_ + 1)

            def conv_taps(q_, m, n, taps, first_tile):
                if 0 in taps:
                    wait(pe, *bank_free(q_, m))
                for tap in taps:
                    for c in range(IC):
                        last = pe.matmul(bank(conv_bank(q_, m), n), cw[:, tap, c, m * P:(m + 1) * P],
                                         xinT[:, c, bass.ds((first_tile + tap) * P, n)],
                                         start=(tap == 0 and c == 0), stop=(tap == TAPS - 1 and c == IC - 1))
                if TAPS - 1 in taps:
                    last.then_inc(S["conv_ready"], 1)

            def delta_product(q_, m, n):
                wait(pe, S["xc_ready"], q_ + 1)
                wait(pe, *((S["conv_used"], 3 * q_ + 2 + m) if m < 2 else (S["dlt_used"], 3 * q_ + 1)))
                for c in range(IC):
                    last = pe.matmul(bank(delta_bank(m), n), wdt[:, c, m * P:(m + 1) * P], xcT[:, c, 0:n],
                                     start=(c == 0), stop=(c == IC - 1))
                last.then_inc(S["dlt_ready"], 1)

            def bc_product(q_, tiles, o_copied):
                wait(pe, S["xc_ready"], q_ + 1)
                wait(pe, S["ow_ready"], o_copied)
                for j in range(tiles):
                    for c in range(IC):
                        last = pe.matmul(bank(3, 2 * STATE, off=2 * STATE * j),
                                         xcT[:, c, j * P:(j + 1) * P], wx[:, c, :],
                                         start=(c == 0), stop=(c == IC - 1))
                last.then_inc(S["bc_ready"], 1)

            def turn_inputs(t, j, q_):
                wait(pe, S["uT_ready"], q_ + 1)
                wait(pe, S["state_ready"], t * CH)
                for c in range(IC):
                    last = pe.transpose(bank(4, P, off=c * P), uT[:, c, j * P:(j + 1) * P], ident[:])
                last.then_inc(S["u_turned"], 1)
                wait(pe, S["dxT_ready"], q_ + 1)
                wait(pe, S["bcn_ready"], q_ + 1)
                wait(pe, S["ow_ready"], t - 1)
                for c in range(IC):
                    last = pe.transpose(bank(3, P, off=c * P), dxT[:, c, j * P:(j + 1) * P], ident[:])
                last.then_inc(S["dx_turned"], 1)

            def turn_decays(t, j, pair, i):
                pe.wait_ge(S["decay_made"], 16 * pair + (4 * i + 3) // IC + 1)
                wait(pe, S["decay_used"], (t - 1) * DC + i + 1 - DB)
                for b in range(4 * i, 4 * i + 4):
                    last = pe.transpose(bank(i % DB, P, off=(b % 4) * P),
                                        decay[:, b // IC, b % IC, j * P:(j + 1) * P], ident[:])
                last.then_inc(S["decay_turned"], 1)

            def step(t, j, pair):
                par = (1 + j) % 2
                has = lambda d: pair is not None and (not isinstance(pair, int) or pair < PAIRS - d)
                for k in range(CH):
                    if exists(t):
                        for i in chunks_of(k):
                            turn_decays(t, j, pair, i)
                    if exists(t) and k == 0:
                        turn_inputs(t, j, pair + 1)
                    if k == 0 and exists(t - 3):
                        pe.wait_ge(S["t1_ready"], t - 2)
                        wait(pe, S["f1_used"], t - 3)
                        for c in range(2):
                            last = pe.transpose(bank(6, P, HC, c * P), t1[:, c * HC:(c + 1) * HC], ident[:])
                        last.then_inc(S["q1_turned"], 1)
                    if k == 0 and exists(t - 5):
                        pe.wait_ge(S["t2_ready"], t - 4)
                        wait(pe, S["f1_used"], min(t - 3, T) if isinstance(t, int) else t - 3)
                        wait(pe, S["final_ready"], t - 5)
                        for c in range(FC):
                            last = pe.transpose(bank(7, P, off=c * P), t2[:, c * P:(c + 1) * P], ident[:])
                        last.then_inc(S["q2_turned"], 1)
                    if k == 3 and exists(t - 1):
                        pe.wait_ge(S["yz_ready"], t)
                        pe.wait_ge(S["dx_ready"], min(t + 1, T) if isinstance(t, int) else t + 1)
                        for c in range(IC):
                            last = pe.transpose(bank(3, P, off=c * P), yz[:, c * P:(c + 1) * P], ident[:])
                        last.then_inc(S["yz_turned"], 1)
                    if k == 4 and exists(t - 1):
                        pe.wait_ge(S["yzT_ready"], t)
                        for c in range(IC):
                            last = pe.matmul(bank(3, HID), yzT[:, c, :], wo[:, c, :],
                                             start=(c == 0), stop=(c == IC - 1))
                        last.then_inc(S["o_ready"], 1)
                    if k == 4 and exists(t - 3):
                        pe.wait_ge(S["q1_ready"], t - 2)
                        wait(pe, S["final_ready"], t - 4)
                        for half in range(2):
                            for c in range(2):
                                last = pe.matmul(bank(6 + half), q1[:, c, :],
                                                 f1[:, c, (1 - half) * FFN:(2 - half) * FFN],
                                                 start=(c == 0), stop=(c == 1))
                        last.then_inc(S["f1_ready"], 1)
                    if k == 2 and exists(t - 5):
                        pe.wait_ge(S["q2_ready"], t - 4)
                        for c in range(FC):
                            last = pe.matmul(bank(7, HID), q2[:, c, :], f2[:, c, :],
                                             start=(c == 0), stop=(c == FC - 1))
                        last.then_inc(S["f2_ready"], 1)
                    if has(1):
                        if j == 0 and 2 <= k < 5:
                            delta_product(pair + 2, k - 2, 2 * P)
                        if j == 1 and k == 5:
                            bc_product(pair + 2, 2, t)
                    if has(2):
                        if j == 0 and k >= 5:
                            conv_taps(pair + 3, 0, 2 * P, ((0,), (1, 2), (3,))[k - 5], pair * 2 + 5)
                        if j == 1:
                            conv_taps(pair + 3, 1 + k // 4, 2 * P, (k % 4,), pair * 2 + 5)

            pe.wait_ge(S["conv_loaded"], 16 * (n_conv + 1))
            pe.wait_ge(S["pads_zeroed"], 1)
            pe.wait_ge(S["xin_act"], GRID + 1)
            pe.wait_ge(S["xin_dve"], GRID + 1)
            pe.wait_ge(S["z_used"], T)
            for m in range(IC):
                conv_taps(0, m, P, range(TAPS), 0)
            conv_taps(1, 0, 2 * P, range(TAPS), 1)
            for m in range(IC):
                delta_product(0, m, P)
            bc_product(0, 1, 0)
            for m in range(1, IC):
                conv_taps(1, m, 2 * P, range(TAPS), 1)
            turn_inputs(0, 0, 0)
            conv_taps(2, 0, 2 * P, range(TAPS), 3)
            for m in range(IC):
                delta_product(1, m, 2 * P)
            bc_product(1, 2, 0)
            for m in range(1, IC):
                conv_taps(2, m, 2 * P, range(TAPS), 3)
            walk(pe, step, None, 0)


FIRST_LOOPED, LOOPED = 2, 4
POOL_STEPS, ACT_STEPS, DVE_STEPS = 26, 7, 10


def walk(eng, step, own, per_turn):
    def both(pair):
        for j in range(2):
            step(pair * 2 + 1 + j, j, pair)

    for pair in range(FIRST_LOOPED):
        both(pair)
    with eng.Fori(FIRST_LOOPED, FIRST_LOOPED + LOOPED) as pair:
        if own:
            own.enter(pair - FIRST_LOOPED, per_turn)
        both(pair)
        if own:
            own.leave(LOOPED)
    for pair in range(FIRST_LOOPED + LOOPED, PAIRS):
        both(pair)
    for t in range(T, T + LAST_LAG - 1):
        step(t, (t + 1) % 2, None)


_INS = ["x", "cls_tok", "L0_tok_conv_w", "L0_tok_conv_b", "L0_tok_pos_table", "L0_attn_W_in", "L0_attn_conv_w",
        "L0_attn_conv_b", "L0_attn_W_x", "L0_attn_W_dt", "L0_attn_b_dt", "L0_attn_A_log", "L0_attn_D",
        "L0_attn_W_out", "L0_attn_gamma", "L0_attn_beta", "L0_ffn_w_in", "L0_ffn_g_in", "L0_ffn_w_out",
        "L0_ffn_g_out"]


def kernel(**inputs):
    import concourse.bacc as bacc
    from concourse.bass_utils import run_bass_kernel_spmd

    nc = bacc.Bacc("TRN2", target_bir_lowering=False, num_devices=1)
    arrays, args = {}, []
    for name in _INS:
        a = np.ascontiguousarray(inputs[name])
        arrays[f"in_{name}"] = a
        args.append(nc.dram_tensor(f"in_{name}", a.shape, mybir.dt.from_np(a.dtype), kind="ExternalInput").ap())
    args.append(nc.dram_tensor("out", (P, T, HID), F32, kind="ExternalOutput").ap())
    vit_block(nc, *args)
    r = run_bass_kernel_spmd(nc, [arrays], core_ids=[0])
    return r.results[0]["out"]
```

```python
from contextlib import ExitStack

import numpy as np
import concourse.bass as bass
import concourse.mybir as mybir

F32 = mybir.dt.float32
BF16 = mybir.dt.bfloat16
ACT = mybir.ActivationFunctionType
ALU = mybir.AluOpType
AX = mybir.AxisListType

P = 128
SIDE, PATCH, GRID = 64, 16, 4
T = 1 + GRID * GRID
HID, HC = 192, 96
KP = 3 * PATCH * PATCH // P
INNER, IC = 384, 3
STATE, TAPS = 16, 4
FFN, FC = 512, 4
PAIRS = (T - 1) // 2
CH = STATE // 2
BANK = 512
DC = STATE * INNER // BANK
DVE_OUT = (3, 7)
ACT_OUT = tuple(k for k in range(1, CH) if k not in DVE_OUT)
DECAYS_EARLY = ((), (0, 1), (2,), (3, 4), (5,), (6, 7), (8,), ())
DECAYS_LATE = ((9, 10), (11,), (12, 13), (14,), (15,), (), (), ())
LATE_FIRST = 9
AT = {
    "join": 1,
    "weigh": 0,
    "residual": 1,
    "second_scales": 2,
    "first_scales": 3,
    "small_root": 6,
    "inputs": 1,
    "conv_gate": 0,
    "d_term": 2,
    "q1": 1,
    "q2": 1,
    "conv_first": 1,
    "conv_second": 4,
    "conv_last": 0,
    "delta_chunks": 3,
    "softplus": 6,
    "bc_copy": 6,
    "yzT": 2,
    "ow": 3,
    "t1": 6,
    "fsig": 5,
    "sumsq": 1,
    "t2": 4,
    "yz": 2,
    "mvA": 5,
    "o1": 0,
    "w": 3,
    "y2": 7,
    "am2": 1,
    "final": 2,
    "make_delta": 7,
    "turn_q1": 0,
    "turn_q2": 0,
    "turn_yz": 3,
    "project": 4,
    "ffn_first": 5,
    "ffn_second": 2,
    "delta_products": 2,
    "bc_product": 5,
}
AT_END = AT | {
    "second_scales": 3, "first_scales": 4, "q1": 2, "q2": 2, "yzT": 3, "ow": 4, "sumsq": 2, "t2": 6, "yz": 3,
    "mvA": 7, "w": 5, "am2": 2, "final": 4, "turn_yz": 2, "project": 3, "ffn_first": 4,
}
CONV_AT = (((), (), (), (), (), (), ((0, 0), (0, 1)), ((0, 2), (0, 3))),
           (((1, 0),), ((1, 1),), ((1, 2),), ((1, 3),), ((2, 0),), ((2, 1), (2, 2)), ((2, 3),), ()))
DB = 2
LIN = (5, 2)
TURN_BANKS = 6
XIN_BANKS = (2, 3, 4)
Z_BANKS = (5, 7, 6, 2)
ROUND = 12582912.0
SHARED = 16832
LAST_LAG = 6
POS_TABLE_SIDE = 32


class Steps:

    def __init__(self, eng, sem, apart=None):
        self.eng, self.sem, self.n, self.turns, self.apart = eng, sem, 0, 0, apart

    def mark(self, ins):
        ins.then_inc(self.sem, 1)
        self.n += 1
        return self.n

    def wait(self, n):
        if self.apart:
            self.apart(self.eng, self.sem, self.turns + n)
        else:
            self.eng.wait_ge(self.sem, self.turns + n)

    def then(self, ins):
        self.wait(self.mark(ins))

    def enter(self, turn, per_turn):
        self.first, self.per_turn, self.turns = self.n, per_turn, turn * per_turn

    def leave(self, turns):
        assert self.n - self.first == self.per_turn, (self.sem, self.n - self.first)
        self.n, self.turns = self.first + turns * self.per_turn, 0


def wait(eng, sem, value):
    if not isinstance(value, int) or value > 0:
        eng.wait_ge(sem, value)


def chunks_of(k):
    upto = lambda states: -(-states * INNER // BANK)
    return range(upto(2 * k), upto(2 * k + 2))


def last_slot(i):
    return (BANK * (i + 1) - 1) // (2 * INNER)


def conv_bank(q, m):
    early = {(1, 0): 0, (1, 1): 1, (1, 2): 6, (2, 0): 7, (2, 1): 6}
    return early[q, m] if isinstance(q, int) and (q, m) in early else LIN[m % 2]


def delta_bank(m):
    return LIN[(1 + m) % 2]


def exists(tile):
    return not isinstance(tile, int) or 0 <= tile < T


def vit_block(nc, x, cls_tok, tok_w, tok_b, pos_table, w_in, conv_w, conv_b, w_x, w_dt, b_dt, a_log, d_skip,
              w_out, gamma, beta, f_in, g_in, f_out, g_out, out):
    ctx = ExitStack()
    with ctx:
        def sb(name, shape, dt=F32):
            return ctx.enter_context(nc.sbuf_tensor(name, shape, dt))

        def sem(name):
            return ctx.enter_context(nc.semaphore(name))

        ident = sb("ident", [P, P])
        ones = sb("ones", [P, P])
        mhalf = sb("mhalf", [P, 1])
        mone = sb("mone", [P, 1])
        res = sb("res", [P, T, HID])
        gate = [sb(f"gate{i}", [P, INNER]) for i in range(2)]
        xinT = sb("xinT", [P, IC, (T + 3) * P])
        cw = sb("cw", [P, TAPS, IC, INNER])
        wdt = sb("wdt", [P, IC, INNER])
        wx = sb("wx", [P, IC, 2 * STATE])
        wo = sb("wo", [P, IC, HID])
        cb = sb("cb", [P, IC])
        bdt = sb("bdt", [P, IC])
        dsk = sb("dsk", [P, IC])
        A = sb("A", [P, IC, STATE])
        gam = sb("gam", [P, HID])
        gi = sb("gi", [P, HID])
        go = sb("go", [P, FFN])
        f1 = sb("f1", [HC, 2, 2 * FFN], BF16)
        f2 = sb("f2", [P, FC, HID], BF16)
        ws = sb("ws", [P, 2])
        state = sb("state", [P, STATE, INNER])
        xb = sb("xb", [P, IC, 2 * P])
        sg = sb("sg", [P, IC, 2 * P])
        db, sp = xb, sg
        xcT = sb("xcT", [P, IC, 2 * P])
        dltT = sb("dltT", [P, IC, 2 * P])
        uT = sb("uT", [P, IC, 2 * P])
        dxT = sb("dxT", [P, IC, 2 * P])
        bc = sb("bc", [P, 2, 2 * STATE])
        bcn = sb("bcn", [P, 2, 2 * STATE])
        ow = sb("ow", [P, HID])
        dx = sb("dx", [P, INNER])
        acc = sb("acc", [P, 2, INNER])
        ysum = sb("ysum", [P, INNER])
        ydve = sb("ydve", [P, INNER])
        shared = sb("shared", [P, SHARED])
        at = [0]

        def part(n):
            at[0] += n
            assert at[0] <= SHARED, at[0]
            return shared[:, at[0] - n:at[0]]

        xr = [part(3 * PATCH * SIDE).rearrange("p (c i w) -> p c i w", c=3, i=PATCH) for _ in range(2)]
        wi = part(2 * 2 * INNER)[0:HC].rearrange("p (c n) -> p c n", c=2)
        twT = part(KP * HID).rearrange("p (c n) -> p c n", c=KP)
        pos = part(T * HID).rearrange("p (t n) -> p t n", t=T)
        tb = part(HID)
        bet = part(HID)
        patch = [b[:].rearrange("p c n -> p (c n)").rearrange("p (c n) -> p c n", c=KP) for b in (xcT, dltT)]
        px = [b[:].rearrange("p c n -> p (c n)") for b in (uT, dxT, xb, sg)]
        xn = [part(HID) for _ in range(GRID)]
        xnT = part(2 * GRID * P)[0:HC].rearrange("p (c n) -> p c n", c=2)
        zs = [part(INNER) for _ in range(2)]
        raw = state[:].rearrange("p s n -> p (s n)")
        rawT = raw[0:HC, 0:2 * KP * P].rearrange("p (c n) -> p c n", c=2)
        raw1 = raw[:, 1536:1536 + 8 * HID].rearrange("p (c n) -> p c n", c=8)
        raw2 = raw[0:HC, 3072:3072 + 2 * FFN].rearrange("p (c n) -> p c n", c=2)
        at[0] = 0
        decay = part(STATE * IC * 2 * P).rearrange("p (s c n) -> p s c n", s=STATE, c=IC)
        prod = [part(2 * INNER).rearrange("p (s n) -> p s n", s=2) for _ in range(2)]
        yz, o1, wq, t1, sig, aa = (part(n) for n in (INNER, HID, HID, HID, FFN, FFN))
        yzT = sb("yzT", [P, IC, P])
        y2 = sb("y2", [P, FFN])
        v2 = sb("v2", [P, FFN])
        t2 = part(FFN)
        sq = part(FFN)
        q1 = sb("q1", [HC, 2, P], BF16)
        q2 = sb("q2", [P, FC, P], BF16)
        st = sb("st", [P, 6])
        mv = [sb(f"mv{i}", [P, 2]) for i in range(2)]
        rs = [sb(f"rs{i}", [P, 2]) for i in range(2)]
        stA = sb("stA", [P, 6])
        mvA = sb("mvA", [P, 2])
        rsA = sb("rsA", [P, 2])
        stF = sb("stF", [P, 6])
        mvF = sb("mvF", [P, 2])
        amF = sb("amF", [P, 1])
        s1 = sb("s1", [P, 5])
        c2 = sb("c2", [P, 2])
        c1 = sb("c1", [P, 2, 2])
        ss = sb("ss", [P, 1])
        am2 = sb("am2", [P, 1])
        s2 = sb("s2", [P, 8])
        wsum = sb("wsum", [P, 2])
        wsc = sb("wsc", [P, 2])

        gate_d = nc.dram_tensor("gate_d", (T - 1, P, INNER), F32, kind="Internal").ap()
        ps = ctx.enter_context(nc.psum_tensor("ps", [P, 8 * BANK], F32))

        def bank(b, n=BANK, rows=P, off=0):
            return ps[0:rows, b * BANK + off:b * BANK + off + n]

        S = {n: sem(n) for n in (
            "x_even x_odd consts_loaded raws_loaded conv_loaded ident_built ones_set raw_scaled raw_turned "
            "tok_turned wsum_ready ws_ready ws_inverse patch_packed patch_turned patch_act patch_dve "
            "emb_ready mv_ready rs_ready xn_ready xn_turned xnT_ready xin_ready xin_act xin_dve z_ready "
            "zsig_ready z_used act_step dve_step pool_step a_ready pads_zeroed conv_ready conv_used dlt_ready "
            "dlt_used sig_ready xc_ready sp_ready delta_ready uT_ready dxT_ready bc_ready bcn_ready bc_copied "
            "decay_made decay_turned decay_used u_turned dx_turned dx_ready state_ready rows_read y_ready "
            "gate_kept gate_even_in gate_odd_in yz_ready yz_turned yzT_ready o_ready ow_ready mvA_ready "
            "rsA_ready o1_ready h1_ready first_read prod_used y_dve y_joined w_ready s1_ready t1_ready "
            "q1_turned q1_ready f1_ready fsig_ready f1_used v2_ready sumsq_ready am2_ready s2_ready t2_ready "
            "q2_turned q2_ready f2_ready final_ready stored").split()}

        def apart(eng, sem, value):
            if isinstance(value, int):
                wait(eng, sem, value)
            else:
                value = eng.lower_val(value)
                eng.wait_ge(S["consts_loaded"], 16 * n_const)
                eng.wait_ge(sem, value)

        def product_read(g, j):
            return (S["emb_ready"], g * GRID + j - 1) if j >= 2 else (S["xn_turned"], g * GRID + 1)

        block = ctx.enter_context(nc.Block())
        x_rows = x.rearrange("b c (g i) w -> g b c i w", g=GRID)
        n_const, n_conv = 15, 3

        def chunks(v, c):
            return v.rearrange("(c p) -> p c", c=c)

        @block.sync
        def _(q):
            q.dma_start(rawT, tok_w.rearrange("(c p) k i j -> p c (k i j)", c=2)).then_inc(S["raws_loaded"], 16)
            q.dma_start(raw1, f_in.rearrange("(c p) n -> p c n", c=8)).then_inc(S["raws_loaded"], 16)
            q.dma_start(raw2, f_out.rearrange("(c p) n -> p c n", c=2)).then_inc(S["raws_loaded"], 16)
            q.dma_start(xr[0], x_rows[0]).then_inc(S["x_even"], 16)
            q.wait_ge(S["consts_loaded"], 16 * n_const)
            q.dma_start(xr[1], x_rows[1]).then_inc(S["x_odd"], 16)
            for tap_w, src in ((cw[:], conv_w.rearrange("t (c p) n -> p t c n", c=IC)),
                               (wdt[:], w_dt.rearrange("(c p) n -> p c n", c=IC)),
                               (wo[:], w_out.rearrange("(c p) n -> p c n", c=IC))):
                q.dma_start(tap_w, src).then_inc(S["conv_loaded"], 16)

            for g in range(GRID):
                if g + 2 < GRID:
                    q.wait_ge(S["patch_packed"], GRID * (g + 1))
                    q.dma_start(xr[g % 2], x_rows[g + 2]).then_inc(S[("x_even", "x_odd")[g % 2]], 16)
                q.wait_ge(S["z_used"], 1 + GRID * (g + 1))
                q.dma_start(gate_d[g * GRID:(g + 1) * GRID].rearrange("t p n -> p t n"),
                            state[:, g * GRID:(g + 1) * GRID, :]).then_inc(S["gate_kept"], 16)
            q.wait_ge(S["gate_kept"], 16 * GRID)

            def fetch_gate(t, par):
                wait(q, S["yz_ready"], t - 1)
                q.dma_start(gate[par][:], gate_d[bass.ds(t - 1, 1)].rearrange("o p n -> (o p) n")).then_inc(
                    S[("gate_even_in", "gate_odd_in")[par]], 16)

            def store(t):
                q.wait_ge(S["final_ready"], t + 1)
                q.dma_start(out[:, bass.ds(t, 1), :], res[:, bass.ds(t, 1), :]).then_inc(S["stored"], 16)

            for t in range(1, 5):
                fetch_gate(t, t % 2)
            with q.Fori(0, 6) as i:
                for h in range(2):
                    fetch_gate(2 * i + 5 + h, (1 + h) % 2)
                    store(2 * i + h)
            for t in range(12, T):
                store(t)
            q.wait_ge(S["stored"], 16 * T)

        @block.gpsimd
        def _(pool):
            own = Steps(pool, S["pool_step"], apart)
            pool.memset(mhalf[:], -0.5)
            pool.memset(mone[:], -1.0)
            pool.memset(ones[:], 1.0).then_inc(S["ones_set"], 1)
            own.then(pool.memset(ident[:], 0.0))
            pool.affine_select(out=ident[:], in_=ident[:], compare_op=ALU.not_equal, fill=1.0, base=0,
                               pattern=[[-1, P]], channel_multiplier=1).then_inc(S["ident_built"], 1)
            pool.memset(xinT[:, :, 0:P], 0.0)
            pool.memset(xinT[:, :, (T + 1) * P:(T + 3) * P], 0.0).then_inc(S["pads_zeroed"], 1)
            pool.wait_ge(S["ws_ready"], 1)
            pool.wait_ge(S["ones_set"], 1)
            pool.tensor_tensor(wsc[:], ws[:], mone[:].to_broadcast([P, 2]), ALU.pow).then_inc(S["ws_inverse"], 1)

            def root(t, par):
                apart(pool, S["mv_ready"], t + 1)
                own.then(pool.tensor_scalar(rs[par][:, 0:1], mv[par][:, 1:2], 1e-5, None, ALU.add))
                pool.tensor_tensor(rs[par][:, 1:2], rs[par][:, 0:1], mhalf[:], ALU.pow).then_inc(S["rs_ready"], 1)
                wait(pool, S["xn_ready"], t + 1)
                r = res[:, bass.ds(t, 1), :]
                pool.tensor_tensor(r, r, bet.rearrange("p (o n) -> p o n", o=1), ALU.add)

            def pack(n):
                g, j = n // GRID, n % GRID
                if j == 0:
                    pool.wait_ge(S[("x_even", "x_odd")[g % 2]], 16 * (g // 2) + 16)
                wait(pool, S["patch_turned"], n + 1 - GRID)
                pool.tensor_copy(px[j].rearrange("p (i n) -> p i n", n=PATCH),
                                 xr[g % 2].rearrange("p c i w -> p (c i) w")[
                                     :, :, j * PATCH:(j + 1) * PATCH]).then_inc(S["patch_packed"], 1)

            pack(0)
            pack(1)
            root(0, 0)
            pack(2)
            pack(3)
            for n in range(GRID * GRID):
                root(n + 1, (n + 1) % 2)
                if n + GRID < GRID * GRID:
                    pack(n + GRID)

            def conv_gate(q_, n):
                wait(pool, S["sig_ready"], q_ + 1)
                wait(pool, S["dlt_ready"], 3 * q_)
                wait(pool, S["bc_ready"], q_)
                wait(pool, S["dxT_ready"], q_)
                pool.tensor_tensor(xcT[:, :, 0:n], xb[:, :, 0:n], sg[:, :, 0:n],
                                   ALU.mult).then_inc(S["xc_ready"], 1)

            def inputs(q_, n):
                wait(pool, S["delta_ready"], q_ + 1)
                wait(pool, S["xc_ready"], q_ + 1)
                wait(pool, S["u_turned"], 2 * q_ - 1)
                pool.tensor_tensor(uT[:, :, 0:n], dltT[:, :, 0:n], xcT[:, :, 0:n],
                                   ALU.mult).then_inc(S["uT_ready"], 1)
                wait(pool, S["dx_turned"], 2 * q_ - 1)
                pool.tensor_tensor(dxT[:, :, 0:n], xcT[:, :, 0:n],
                                   dsk[:].rearrange("p (c o) -> p c o", o=1).to_broadcast([P, IC, n]),
                                   ALU.mult).then_inc(S["dxT_ready"], 1)

            def outputs(t, par, k):
                if k == 0:
                    wait(pool, S["y_ready"], t)
                    apart(pool, S["state_ready"], t * CH + 1)
                    for r in range(2):
                        last = pool.tensor_scalar(acc[:, r, :], state[:, r, :],
                                                  bc[:, par, STATE + r:STATE + r + 1], 1.0, ALU.mult, ALU.mult)
                    last.then_inc(S["first_read"], 1)
                    return
                i, n = ACT_OUT.index(k), len(ACT_OUT)
                pool.wait_ge(S["rows_read"], t * n + i + 1)
                if i == 0:
                    pool.wait_ge(S["first_read"], t + 1)
                else:
                    pool.wait_ge(S["prod_used"], t * n + i)
                pool.tensor_tensor(acc[:], acc[:], prod[i % 2], ALU.add).then_inc(S["prod_used"], 1)
                if k == ACT_OUT[-1]:
                    pool.wait_ge(S["prod_used"], (t + 1) * n)
                    wait(pool, S["yz_ready"], t)
                    pool.tensor_tensor(ysum[:], acc[:, 0, :], acc[:, 1, :], ALU.add).then_inc(S["y_ready"], 1)

            def small_root(t):
                apart(pool, S["mvA_ready"], t + 1)
                own.then(pool.tensor_scalar(rsA[:, 0:1], mvA[:, 1:2], 1e-5, None, ALU.add))
                pool.tensor_tensor(rsA[:, 1:2], rsA[:, 0:1], mhalf[:], ALU.pow).then_inc(S["rsA_ready"], 1)

            def residual(t):
                pool.wait_ge(S["o1_ready"], t + 1)
                own.then(pool.tensor_tensor(o1, o1, gam[:], ALU.mult))
                r = res[:, bass.ds(t, 1), :]
                pool.tensor_tensor(r, r, o1.rearrange("p (o n) -> p o n", o=1), ALU.add).then_inc(S["h1_ready"], 1)

            def first_scales(t, par):
                apart(pool, S["w_ready"], t + 1)
                own.then(pool.tensor_scalar(s1[:, 0:1], mvF[:, 1:2], 1.0 + 1e-6, 1e-11, ALU.mult, ALU.add))
                own.then(pool.tensor_tensor(s1[:, 1:2], s1[:, 0:1], mhalf[:], ALU.pow))
                own.then(pool.tensor_scalar(s1[:, 2:3], amF[:], s1[:, 1:2], 1e-5, ALU.mult, ALU.max))
                own.then(pool.tensor_tensor(s1[:, 3:4], s1[:, 2:3], mone[:], ALU.pow))
                apart(pool, S["t1_ready"], t)
                pool.tensor_scalar(s1[:, 4:5], s1[:, 3:4], s1[:, 1:2], 127.0, ALU.mult, ALU.mult)
                apart(pool, S["fsig_ready"], t - 1)
                pool.tensor_scalar(c1[:, par, 1:2], s1[:, 2:3], ws[:, 0:1], -1.0 / 127.0, ALU.mult, ALU.mult)
                pool.tensor_scalar(c1[:, par, 0:1], s1[:, 2:3], ws[:, 0:1], 1.0 / 127.0, ALU.mult,
                                   ALU.mult).then_inc(S["s1_ready"], 1)

            def weigh(t):
                pool.wait_ge(S["f1_used"], t + 1)
                wait(pool, S["t2_ready"], t)
                wait(pool, S["am2_ready"], t)
                pool.tensor_tensor(v2[:], y2[:], go[:], ALU.mult).then_inc(S["v2_ready"], 1)

            def second_scales(t, par):
                apart(pool, S["sumsq_ready"], t + 1)
                pool.wait_ge(S["am2_ready"], t + 1)
                c = c1[:, par, 0:1]
                apart(pool, S["s1_ready"], t + 1)
                own.then(pool.tensor_scalar(s2[:, 0:1], c, c, 1.0, ALU.mult, ALU.mult))
                own.then(pool.tensor_scalar(s2[:, 1:2], ss[:], s2[:, 0:1], s2[:, 0:1], ALU.mult, ALU.mult))
                own.then(pool.tensor_scalar(s2[:, 2:3], s2[:, 1:2], 1.0 / FFN, 1e-6, ALU.mult, ALU.add))
                own.then(pool.tensor_tensor(s2[:, 3:4], s2[:, 2:3], mhalf[:], ALU.pow))
                own.then(pool.tensor_tensor(s2[:, 4:5], s2[:, 3:4], s2[:, 0:1], ALU.mult))
                own.then(pool.tensor_scalar(s2[:, 5:6], am2[:], s2[:, 4:5], 1e-5, ALU.mult, ALU.max))
                own.then(pool.tensor_tensor(s2[:, 6:7], s2[:, 5:6], mone[:], ALU.pow))
                apart(pool, S["t2_ready"], t)
                pool.tensor_scalar(s2[:, 7:8], s2[:, 6:7], s2[:, 4:5], 127.0, ALU.mult, ALU.mult)
                apart(pool, S["final_ready"], t - 1)
                pool.tensor_scalar(c2[:, par:par + 1], s2[:, 5:6], ws[:, 1:2], 1.0 / 127.0, ALU.mult,
                                   ALU.mult).then_inc(S["s2_ready"], 1)

            def step(t, j, pair):
                at = AT if pair is not None else AT_END
                par = (1 + j) % 2
                scan = exists(t)
                has = lambda d: pair is not None and (not isinstance(pair, int) or pair < PAIRS - d)
                for k in range(CH):
                    if k == at["join"] and exists(t - 1):
                        pool.wait_ge(S["y_ready"], t)
                        pool.wait_ge(S["y_dve"], t * 2 * len(DVE_OUT))
                        pool.tensor_tensor(ysum[:], ysum[:], ydve[:], ALU.add).then_inc(S["y_joined"], 1)
                    if k == at["second_scales"] and exists(t - 4):
                        second_scales(t - 4, par)
                    if k == at["first_scales"] and exists(t - 2):
                        first_scales(t - 2, par)
                    if k == at["small_root"] and exists(t - 1):
                        small_root(t - 1)
                    if k == at["residual"] and exists(t - 2):
                        residual(t - 2)
                    if k == at["weigh"] and exists(t - 4):
                        weigh(t - 4)
                    if scan and k - 1 in (0,) + ACT_OUT:
                        outputs(t, par, k - 1)
                    if j == 1 and k == at["inputs"] and has(1):
                        inputs(pair + 2, 2 * P)
                    if j == 0 and k == at["conv_gate"] and has(1):
                        conv_gate(pair + 2, 2 * P)

            conv_gate(0, P)
            inputs(0, P)
            conv_gate(1, 2 * P)
            for k in (0,) + ACT_OUT[:2]:
                outputs(0, 0, k)
            inputs(1, 2 * P)
            for k in ACT_OUT[2:]:
                outputs(0, 0, k)
            walk(pool, step, own, POOL_STEPS)

        @block.scalar
        def _(act):
            own = Steps(act, S["act_step"])
            act.preload_act_table_set("natural_log_exp_and_others")

            def load(dst, src):
                act.dma_start(dst, src).then_inc(S["consts_loaded"], 16)

            def spread(vector, n):
                return vector.rearrange("(o n) -> o n", o=1).to_broadcast([P, n])

            step_ = POS_TABLE_SIDE // GRID
            rows = pos_table.rearrange("(h a w b) n -> a b h w n", h=GRID, a=step_, w=GRID)[0, 0]
            for h in range(GRID):
                load(pos[:, 1 + GRID * h:1 + GRID * (h + 1), :], rows[h:h + 1].to_broadcast([P, GRID, HID]))
            load(tb, spread(tok_b, HID))
            load(res[:, 0, :], cls_tok.rearrange("a b n -> (a b) n").to_broadcast([P, HID]))
            load(wi, w_in.rearrange("(c p) n -> p c n", c=2))
            load(bet, spread(beta, HID))
            load(gam[:], spread(gamma, HID))
            load(gi[:], spread(g_in, HID))
            load(go[:], spread(g_out, FFN))
            with nc.allow_non_contiguous_dma(reason="a few hundred numbers"):
                load(cb[:], chunks(conv_b, IC))
                load(bdt[:], chunks(b_dt, IC))
                load(dsk[:], chunks(d_skip, IC))
            load(A[:], a_log.rearrange("(c p) s -> p c s", c=IC))
            act.dma_start(wx[:], w_x.rearrange("(c p) n -> p c n", c=IC)).then_inc(S["conv_loaded"], 16)
            act.wait_ge(S["consts_loaded"], 16 * n_const)
            own.then(act.activation(A[:], A[:], ACT.Exp))
            act.activation(A[:], A[:], ACT.Copy, scale=-1.0).then_inc(S["a_ready"], 1)

            def normal_T(t, j, par):
                wait(act, S["xn_turned"], t + 1)
                if j == 0:
                    wait(act, S["z_ready"], t)
                act.activation(xnT[:, :, j * P:(j + 1) * P],
                               bank(6 + par, 2 * P, HC).rearrange("p (c n) -> p c n", c=2),
                               ACT.Copy).then_inc(S["xnT_ready"], 1)

            def z_sigmoid(t, j, par):
                z = bank(Z_BANKS[j], INNER)
                wait(act, S["z_ready"], t + 1)
                wait(act, S["z_used"], t - 1 if j else t)
                own.then(act.activation(zs[par], z, ACT.Exp, scale=-1.0))
                own.then(act.activation(zs[par], zs[par], ACT.Ln, bias=1.0))
                act.activation(zs[par], zs[par], ACT.Exp, scale=-1.0).then_inc(S["zsig_ready"], 1)

            def patch_part(g, j):
                wait(act, S["patch_turned"], g * GRID + 1 + j)
                act.wait_ge(*product_read(g, j))
                act.activation(patch[j % 2][:, 0:4, :], bank(2 * (j % 2)).rearrange("p (c n) -> p c n", c=4),
                               ACT.Copy).then_inc(S["patch_act"], 1)

            normal_T(0, 0, 0)
            patch_part(0, 0)
            wait(act, S["xin_ready"], 3)
            act.activation(xinT[:, 0:2, P:2 * P],
                           ps[:, 2 * BANK:4 * BANK].rearrange("p (c n) -> p c n", c=2)[:, :, 0:P],
                           ACT.Copy).then_inc(S["xin_act"], 1)
            z_sigmoid(0, 0, 0)

            def row(g, last_row):
                for j in range(1, GRID + (not last_row)):
                    patch_part(g, j)
                for j in range(GRID - 1):
                    normal_T(g * GRID + 1 + j, j, (1 + j) % 2)
                normal_T(g * GRID + GRID, GRID - 1, GRID % 2)
                for j in range(2):
                    z_sigmoid(g * GRID + 1 + j, j, (1 + j) % 2)
                act.wait_ge(S["xin_ready"], 2 * IC * g + 3 * IC)
                for c in range(2):
                    last = act.activation(xinT[:, c, bass.ds((g * GRID + 2) * P, GRID * P)], bank(XIN_BANKS[c]),
                                          ACT.Copy)
                last.then_inc(S["xin_act"], 1)
                for j in range(2, GRID):
                    z_sigmoid(g * GRID + 1 + j, j, (1 + j) % 2)

            with act.Fori(0, GRID - 1) as g:
                own.enter(g, 2 * GRID)
                row(g, False)
                own.leave(GRID - 1)
            row(GRID - 1, True)

            def conv_chunk(q_, m, n):
                wait(act, S["delta_ready"], q_)
                wait(act, S["conv_ready"], 3 * q_ + m + 1)
                act.activation(xb[:, m, 0:n], bank(conv_bank(q_, m), n), ACT.Identity,
                               bias=cb[:, m:m + 1]).then_inc(S["conv_used"], 1)

            def conv_sigmoid(q_, n):
                act.wait_ge(S["conv_used"], 3 * q_ + 3)
                own.then(act.activation(sg[:, :, 0:n], xb[:, :, 0:n], ACT.Exp, scale=-1.0))
                own.then(act.activation(sg[:, :, 0:n], sg[:, :, 0:n], ACT.Ln, bias=1.0))
                act.activation(sg[:, :, 0:n], sg[:, :, 0:n], ACT.Exp, scale=-1.0).then_inc(S["sig_ready"], 1)

            def delta_chunk(q_, m, n):
                wait(act, S["xc_ready"], q_ + 1)
                wait(act, S["dlt_ready"], 3 * q_ + m + 1)
                act.activation(db[:, m, 0:n], bank(delta_bank(m), n), ACT.Identity,
                               bias=bdt[:, m:m + 1]).then_inc(S["dlt_used"], 1)

            def softplus(q_, n):
                act.wait_ge(S["dlt_used"], 3 * q_ + 3)
                own.then(act.activation(sp[:, :, 0:n], db[:, :, 0:n], ACT.Exp))
                act.activation(sp[:, :, 0:n], sp[:, :, 0:n], ACT.Ln, bias=1.0).then_inc(S["sp_ready"], 1)

            def decays(pair, s_):
                if s_ in (0, LATE_FIRST):
                    act.wait_ge(S["delta_ready"], pair + 2)
                wait(act, S["decay_turned"], (2 * pair - 1) * DC + (IC * s_ + IC - 1) * P // BANK + 1)
                for c in range(IC):
                    last = act.activation(decay[:, s_, c, :], dltT[:, c, :], ACT.Exp, scale=A[:, c, s_:s_ + 1])
                last.then_inc(S["decay_made"], 1)

            def bc_copy(q_, tiles=2):
                wait(act, S["bc_ready"], q_ + 1)
                wait(act, S["bc_copied"], 2 * q_ - 1)
                act.activation(bcn[:].rearrange("p t n -> p (t n)")[:, 0:tiles * 2 * STATE],
                               bank(3, tiles * 2 * STATE), ACT.Copy).then_inc(
                    S["bcn_ready"], 1)

            def d_term(t):
                act.wait_ge(S["dx_turned"], t + 1)
                wait(act, S["y_dve"], (t - 1) * 2 * len(DVE_OUT) + 1)
                act.activation(dx[:], bank(3, INNER), ACT.Copy).then_inc(S["dx_ready"], 1)

            def products(t, par, k):
                i, n = ACT_OUT.index(k), len(ACT_OUT)
                if i == 0:
                    wait(act, S["prod_used"], t * n)
                if i > 1:
                    act.wait_ge(S["prod_used"], t * n + i - 1)
                act.wait_ge(S["state_ready"], t * CH + k + 1)
                for r in range(2):
                    s_ = 2 * k + r
                    last = act.activation(prod[i % 2][:, r, :], state[:, s_, :], ACT.Copy,
                                          scale=bc[:, par, STATE + s_:STATE + s_ + 1])
                last.then_inc(S["rows_read"], 1)

            def step(t, j, pair):
                at = AT if pair is not None else AT_END
                par = (1 + j) % 2
                has = lambda d: pair is not None and (not isinstance(pair, int) or pair < PAIRS - d)
                for k in range(CH):
                    if k == at["d_term"] and exists(t):
                        d_term(t)
                    if k == at["q1"] and exists(t - 3):
                        act.wait_ge(S["q1_turned"], t - 2)
                        wait(act, S["f1_ready"], t - 3)
                        act.activation(q1[:], bank(6, 2 * P, HC).rearrange("p (c n) -> p c n", c=2), ACT.Copy,
                                       bias=-ROUND).then_inc(S["q1_ready"], 1)
                    if k == at["q2"] and exists(t - 5):
                        act.wait_ge(S["q2_turned"], t - 4)
                        wait(act, S["f2_ready"], t - 5)
                        act.activation(q2[:].rearrange("p c n -> p (c n)"), bank(7), ACT.Copy,
                                       bias=-ROUND).then_inc(S["q2_ready"], 1)
                    if has(1) and j == 0:
                        if k == at["conv_last"] and not (isinstance(pair, int) and pair == 0):
                            conv_chunk(pair + 2, 2, 2 * P)
                            conv_sigmoid(pair + 2, 2 * P)
                        if at["delta_chunks"] <= k < at["delta_chunks"] + IC:
                            delta_chunk(pair + 2, k - at["delta_chunks"], 2 * P)
                        if k == at["softplus"]:
                            softplus(pair + 2, 2 * P)
                    if has(2) and j == 1 and k in (at["conv_first"], at["conv_second"]):
                        conv_chunk(pair + 3, int(k == at["conv_second"]), 2 * P)
                    if has(1) and j == 1 and k == at["bc_copy"]:
                        bc_copy(pair + 2)
                    if has(0) and j == 0:
                        for s_ in DECAYS_LATE[k]:
                            decays(pair, s_)
                    if has(1) and j == 1:
                        for s_ in DECAYS_EARLY[k]:
                            decays(pair + 1, s_)
                    if exists(t) and k - 1 in ACT_OUT:
                        products(t, par, k - 1)
                    if k == at["yzT"] and exists(t - 1):
                        act.wait_ge(S["yz_turned"], t)
                        wait(act, S["o_ready"], t - 1)
                        act.activation(yzT[:].rearrange("p c n -> p (c n)"), bank(3, INNER),
                                       ACT.Copy).then_inc(S["yzT_ready"], 1)
                    if k == at["ow"] and exists(t - 1):
                        act.wait_ge(S["o_ready"], t)
                        wait(act, S["o1_ready"], t - 1)
                        act.activation(ow[:], bank(3, HID), ACT.Copy).then_inc(S["ow_ready"], 1)
                    if k == at["t1"] and exists(t - 2):
                        act.wait_ge(S["s1_ready"], t - 1)
                        wait(act, S["q1_turned"], t - 2)
                        act.activation(t1, wq, ACT.Copy, bias=ROUND, scale=s1[:, 4:5]).then_inc(S["t1_ready"], 1)
                    if k == at["fsig"] and exists(t - 3):
                        act.wait_ge(S["f1_ready"], t - 2)
                        own.then(act.activation(sig, bank(6), ACT.Exp, scale=c1[:, 1 - par, 1:2]))
                        own.then(act.activation(sig, sig, ACT.Ln, bias=1.0))
                        act.activation(sig, sig, ACT.Exp, scale=-1.0).then_inc(S["fsig_ready"], 1)
                    if k == at["sumsq"] and exists(t - 4):
                        act.wait_ge(S["f1_used"], t - 3)
                        wait(act, S["s2_ready"], t - 4)
                        act.activation(sq[:], y2[:], ACT.Square, accum_out=ss[:]).then_inc(S["sumsq_ready"], 1)
                    if k == at["t2"] and exists(t - 4):
                        act.wait_ge(S["s2_ready"], t - 3)
                        wait(act, S["q2_turned"], t - 4)
                        act.activation(t2[:], v2[:], ACT.Copy, bias=ROUND,
                                       scale=s2[:, 7:8]).then_inc(S["t2_ready"], 1)

            for q_, n in ((0, P), (1, 2 * P)):
                for m in range(IC):
                    conv_chunk(q_, m, n)
                if q_ == 1:
                    d_term(0)
                conv_sigmoid(q_, n)
                if q_ == 1:
                    for k in ACT_OUT[:2]:
                        products(0, 0, k)
                for m in range(IC):
                    delta_chunk(q_, m, n)
                softplus(q_, n)
                bc_copy(q_, n // P)
            for m in range(2):
                conv_chunk(2, m, 2 * P)
            for s_ in range(2):
                decays(0, s_)
            for k in ACT_OUT[2:]:
                products(0, 0, k)
            conv_chunk(2, 2, 2 * P)
            conv_sigmoid(2, 2 * P)
            for s_ in range(2, LATE_FIRST):
                decays(0, s_)
            walk(act, step, own, ACT_STEPS)

        @block.vector
        def _(dve):
            own = Steps(dve, S["dve_step"], apart)
            dve.wait_ge(S["raws_loaded"], 48)
            own.then(dve.memset(wsum[:], 0.0))
            dve.tensor_reduce(wsum[:, 0:1], raw1, AX.XY, ALU.add, apply_absolute_value=True)
            dve.tensor_reduce(wsum[0:HC, 1:2], raw2, AX.XY, ALU.add,
                              apply_absolute_value=True).then_inc(S["wsum_ready"], 1)
            dve.wait_ge(S["wsum_ready"], 2)
            for i, n in enumerate((2 * FFN * HID, FFN * HID)):
                last = dve.tensor_scalar(ws[:, i:i + 1], bank(7, 2)[:, i:i + 1], 1.0 / n, 1e-5, ALU.mult, ALU.max)
            last.then_inc(S["ws_ready"], 1)
            dve.wait_ge(S["ws_inverse"], 1)
            for i, w in ((0, raw1), (1, raw2)):
                rows_ = w.shape[0]
                own.then(dve.tensor_scalar(w, w, wsc[0:rows_, i:i + 1], 1.0, ALU.mult, ALU.min))
                dve.tensor_scalar(w, w, -1.0, ROUND, ALU.max, ALU.add).then_inc(S["raw_scaled"], 1)
            for k in range(KP):
                dve.wait_ge(S["tok_turned"], k + 1)
                dve.tensor_copy(twT[:, k, :], bank(k % TURN_BANKS, HID)).then_inc(S["raw_turned"], 1)
            for c in range(8):
                dve.wait_ge(S["tok_turned"], KP + c + 1)
                dve.tensor_scalar(f1[:, :, c * P:(c + 1) * P],
                                  bank((KP + c) % TURN_BANKS, 2 * P, HC).rearrange("p (c n) -> p c n", c=2),
                                  ROUND, None, ALU.subtract).then_inc(S["raw_turned"], 1)
            for c in range(FC):
                dve.wait_ge(S["tok_turned"], KP + 8 + c + 1)
                dve.tensor_scalar(f2[:, c, :], bank((KP + 8 + c) % TURN_BANKS, HID), ROUND, None,
                                  ALU.subtract).then_inc(S["raw_turned"], 1)

            def stats(par, src):
                own.then(dve.bn_stats(st[:], src))
                dve.bn_aggr(mv[par][:], st[:]).then_inc(S["mv_ready"], 1)

            def normalise(t, j, par, src):
                wait(dve, S["rs_ready"], t + 1)
                wait(dve, S["xn_turned"], t - j)
                dve.tensor_scalar(xn[j], src, mv[par][:, 0:1], rs[par][:, 1:2], ALU.subtract,
                                  ALU.mult).then_inc(S["xn_ready"], 1)

            def z_gate(t, j, par, kept):
                wait(dve, S["zsig_ready"], t + 1)
                dve.tensor_tensor(kept, bank(Z_BANKS[j], INNER), zs[par], ALU.mult).then_inc(S["z_used"], 1)

            dve.wait_ge(S["consts_loaded"], 16 * n_const)
            stats(0, res[:, 0, :])

            def patch_part(g, j):
                wait(dve, S["patch_turned"], g * GRID + 1 + j)
                dve.wait_ge(*product_read(g, j))
                dve.tensor_copy(patch[j % 2][:, 4:6, :],
                                bank(2 * (j % 2) + 1, 2 * P).rearrange("p (c n) -> p c n", c=2)
                                ).then_inc(S["patch_dve"], 1)

            normalise(0, 0, 0, res[:, 0, :])
            patch_part(0, 0)
            dve.wait_ge(S["xin_ready"], 3)
            dve.tensor_copy(xinT[:, 2, P:2 * P], bank(XIN_BANKS[2], P)).then_inc(S["xin_dve"], 1)
            z_gate(0, 0, 0, gate[0][:])
            own.then(dve.tensor_tensor(pos[:, 1:T, :], pos[:, 1:T, :],
                                       tb.rearrange("p (o n) -> p o n", o=1).to_broadcast([P, T - 1, HID]),
                                       ALU.add))

            def row(g, last_row):
                for j in range(GRID):
                    t = g * GRID + 1 + j
                    dve.wait_ge(S["emb_ready"], t)
                    e = res[:, bass.ds(t, 1), :].rearrange("p o n -> p (o n)")
                    own.then(dve.tensor_tensor(e, bank(4 + j % 2, HID),
                                               pos[:, bass.ds(t, 1), :].rearrange("p o n -> p (o n)"), ALU.add))
                    stats((1 + j) % 2, e)
                    if j == 0:
                        patch_part(g, 1)
                    if j + 2 < GRID + (not last_row):
                        patch_part(g, j + 2)
                    normalise(t, j, (1 + j) % 2, e)

                def row_gate(j):
                    z_gate(g * GRID + 1 + j, j, (1 + j) % 2,
                           state[:, bass.ds(g * GRID + j, 1), :].rearrange("p o n -> p (o n)"))

                row_gate(0)
                row_gate(1)
                dve.wait_ge(S["xin_ready"], 2 * IC * g + 3 * IC)
                dve.tensor_copy(xinT[:, 2, bass.ds((g * GRID + 2) * P, GRID * P)],
                                bank(XIN_BANKS[2])).then_inc(S["xin_dve"], 1)
                row_gate(2)
                row_gate(3)

            with dve.Fori(0, GRID - 1) as g:
                own.enter(g, 2 * GRID)
                row(g, False)
                own.leave(GRID - 1)
            row(GRID - 1, True)

            def make_delta(q_, n):
                dve.wait_ge(S["sp_ready"], q_ + 1)
                wait(dve, S["decay_made"], 16 * (q_ - 1))
                wait(dve, S["uT_ready"], q_)
                dve.scalar_tensor_tensor(dltT[:, :, 0:n], sp[:, :, 0:n], 80.0, db[:, :, 0:n], ALU.min,
                                         ALU.max).then_inc(S["delta_ready"], 1)

            u = bank(4, INNER)

            def copy_bc(t, j, par, place):
                wait(dve, S["bcn_ready"], place)
                wait(dve, S["rows_read"], (t - 1) * len(ACT_OUT))
                wait(dve, S["first_read"], t - 1)
                dve.tensor_copy(bc[:, par, :], bcn[:, j, :]).then_inc(S["bc_copied"], 1)
                wait(dve, S["bc_copied"], t + 1)

            def decay_state(t, i):
                dve.wait_ge(S["decay_turned"], (t - 1) * DC + i + 1)
                if i < 2:
                    dve.wait_ge(S["first_read"], t)
                wait(dve, S["rows_read"], (t - 1) * len(ACT_OUT) + sum(k <= last_slot(i) for k in ACT_OUT))
                h = state[:].rearrange("p s n -> p (s n)")[:, i * BANK:(i + 1) * BANK]
                dve.tensor_tensor(h, bank(i % DB), h, ALU.mult).then_inc(S["decay_used"], 1)

            def add_input(t, par, k):
                dve.wait_ge(S["decay_used"], (t - 1) * DC + chunks_of(k)[-1] + 1)
                for r in range(2):
                    s_ = 2 * k + r
                    last = dve.scalar_tensor_tensor(state[:, s_, :], u, bc[:, par, s_:s_ + 1], state[:, s_, :],
                                                    ALU.mult, ALU.add)
                last.then_inc(S["state_ready"], 1)

            def output(t, par, k, r):
                s_, n = 2 * k + r, 2 * DVE_OUT.index(k) + r
                if n == 0:
                    dve.wait_ge(S["dx_ready"], t + 1)
                    wait(dve, S["yz_ready"], t)
                    before = dx
                else:
                    wait(dve, S["y_dve"], t * 2 * len(DVE_OUT) + n)
                    before = ydve
                dve.wait_ge(S["state_ready"], t * CH + k + 1)
                dve.scalar_tensor_tensor(ydve[:], state[:, s_, :], bc[:, par, STATE + s_:STATE + s_ + 1],
                                         before[:], ALU.mult, ALU.add).then_inc(S["y_dve"], 1)

            def step(t, j, pair):
                at = AT if pair is not None else AT_END
                par = (1 + j) % 2
                has = lambda d: pair is not None and (not isinstance(pair, int) or pair < PAIRS - d)
                flat = lambda a: a.rearrange("p o n -> p (o n)")
                scan = exists(t)
                if scan and pair is not None:
                    copy_bc(t, j, par, pair + 2)
                for k in range(CH):
                    if k == 0 and exists(t - 1):
                        output(t - 1, 1 - par, CH - 1, 0)
                    if scan:
                        for i in chunks_of(k):
                            decay_state(t, i)
                    if k == at["yz"] and exists(t - 1):
                        dve.wait_ge(S["y_joined"], t)
                        wait(dve, S["yz_turned"], t - 1)
                        loads = (t - 1) // 2 if isinstance(t, int) else pair
                        if 1 - par:
                            dve.wait_ge(S["gate_odd_in"], 16 * loads + 16)
                        else:
                            wait(dve, S["gate_even_in"], 16 * loads)
                        dve.tensor_tensor(yz, ysum[:], gate[1 - par][:],
                                          ALU.mult).then_inc(S["yz_ready"], 1)
                    if k == at["mvA"] and exists(t - 1):
                        apart(dve, S["ow_ready"], t)
                        own.then(dve.bn_stats(stA[:], ow[:]))
                        dve.bn_aggr(mvA[:], stA[:]).then_inc(S["mvA_ready"], 1)
                    if k == at["o1"] and exists(t - 2):
                        dve.wait_ge(S["rsA_ready"], t - 1)
                        wait(dve, S["h1_ready"], t - 2)
                        dve.tensor_scalar(o1, ow[:], mvA[:, 0:1], rsA[:, 1:2], ALU.subtract,
                                          ALU.mult).then_inc(S["o1_ready"], 1)
                    if k == at["w"] and exists(t - 2):
                        apart(dve, S["h1_ready"], t - 1)
                        h1 = flat(res[:, bass.ds(t - 2, 1), :])
                        own.then(dve.bn_stats(stF[:], h1))
                        apart(dve, S["s1_ready"], t - 2)
                        own.then(dve.bn_aggr(mvF[:], stF[:]))
                        wait(dve, S["t1_ready"], t - 2)
                        own.then(dve.scalar_tensor_tensor(wq, h1, mvF[:, 0:1], gi[:], ALU.subtract, ALU.mult))
                        dve.tensor_reduce(amF[:], wq, AX.X, ALU.max, apply_absolute_value=True).then_inc(
                            S["w_ready"], 1)
                    if k == at["y2"] and exists(t - 3):
                        dve.wait_ge(S["fsig_ready"], t - 2)
                        own.then(dve.tensor_tensor(aa, bank(7), sig, ALU.mult))
                        wait(dve, S["v2_ready"], t - 3)
                        wait(dve, S["sumsq_ready"], t - 3)
                        dve.tensor_tensor(y2[:], bank(6), aa, ALU.mult).then_inc(S["f1_used"], 1)
                    if k == at["am2"] and exists(t - 4):
                        dve.wait_ge(S["v2_ready"], t - 3)
                        wait(dve, S["s2_ready"], t - 4)
                        dve.tensor_reduce(am2[:], v2[:], AX.X, ALU.max, apply_absolute_value=True).then_inc(
                            S["am2_ready"], 1)
                    if k == at["final"] and exists(t - 5):
                        dve.wait_ge(S["f2_ready"], t - 4)
                        r = flat(res[:, bass.ds(t - 5, 1), :])
                        dve.wait_ge(S["s2_ready"], t - 4)
                        dve.scalar_tensor_tensor(r, bank(7, HID), c2[:, 1 - par:2 - par], r, ALU.mult,
                                                 ALU.add).then_inc(S["final_ready"], 1)
                    if k == at["make_delta"] and j == 0 and has(1):
                        make_delta(pair + 2, 2 * P)
                    if scan and k - 1 in DVE_OUT:
                        output(t, par, k - 1, 0)
                    if scan:
                        if k == 0:
                            dve.wait_ge(S["u_turned"], t + 1)
                        add_input(t, par, k)
                    if k == 0 and exists(t - 1):
                        output(t - 1, 1 - par, CH - 1, 1)
                    if scan and k - 1 in DVE_OUT:
                        output(t, par, k - 1, 1)

            make_delta(0, P)
            copy_bc(0, 0, 0, 1)
            dve.wait_ge(S["gate_kept"], 16 * GRID)
            dve.wait_ge(S["u_turned"], 1)
            for k in range(CH):
                for r in range(2):
                    s_ = 2 * k + r
                    last = dve.tensor_scalar(state[:, s_, :], u, bc[:, 0, s_:s_ + 1], None, ALU.mult)
                last.then_inc(S["state_ready"], 1)
            make_delta(1, 2 * P)
            for k in DVE_OUT[:-1]:
                for r in range(2):
                    output(0, 0, k, r)
            walk(dve, step, own, DVE_STEPS)

        @block.tensor
        def _(pe):
            pe.wait_ge(S["ones_set"], 1)
            pe.wait_ge(S["wsum_ready"], 1)
            pe.matmul(bank(7, 2), ones[:], wsum[:], start=True, stop=True).then_inc(S["wsum_ready"], 1)
            pe.wait_ge(S["ident_built"], 1)
            pe.wait_ge(S["raws_loaded"], 48)
            n = 0
            for k in range(KP):
                wait(pe, S["raw_turned"], n + 1 - TURN_BANKS)
                for c in range(2):
                    last = pe.transpose(bank(n % TURN_BANKS, HC, off=c * HC),
                                        rawT[:, c, k * P:(k + 1) * P], ident[0:HC, 0:HC])
                last.then_inc(S["tok_turned"], 1)
                n += 1
            pe.wait_ge(S["raw_scaled"], 2)
            for c in range(8):
                wait(pe, S["raw_turned"], n + 1 - TURN_BANKS)
                for h in range(2):
                    last = pe.transpose(bank(n % TURN_BANKS, P, HC, h * P),
                                        raw1[:, c, h * HC:(h + 1) * HC], ident[:])
                last.then_inc(S["tok_turned"], 1)
                n += 1
            for c in range(FC):
                wait(pe, S["raw_turned"], n + 1 - TURN_BANKS)
                for h in range(2):
                    last = pe.transpose(bank(n % TURN_BANKS, HC, off=h * HC),
                                        raw2[:, h, c * P:(c + 1) * P], ident[0:HC, 0:HC])
                last.then_inc(S["tok_turned"], 1)
                n += 1

            def turn_normal(t, j, par):
                wait(pe, S["xn_ready"], t + 1)
                wait(pe, S["xnT_ready"], t - 1 if j else t)
                for c in range(2):
                    last = pe.transpose(bank(6 + par, P, HC, c * P), xn[j][:, c * HC:(c + 1) * HC], ident[:])
                last.then_inc(S["xn_turned"], 1)

            def x_inner(t0, first, tiles):
                wait(pe, S["xnT_ready"], t0 + first + tiles)
                cols = slice(first * P, (first + tiles) * P)
                for m in range(IC):
                    for c in range(2):
                        last = pe.matmul(bank(XIN_BANKS[m], tiles * P, off=first * P), wi[:, c, m * P:(m + 1) * P],
                                         xnT[:, c, cols], start=(c == 0), stop=(c == 1))
                    last.then_inc(S["xin_ready"], 1)

            def z_product(j):
                for c in range(2):
                    last = pe.matmul(bank(Z_BANKS[j], INNER), xnT[:, c, j * P:(j + 1) * P],
                                     wi[:, c, INNER:2 * INNER], start=(c == 0), stop=(c == 1))
                last.then_inc(S["z_ready"], 1)

            pe.wait_ge(S["raw_turned"], n)
            pe.wait_ge(S["consts_loaded"], 16 * n_const)
            turn_normal(0, 0, 0)

            def turn_patch(g, j):
                t = g * GRID + 1 + j
                if j == 1:
                    pe.wait_ge(S["xin_act"], g + 1)
                    pe.wait_ge(S["z_used"], t - 1)
                if j >= 2:
                    pe.wait_ge(S["patch_act"], t - 2)
                    pe.wait_ge(S["patch_dve"], t - 2)
                pe.wait_ge(S["patch_packed"], t)
                for k in range(KP):
                    last = pe.transpose(bank(2 * (j % 2) + k // 4, P, off=(k % 4) * P),
                                        px[j % GRID][:, k * P:(k + 1) * P], ident[:])
                last.then_inc(S["patch_turned"], 1)

            def embed(g, j):
                t = g * GRID + 1 + j
                pe.wait_ge(S["patch_act"], t)
                pe.wait_ge(S["patch_dve"], t)
                if j == 0:
                    pe.wait_ge(S["xin_dve"], g + 1)
                if j >= 2:
                    pe.wait_ge(S["mv_ready"], t - 1)
                for k in range(KP):
                    last = pe.matmul(bank(4 + j % 2, HID), patch[j % 2][:, k, :], twT[:, k, :],
                                     start=(k == 0), stop=(k == KP - 1))
                last.then_inc(S["emb_ready"], 1)

            def row(g, last_row):
                embed(g, 0)
                turn_patch(g, 1)
                for j in range(1, GRID):
                    if j + 1 < GRID + (not last_row):
                        turn_patch(g, j + 1)
                    if j == GRID - 1:
                        turn_normal(g * GRID + 1, 0, 1)
                    embed(g, j)
                t0 = g * GRID + 1
                turn_normal(t0 + 1, 1, 0)
                turn_normal(t0 + 2, 2, 1)
                x_inner(t0, 0, 2)
                pe.wait_ge(S["mv_ready"], t0 + GRID)
                z_product(0)
                turn_normal(t0 + 3, 3, 0)
                pe.wait_ge(S["xnT_ready"], t0 + 3)
                z_product(1)
                x_inner(t0, 2, 2)
                z_product(2)
                pe.wait_ge(S["xin_act"], g + 2)
                z_product(3)

            turn_patch(0, 0)
            x_inner(0, 0, 1)
            z_product(0)
            with pe.Fori(0, GRID - 1) as g:
                row(g, False)
            row(GRID - 1, True)

            def bank_free(q_, m):
                if isinstance(q_, int) and q_ in (1, 2) and (q_, m) != (2, 2):
                    return S["conv_used"], 6 if (q_, m) == (2, 1) else 0
                if isinstance(q_, int) and q_ == 2:
                    return S["dlt_used"], 5
                return (S["dlt_used"], 3 * q_ - 1 + m) if m < 2 else (S["conv_used"], 3 * q_ + 1)

            def conv_taps(q_, m, n, taps, first_tile):
                if 0 in taps:
                    wait(pe, *bank_free(q_, m))
                for tap in taps:
                    for c in range(IC):
                        last = pe.matmul(bank(conv_bank(q_, m), n), cw[:, tap, c, m * P:(m + 1) * P],
                                         xinT[:, c, bass.ds((first_tile + tap) * P, n)],
                                         start=(tap == 0 and c == 0), stop=(tap == TAPS - 1 and c == IC - 1))
                if TAPS - 1 in taps:
                    last.then_inc(S["conv_ready"], 1)

            def delta_product(q_, m, n):
                wait(pe, S["xc_ready"], q_ + 1)
                wait(pe, *((S["conv_used"], 3 * q_ + 2 + m) if m < 2 else (S["dlt_used"], 3 * q_ + 1)))
                for c in range(IC):
                    last = pe.matmul(bank(delta_bank(m), n), wdt[:, c, m * P:(m + 1) * P], xcT[:, c, 0:n],
                                     start=(c == 0), stop=(c == IC - 1))
                last.then_inc(S["dlt_ready"], 1)

            def bc_product(q_, tiles, ow_copied):
                wait(pe, S["xc_ready"], q_ + 1)
                wait(pe, S["ow_ready"], ow_copied)
                for j in range(tiles):
                    for c in range(IC):
                        last = pe.matmul(bank(3, 2 * STATE, off=2 * STATE * j),
                                         xcT[:, c, j * P:(j + 1) * P], wx[:, c, :],
                                         start=(c == 0), stop=(c == IC - 1))
                last.then_inc(S["bc_ready"], 1)

            def turn_inputs(t, j, q_):
                wait(pe, S["uT_ready"], q_ + 1)
                wait(pe, S["state_ready"], t * CH)
                for c in range(IC):
                    last = pe.transpose(bank(4, P, off=c * P), uT[:, c, j * P:(j + 1) * P], ident[:])
                last.then_inc(S["u_turned"], 1)
                wait(pe, S["dxT_ready"], q_ + 1)
                wait(pe, S["bcn_ready"], q_ + 1)
                wait(pe, S["ow_ready"], t - 1)
                for c in range(IC):
                    last = pe.transpose(bank(3, P, off=c * P), dxT[:, c, j * P:(j + 1) * P], ident[:])
                last.then_inc(S["dx_turned"], 1)

            def turn_decays(t, j, pair, i):
                pe.wait_ge(S["decay_made"], 16 * pair + (4 * i + 3) // IC + 1)
                wait(pe, S["decay_used"], (t - 1) * DC + i + 1 - DB)
                for b in range(4 * i, 4 * i + 4):
                    last = pe.transpose(bank(i % DB, P, off=(b % 4) * P),
                                        decay[:, b // IC, b % IC, j * P:(j + 1) * P], ident[:])
                last.then_inc(S["decay_turned"], 1)

            def step(t, j, pair):
                at = AT if pair is not None else AT_END
                par = (1 + j) % 2
                has = lambda d: pair is not None and (not isinstance(pair, int) or pair < PAIRS - d)
                for k in range(CH):
                    if exists(t):
                        for i in chunks_of(k):
                            turn_decays(t, j, pair, i)
                    if exists(t) and k == 0:
                        turn_inputs(t, j, pair + 1)
                    if k == at["turn_q1"] and exists(t - 3):
                        pe.wait_ge(S["t1_ready"], t - 2)
                        wait(pe, S["f1_used"], t - 3)
                        for c in range(2):
                            last = pe.transpose(bank(6, P, HC, c * P), t1[:, c * HC:(c + 1) * HC], ident[:])
                        last.then_inc(S["q1_turned"], 1)
                    if k == at["turn_q2"] and exists(t - 5):
                        pe.wait_ge(S["t2_ready"], t - 4)
                        wait(pe, S["f1_used"], min(t - 3, T) if isinstance(t, int) else t - 3)
                        wait(pe, S["final_ready"], t - 5)
                        for c in range(FC):
                            last = pe.transpose(bank(7, P, off=c * P), t2[:, c * P:(c + 1) * P], ident[:])
                        last.then_inc(S["q2_turned"], 1)
                    if k == at["turn_yz"] and exists(t - 1):
                        pe.wait_ge(S["yz_ready"], t)
                        pe.wait_ge(S["dx_ready"], min(t + 1, T) if isinstance(t, int) else t + 1)
                        for c in range(IC):
                            last = pe.transpose(bank(3, P, off=c * P), yz[:, c * P:(c + 1) * P], ident[:])
                        last.then_inc(S["yz_turned"], 1)
                    if k == at["project"] and exists(t - 1):
                        pe.wait_ge(S["yzT_ready"], t)
                        for c in range(IC):
                            last = pe.matmul(bank(3, HID), yzT[:, c, :], wo[:, c, :],
                                             start=(c == 0), stop=(c == IC - 1))
                        last.then_inc(S["o_ready"], 1)
                    if k == at["ffn_first"] and exists(t - 3):
                        pe.wait_ge(S["q1_ready"], t - 2)
                        wait(pe, S["final_ready"], t - 4)
                        for half in range(2):
                            for c in range(2):
                                last = pe.matmul(bank(6 + half), q1[:, c, :],
                                                 f1[:, c, (1 - half) * FFN:(2 - half) * FFN],
                                                 start=(c == 0), stop=(c == 1))
                        last.then_inc(S["f1_ready"], 1)
                    if k == at["ffn_second"] and exists(t - 5):
                        pe.wait_ge(S["q2_ready"], t - 4)
                        for c in range(FC):
                            last = pe.matmul(bank(7, HID), q2[:, c, :], f2[:, c, :],
                                             start=(c == 0), stop=(c == FC - 1))
                        last.then_inc(S["f2_ready"], 1)
                    if has(1):
                        if j == 0 and at["delta_products"] <= k < at["delta_products"] + IC:
                            delta_product(pair + 2, k - at["delta_products"], 2 * P)
                        if j == 1 and k == at["bc_product"]:
                            bc_product(pair + 2, 2, t)
                    if has(2):
                        for m, tap in CONV_AT[j][k]:
                            conv_taps(pair + 3, m, 2 * P, (tap,), pair * 2 + 5)

            pe.wait_ge(S["conv_loaded"], 16 * (n_conv + 1))
            pe.wait_ge(S["pads_zeroed"], 1)
            pe.wait_ge(S["xin_act"], GRID + 1)
            pe.wait_ge(S["xin_dve"], GRID + 1)
            pe.wait_ge(S["z_used"], T)
            for m in range(IC):
                conv_taps(0, m, P, range(TAPS), 0)
            conv_taps(1, 0, 2 * P, range(TAPS), 1)
            for m in range(IC):
                delta_product(0, m, P)
            bc_product(0, 1, 0)
            for m in range(1, IC):
                conv_taps(1, m, 2 * P, range(TAPS), 1)
            turn_inputs(0, 0, 0)
            conv_taps(2, 0, 2 * P, range(TAPS), 3)
            for m in range(IC):
                delta_product(1, m, 2 * P)
            bc_product(1, 2, 0)
            for m in range(1, IC):
                conv_taps(2, m, 2 * P, range(TAPS), 3)
            walk(pe, step, None, 0)


FIRST_LOOPED, LOOPED = 3, 3
POOL_STEPS, ACT_STEPS, DVE_STEPS = 26, 7, 10


def walk(eng, step, own, per_turn):
    def both(pair):
        for j in range(2):
            step(pair * 2 + 1 + j, j, pair)

    for pair in range(FIRST_LOOPED):
        both(pair)
    with eng.Fori(FIRST_LOOPED, FIRST_LOOPED + LOOPED) as pair:
        if own:
            own.enter(pair - FIRST_LOOPED, per_turn)
        both(pair)
        if own:
            own.leave(LOOPED)
    for pair in range(FIRST_LOOPED + LOOPED, PAIRS):
        both(pair)
    for t in range(T, T + LAST_LAG - 1):
        step(t, (t + 1) % 2, None)


_INS = ["x", "cls_tok", "L0_tok_conv_w", "L0_tok_conv_b", "L0_tok_pos_table", "L0_attn_W_in", "L0_attn_conv_w",
        "L0_attn_conv_b", "L0_attn_W_x", "L0_attn_W_dt", "L0_attn_b_dt", "L0_attn_A_log", "L0_attn_D",
        "L0_attn_W_out", "L0_attn_gamma", "L0_attn_beta", "L0_ffn_w_in", "L0_ffn_g_in", "L0_ffn_w_out",
        "L0_ffn_g_out"]


def kernel(**inputs):
    import concourse.bacc as bacc
    from concourse.bass_utils import run_bass_kernel_spmd

    nc = bacc.Bacc("TRN2", target_bir_lowering=False, num_devices=1)
    arrays, args = {}, []
    for name in _INS:
        a = np.ascontiguousarray(inputs[name])
        arrays[f"in_{name}"] = a
        args.append(nc.dram_tensor(f"in_{name}", a.shape, mybir.dt.from_np(a.dtype), kind="ExternalInput").ap())
    args.append(nc.dram_tensor("out", (P, T, HID), F32, kind="ExternalOutput").ap())
    vit_block(nc, *args)
    r = run_bass_kernel_spmd(nc, [arrays], core_ids=[0])
    return r.results[0]["out"]
```
